# Optimizing a Trainium2 kernel written in Bass

```python
import numpy as np
import jax
import jax.numpy as jnp

def _softmax(x, axis=-1):
    return jax.nn.softmax(x, axis=axis)

def _gelu(x):
    return jax.nn.gelu(x, approximate=True)

def _silu(x):
    return jax.nn.silu(x)

def _sigmoid(x):
    return jax.nn.sigmoid(x)

def _layernorm(x, axis=-1, eps=1e-05):
    m = jnp.mean(x, axis=axis, keepdims=True)
    v = jnp.var(x, axis=axis, keepdims=True)
    return (x - m) / jnp.sqrt(v + eps)

def _scatter_add(tgt, idx, src, axis=0):
    return tgt.at[idx].add(src)

def _segment_sum(src, seg, n):
    return jax.ops.segment_sum(src, seg, n)
kernel_name = 'mk_perceiver_d1_seqx_r4_bc1ea7'

def setup_inputs(seed: int=0):
    np.random.seed(seed)
    _w = jnp.asarray

    def _rec_inputs():
        import jax
        import jax.numpy as jnp
        _rk = jax.random.key(seed)
        x = 7.22e-05 + 1 * jax.random.normal(jax.random.fold_in(_rk, 1), (32, 64, 256), jnp.float32)
        _lenS = 64 - jax.random.randint(jax.random.fold_in(_rk, 7), (32,), 0, max(1, 64 // 4) + 1, jnp.int32)
        _lenS2 = 1601 - jax.random.randint(jax.random.fold_in(_rk, 8), (32,), 0, max(1, 1601 // 4) + 1, jnp.int32)
        _ctx_768P = jax.random.normal(jax.random.fold_in(_rk, 11), (32, 16, 192), jnp.float32)
        _ctx_768c = jax.random.dirichlet(jax.random.fold_in(_rk, 511), 0.3 * jnp.ones((16,), jnp.float32), (32, 1601))
        _ctx_768t = jnp.einsum('bsk,bkd->bsd', _ctx_768c, _ctx_768P)
        _ctx_768t = _ctx_768t * jax.lax.rsqrt(jnp.mean(jnp.square(_ctx_768t)) + 1e-12) * 0.953939
        ctx_768 = -7.36909e-05 + 0.999899 * (_ctx_768t + 0.3 * jax.random.normal(jax.random.fold_in(_rk, 611), (32, 1601, 192), jnp.float32))
        return (x, ctx_768)
    x, ctx_768 = _rec_inputs()

    def _L0_xattn_setup():
        import jax, jax.numpy as jnp
        import numpy as np
        NUM_HEADS = 16
        HEAD_DIM = 64
        INNER = NUM_HEADS * HEAD_DIM
        QUERY_DIM = 256
        CONTEXT_DIM = 192
        SCALE = HEAD_DIM ** (-0.5)
        key = jax.random.key(seed)
        ks = jax.random.split(key, 6)
        B, NQ, NKV = (8, 256, 512)
        query = jax.random.normal(ks[0], (B, NQ, QUERY_DIM), dtype=jnp.float32)
        context = jax.random.normal(ks[1], (B, NKV, CONTEXT_DIM), dtype=jnp.float32)
        w_q = jax.random.normal(ks[2], (QUERY_DIM, INNER), dtype=jnp.float32) * QUERY_DIM ** (-0.5)
        w_kv = jax.random.normal(ks[3], (CONTEXT_DIM, 2 * INNER), dtype=jnp.float32) * CONTEXT_DIM ** (-0.5)
        w_out = jax.random.normal(ks[4], (INNER, QUERY_DIM), dtype=jnp.float32) * INNER ** (-0.5)
        b_out = jax.random.normal(ks[5], (QUERY_DIM,), dtype=jnp.float32) * 0.01
        return {'query': query, 'context': context, 'w_q': w_q, 'w_kv': w_kv, 'w_out': w_out, 'b_out': b_out}
    _L0_xattn_all = _L0_xattn_setup()
    _L0_xattn_in = {k: v for k, v in _L0_xattn_all.items() if k in ('w_q', 'w_kv', 'w_out', 'b_out')}
    del _L0_xattn_all

    def _L0_attn_setup():
        import jax, jax.numpy as jnp
        import numpy as np
        H = 256
        B = 8
        T = 512
        key = jax.random.key(seed)
        ks = jax.random.split(key, 12)
        s = 1.0 / np.sqrt(H)
        return {'x': jax.random.normal(ks[0], (B, T, H), dtype=jnp.float32), 'time_decay': jax.random.normal(ks[1], (H,), dtype=jnp.float32) * 0.1, 'time_first': jax.random.normal(ks[2], (H,), dtype=jnp.float32) * 0.1, 'time_mix_key': jax.random.uniform(ks[3], (1, 1, H), dtype=jnp.float32), 'time_mix_value': jax.random.uniform(ks[4], (1, 1, H), dtype=jnp.float32), 'time_mix_receptance': jax.random.uniform(ks[5], (1, 1, H), dtype=jnp.float32), 'Wk': jax.random.normal(ks[6], (H, H), dtype=jnp.float32) * s, 'Wv': jax.random.normal(ks[7], (H, H), dtype=jnp.float32) * s, 'Wr': jax.random.normal(ks[8], (H, H), dtype=jnp.float32) * s, 'Wo': jax.random.normal(ks[9], (H, H), dtype=jnp.float32) * s, 'bo': jax.random.normal(ks[10], (H,), dtype=jnp.float32) * 0.01}
    _L0_attn_all = _L0_attn_setup()
    _L0_attn_in = {k: v for k, v in _L0_attn_all.items() if k in ('time_decay', 'time_first', 'time_mix_key', 'time_mix_value', 'time_mix_receptance', 'Wk', 'Wv', 'Wr', 'Wo', 'bo')}
    del _L0_attn_all

    def _L0_ffn_setup():
        import jax, jax.numpy as jnp
        import numpy as np
        B, S, D = (4, 512, 256)
        N_EXPERTS, EXPERT_SIZE = (16, 64)
        WIDTH = N_EXPERTS * EXPERT_SIZE
        key = jax.random.key(seed)
        k_x, k_w1, k_w2, k_g = jax.random.split(key, 4)
        x = jax.random.normal(k_x, (B, S, D), dtype=jnp.float32)
        w1 = jax.random.normal(k_w1, (D, WIDTH), dtype=jnp.float32) / np.sqrt(D).astype(np.float32)
        b1 = jnp.zeros((WIDTH,), dtype=jnp.float32)
        w2 = jax.random.normal(k_w2, (WIDTH, D), dtype=jnp.float32) / np.sqrt(WIDTH).astype(np.float32)
        b2 = jnp.zeros((D,), dtype=jnp.float32)
        return {'x': x, 'w1': w1, 'b1': b1, 'w2': w2, 'b2': b2}
    _L0_ffn_all = _L0_ffn_setup()
    _L0_ffn_in = {k: v for k, v in _L0_ffn_all.items() if k in ('w1', 'b1', 'w2', 'b2')}
    del _L0_ffn_all
    return {'x': x, 'ctx_768': ctx_768, 'L0_xattn_w_q': _L0_xattn_in['w_q'], 'L0_xattn_w_kv': _L0_xattn_in['w_kv'], 'L0_xattn_w_out': _L0_xattn_in['w_out'], 'L0_xattn_b_out': _L0_xattn_in['b_out'], 'L0_attn_time_decay': _L0_attn_in['time_decay'], 'L0_attn_time_first': _L0_attn_in['time_first'], 'L0_attn_time_mix_key': _L0_attn_in['time_mix_key'], 'L0_attn_time_mix_value': _L0_attn_in['time_mix_value'], 'L0_attn_time_mix_receptance': _L0_attn_in['time_mix_receptance'], 'L0_attn_Wk': _L0_attn_in['Wk'], 'L0_attn_Wv': _L0_attn_in['Wv'], 'L0_attn_Wr': _L0_attn_in['Wr'], 'L0_attn_Wo': _L0_attn_in['Wo'], 'L0_attn_bo': _L0_attn_in['bo'], 'L0_ffn_w1': _L0_ffn_in['w1'], 'L0_ffn_b1': _L0_ffn_in['b1'], 'L0_ffn_w2': _L0_ffn_in['w2'], 'L0_ffn_b2': _L0_ffn_in['b2']}

def reference(x, ctx_768, L0_xattn_w_q, L0_xattn_w_kv, L0_xattn_w_out, L0_xattn_b_out, L0_attn_time_decay, L0_attn_time_first, L0_attn_time_mix_key, L0_attn_time_mix_value, L0_attn_time_mix_receptance, L0_attn_Wk, L0_attn_Wv, L0_attn_Wr, L0_attn_Wo, L0_attn_bo, L0_ffn_w1, L0_ffn_b1, L0_ffn_w2, L0_ffn_b2):
    import jax
    import jax.numpy as jnp

    def _L0_xattn_ref(query, context, w_q, w_kv, w_out, b_out):
        import jax, jax.numpy as jnp
        import numpy as np
        NUM_HEADS = 16
        HEAD_DIM = 64
        INNER = NUM_HEADS * HEAD_DIM
        QUERY_DIM = 256
        CONTEXT_DIM = 192
        SCALE = HEAD_DIM ** (-0.5)
        B, NQ, _ = query.shape
        NKV = context.shape[1]
        q = query @ w_q
        kv = context @ w_kv
        k, v = jnp.split(kv, 2, axis=-1)
        q = q.reshape(B, NQ, NUM_HEADS, HEAD_DIM).transpose(0, 2, 1, 3)
        k = k.reshape(B, NKV, NUM_HEADS, HEAD_DIM).transpose(0, 2, 1, 3)
        v = v.reshape(B, NKV, NUM_HEADS, HEAD_DIM).transpose(0, 2, 1, 3)
        scores = jnp.einsum('bhqd,bhkd->bhqk', q, k) * SCALE
        attn = jax.nn.softmax(scores, axis=-1)
        out = jnp.einsum('bhqk,bhkd->bhqd', attn, v)
        out = out.transpose(0, 2, 1, 3).reshape(B, NQ, INNER)
        return out @ w_out + b_out

    def _L0_attn_ref(x, time_decay, time_first, time_mix_key, time_mix_value, time_mix_receptance, Wk, Wv, Wr, Wo, bo):
        import jax, jax.numpy as jnp
        import numpy as np
        H = 256
        B = 8
        T = 512
        shifted = jnp.pad(x, ((0, 0), (1, 0), (0, 0)))[:, :-1]
        k_in = x * time_mix_key + shifted * (1.0 - time_mix_key)
        v_in = x * time_mix_value + shifted * (1.0 - time_mix_value)
        r_in = x * time_mix_receptance + shifted * (1.0 - time_mix_receptance)
        k = jnp.einsum('bth,oh->bto', k_in, Wk)
        v = jnp.einsum('bth,oh->bto', v_in, Wv)
        r = jax.nn.sigmoid(jnp.einsum('bth,oh->bto', r_in, Wr))
        td = jnp.exp(-jnp.exp(time_decay))

        def step(carry, kv):
            num, den = carry
            k_t, v_t = kv
            e = jnp.exp(time_first + k_t)
            out_t = (num + e * v_t) / (den + e)
            ek = jnp.exp(k_t)
            return ((td * num + ek * v_t, td * den + ek), out_t)
        init = (jnp.zeros((x.shape[0], x.shape[2]), x.dtype), jnp.zeros((x.shape[0], x.shape[2]), x.dtype))
        _, wkv = jax.lax.scan(step, init, (k.transpose(1, 0, 2), v.transpose(1, 0, 2)))
        wkv = wkv.transpose(1, 0, 2)
        return jnp.einsum('bth,oh->bto', r * wkv, Wo) + bo

    def _L0_ffn_ref(x, w1, b1, w2, b2):
        import jax, jax.numpy as jnp
        import numpy as np
        B, S, D = (4, 512, 256)
        N_EXPERTS, EXPERT_SIZE = (16, 64)
        WIDTH = N_EXPERTS * EXPERT_SIZE
        h = jax.nn.relu(jnp.einsum('bsd,dw->bsw', x, w1) + b1)
        return jnp.einsum('bsw,wd->bsd', h, w2) + b2
    x = x + _L0_xattn_ref(_layernorm(x, axis=-1), ctx_768, L0_xattn_w_q, L0_xattn_w_kv, L0_xattn_w_out, L0_xattn_b_out)
    x = x + _L0_attn_ref(_layernorm(x, axis=-1), L0_attn_time_decay, L0_attn_time_first, L0_attn_time_mix_key, L0_attn_time_mix_value, L0_attn_time_mix_receptance, L0_attn_Wk, L0_attn_Wv, L0_attn_Wr, L0_attn_Wo, L0_attn_bo)
    x = x + _L0_ffn_ref(_layernorm(x, axis=-1), L0_ffn_w1, L0_ffn_b1, L0_ffn_w2, L0_ffn_b2)
    return x

_drawn_inputs = setup_inputs


def setup_inputs(seed=0):
    import zlib

    import numpy as np

    out = dict(_drawn_inputs(seed))
    spreads = {'L0_ffn_b1': (0.0, 0.1), 'L0_ffn_b2': (0.0, 0.1)}
    factors = {'L0_xattn_b_out': 5.668,
     'L0_attn_time_decay': 5.774,
     'L0_attn_time_first': 7.222,
     'L0_attn_bo': 6.587}
    for name, (base, spread) in spreads.items():
        noise = np.random.default_rng([zlib.crc32(name.encode()), seed]).standard_normal(out[name].shape)
        drawn = base * np.exp(spread * noise) if base else spread * noise
        out[name] = jnp.asarray(drawn.astype(out[name].dtype))
    for name, factor in factors.items():
        out[name] = (out[name] * factor).astype(out[name].dtype)
    return out
```

```python
import numpy as np
import concourse.bass as bass
from concourse import mybir
from contextlib import ExitStack

F32 = mybir.dt.float32
F32R = mybir.dt.float32r
ALU = mybir.AluOpType
ACT = mybir.ActivationFunctionType
AX = mybir.AxisListType

P = 128
NB, NQ, DM = 32, 64, 256
NKV, DC = 1601, 192
NH, DH = 16, 64
INNER = NH * DH
HQ = NH * NQ
TOK = NB * NQ
TT = TOK // P
DCB = DC - P
SCALE = DH ** -0.5
EPS = 1e-5


def bits(ap):
    return ap.bitcast(F32)


def identity(nc, pool, ident, ident_done):
    nc.gpsimd.memset(ident[:, :], 0.0).then_inc(ident_done, 1)
    pool.wait_ge(ident_done, 1)
    nc.gpsimd.affine_select(out=ident[:, :], in_=ident[:, :], compare_op=ALU.not_equal, fill=1.0,
                            base=0, pattern=[[-1, P]], channel_multiplier=1).then_inc(ident_done, 1)


def project_queries(nc, x, w_q, w_kv, qk_dram):
    KB = DM // P
    NC, CT = 4, TOK // 4
    CB = CT // NQ
    HP = NH // 2
    HALF = HP // 2
    with ExitStack() as ctx:
        sb = lambda name, shape, dt=F32: ctx.enter_context(nc.sbuf_tensor("p1_" + name, shape, dt))
        pb = lambda name, shape: ctx.enter_context(nc.psum_tensor("p1_" + name, shape, F32))
        sem = lambda name: ctx.enter_context(nc.semaphore("p1_" + name))

        xt = sb("x", [P, TT, DM])
        stats = sb("stats", [P, TT, 6])
        mv = sb("mv", [P, TT, 2])
        std = sb("std", [P, 4, TT])
        wq = sb("wq", [P, KB, INNER])
        wq_hi, wq_lo = sb("wq_hi", [P, KB, INNER], F32R), sb("wq_lo", [P, KB, INNER], F32R)
        wk_a, wk_b = sb("wk_a", [P, INNER]), sb("wk_b", [DCB, INNER])
        wk2 = sb("wk2", [P, INNER // DH, 2, DH])
        wk2_b = sb("wk2_b", [DCB, INNER // DH, 2, DH])
        wks_hi, wks_lo = sb("wks_hi", [P, NH, DC], F32R), sb("wks_lo", [P, NH, DC], F32R)
        xT_hi, xT_lo = sb("xT_hi", [P, KB, TOK], F32R), sb("xT_lo", [P, KB, TOK], F32R)
        stack = sb("stack", [P, 2, 2, CT], F32R)
        out_a, out_b = sb("out_a", [P, CB, HALF * 2, NQ]), sb("out_b", [DCB, CB, HALF * 2, NQ])
        out_a2, out_b2 = sb("out_a2", [P, CB, HALF * 2, NQ]), sb("out_b2", [DCB, CB, HALF * 2, NQ])
        staged = ((out_a, out_b), (out_a2, out_b2))
        ident = sb("ident", [P, P])

        tp = [pb(f"tp{i}", [P, 512]) for i in range(2)]
        qp = [pb(f"qp{i}", [P, 512]) for i in range(2)]
        ap = [pb(f"ap{i}", [P, 512]) for i in range(2)]
        bp = [pb(f"bp{i}", [DCB, 512]) for i in range(2)]

        x_in, wq_in, wk_in = sem("x_in"), sem("wq_in"), sem("wk_in")
        ident_done, wq_hi_done, wq_lo_done, wk2_done = sem("ident"), sem("wqh"), sem("wql"), sem("wk2")
        stat_done, std_done, xn_done = sem("stat"), sem("std"), sem("xn")
        tp_ready, tp_hi, tp_lo = sem("tp_ready"), sem("tp_hi"), sem("tp_lo")
        q_ready, stack_hi, stack_lo = sem("q_ready"), sem("stack_hi"), sem("stack_lo")
        qk_ready, evac_act, evac_dve = sem("qk_ready"), sem("evac_act"), sem("evac_dve")
        stored = [sem("stored0"), sem("stored1")]
        block = ctx.enter_context(nc.Block())

        NT = NC * KB + NH // 2

        @block.sync
        def _(sp):
            sp.dma_start(xt[:, :, :], x.rearrange("(t b) q d -> (b q) t d", b=P // NQ)).then_inc(x_in, 16)
            sp.dma_start(wk_a[:, :], w_kv[0:P, 0:INNER]).then_inc(wk_in, 16)
            sp.dma_start(wk_b[:, :], w_kv[P:DC, 0:INNER]).then_inc(wk_in, 16)
            sp.dma_start(wq[:, :, :], w_q.rearrange("(k p) n -> p k n", p=P)).then_inc(wq_in, 16)
            with sp.Fori(0, NC) as c:
                for half in range(2):
                    sp.wait_ge(evac_act, c * (2 * HP) + (half + 1) * HP)
                    sp.wait_ge(evac_dve, c * (2 * HP) + (half + 1) * HP)
                    cols = slice(half * HALF * 2 * NQ, (half + 1) * HALF * 2 * NQ)
                    for buf, rows in zip(staged[half], (slice(0, P), slice(P, DC))):
                        dst = qk_dram[bass.ds(c * CB, CB), rows, cols].rearrange("b c n -> c b n")
                        sp.dma_start(dst, buf[:, :, :, :].rearrange("p b h q -> p b (h q)")).then_inc(stored[half], 16)
            sp.wait_ge(stored[0], 32 * NC)
            sp.wait_ge(stored[1], 32 * NC)

        @block.gpsimd
        def _(pool):
            identity(nc, pool, ident, ident_done)
            pool.wait_ge(wk_in, 32)
            for r in range(2):
                nc.gpsimd.tensor_copy(wk2[:, :, r, :], wk_a[:, :].rearrange("p (h d) -> p h d", d=DH)).then_inc(wk2_done, 1)
                nc.gpsimd.tensor_copy(wk2_b[:, :, r, :], wk_b[:, :].rearrange("p (h d) -> p h d", d=DH)).then_inc(wk2_done, 1)

        def evacuate(eng, scalar, c, j, first):
            half, jj = divmod(j, HALF)
            buf_a, buf_b = staged[half]
            for r in range(2):
                eng.wait_ge(qk_ready, c * NH + (2 * j + r + 1))
                if not first and jj == 0 and r == 0:
                    eng.wait_ge(stored[half], c * 32)
                first = (r == 0) == scalar
                dst = (buf_a if first else buf_b)[:, :, 2 * jj + r, :]
                src = (ap if first else bp)[r][:, :].rearrange("p (b q) -> p b q", q=NQ)
                if scalar:
                    nc.scalar.activation(dst, src, ACT.Copy).then_inc(evac_act, 1)
                else:
                    nc.vector.tensor_copy(dst, src).then_inc(evac_dve, 1)

        @block.scalar
        def _(act):
            act.wait_ge(stat_done, TT + TT + 1)
            nc.scalar.activation(std[:, 1, :], std[:, 0, :], ACT.Sqrt).then_inc(std_done, 1)
            act.wait_ge(wq_in, 16)
            nc.scalar.activation(wq_hi[:, :, :], wq[:, :, :], ACT.Copy).then_inc(wq_hi_done, 1)
            for n in range(NT):
                act.wait_ge(tp_ready, n + 1)
                if n < NC * KB:
                    c, k = divmod(n, KB)
                    nc.scalar.activation(xT_hi[:, k, c * CT:(c + 1) * CT], tp[n % 2][:, :], ACT.Copy).then_inc(tp_hi, 1)
                else:
                    h = 2 * (n - NC * KB)
                    nc.scalar.activation(wks_hi[:, h:h + 2, :], tp[n % 2][:, 0:2 * DC].rearrange("p (h c) -> p h c", c=DC),
                                         ACT.Copy).then_inc(tp_hi, 1)

            def chunk(c, first=False):
                for j in range(HP):
                    act.wait_ge(q_ready, c * HP + (j + 1))
                    if not first or j >= 2:
                        act.wait_ge(qk_ready, c * NH + 2 * (j - 1))
                    s = stack[:, j % 2]
                    nc.scalar.activation(s[0:DH, 0, :], qp[j % 2][0:DH, :], ACT.Copy, scale=SCALE)
                    nc.scalar.activation(s[DH:P, 1, :], qp[j % 2][DH:P, :], ACT.Copy, scale=SCALE).then_inc(stack_hi, 1)
                    if j >= 1:
                        evacuate(act, True, c, j - 1, first)
                evacuate(act, True, c, HP - 1, first)

            chunk(0, first=True)
            with act.Fori(1, NC) as c:
                chunk(c)

        @block.vector
        def _(dve):
            dve.wait_ge(x_in, 16)
            for t in range(TT):
                nc.vector.bn_stats(stats[:, t, :], xt[:, t, :]).then_inc(stat_done, 1)
            for t in range(TT):
                dve.wait_ge(stat_done, t + 1)
                nc.vector.bn_aggr(mv[:, t, :], stats[:, t, :]).then_inc(stat_done, 1)
            dve.wait_ge(stat_done, 2 * TT)
            nc.vector.tensor_scalar(std[:, 0, :], mv[:, :, 1], EPS, None, ALU.add).then_inc(stat_done, 1)
            dve.wait_ge(std_done, 1)
            newton_rstd(nc, dve, std, std_done)
            for t in range(TT):
                nc.vector.tensor_scalar(xt[:, t, :], xt[:, t, :], mv[:, t, 0:1], std[:, 3, t:t + 1],
                                        ALU.subtract, ALU.mult).then_inc(xn_done, 1)
            for n in range(NT):
                dve.wait_ge(tp_hi, n + 1)
                if n < NC * KB:
                    c, k = divmod(n, KB)
                    cols = slice(c * CT, (c + 1) * CT)
                    nc.vector.tensor_tensor(xT_lo[:, k, cols], tp[n % 2][:, :], bits(xT_hi[:, k, cols]),
                                            ALU.subtract).then_inc(tp_lo, 1)
                else:
                    h = 2 * (n - NC * KB)
                    nc.vector.tensor_tensor(wks_lo[:, h:h + 2, :], tp[n % 2][:, 0:2 * DC].rearrange("p (h c) -> p h c", c=DC),
                                            bits(wks_hi[:, h:h + 2, :]), ALU.subtract).then_inc(tp_lo, 1)
            dve.wait_ge(wq_hi_done, 1)
            nc.vector.tensor_tensor(wq_lo[:, :, :], wq[:, :, :], bits(wq_hi[:, :, :]), ALU.subtract).then_inc(wq_lo_done, 1)

            def chunk(c, first=False):
                for j in range(HP):
                    dve.wait_ge(stack_hi, c * HP + (j + 1))
                    s, q = stack[:, j % 2], qp[j % 2]
                    nc.vector.scalar_tensor_tensor(s[DH:P, 0, :], q[0:DH, :], SCALE, bits(s[0:DH, 0, :]), ALU.mult, ALU.subtract)
                    nc.vector.scalar_tensor_tensor(s[0:DH, 1, :], q[DH:P, :], SCALE, bits(s[DH:P, 1, :]), ALU.mult,
                                                   ALU.subtract).then_inc(stack_lo, 1)
                    if j >= 1:
                        evacuate(dve, False, c, j - 1, first)
                evacuate(dve, False, c, HP - 1, first)

            chunk(0, first=True)
            with dve.Fori(1, NC) as c:
                chunk(c)

        @block.tensor
        def _(pe):
            pe.wait_ge(ident_done, 2)
            for n in range(NT):
                if n >= 2:
                    pe.wait_ge(tp_lo, n - 1)
                if n < NC * KB:
                    c, k = divmod(n, KB)
                    per = CT // P
                    pe.wait_ge(xn_done, (c + 1) * per)
                    for i in range(per):
                        last = nc.tensor.transpose(tp[n % 2][:, i * P:(i + 1) * P],
                                                   xt[:, c * per + i, k * P:(k + 1) * P], ident[:, :])
                else:
                    h = 2 * (n - NC * KB)
                    pe.wait_ge(wk2_done, 4)
                    for r in range(2):
                        dst = tp[n % 2][:, r * DC:(r + 1) * DC]
                        nc.tensor.transpose(dst[:, 0:P], wk2[:, h + r, :, :].rearrange("p r d -> p (r d)"), ident[:, :])
                        last = nc.tensor.transpose(dst[:, P:DC], wk2_b[:, h + r, :, :].rearrange("p r d -> p (r d)"),
                                                   ident[0:DCB, 0:DCB])
                last.then_inc(tp_ready, 1)
            pe.wait_ge(wq_lo_done, 1)
            pe.wait_ge(tp_lo, NT)

            def q_pair(c, j, first):
                if not first or j >= 2:
                    pe.wait_ge(stack_lo, c * HP + (j - 1))
                terms = [(wh, xh, k) for k in range(KB) for wh, xh in ((wq_hi, xT_hi), (wq_lo, xT_hi), (wq_hi, xT_lo))]
                for n, (w, xv, k) in enumerate(terms):
                    last = nc.tensor.matmul(qp[j % 2][:, :], w[:, k, j * P:(j + 1) * P], xv[:, k, bass.ds(c * CT, CT)],
                                            start=n == 0, stop=n == len(terms) - 1)
                last.then_inc(q_ready, 1)

            def qk_pair(c, j, first):
                pe.wait_ge(stack_lo, c * HP + (j + 1))
                for r in range(2):
                    s = stack[:, j % 2, r, :]
                    if not first or j >= 1:
                        pe.wait_ge(evac_act, c * NH + (2 * (j - 1) + r + 1))
                        pe.wait_ge(evac_dve, c * NH + (2 * (j - 1) + r + 1))
                    h = 2 * j + r
                    for n, w in enumerate((wks_hi, wks_lo)):
                        nc.tensor.matmul(ap[r][:, :], w[:, h, 0:P], s, start=n == 0, stop=n == 1)
                    for n, w in enumerate((wks_hi, wks_lo)):
                        last = nc.tensor.matmul(bp[r][:, :], w[:, h, P:DC], s, start=n == 0, stop=n == 1)
                    last.then_inc(qk_ready, 1)

            def chunk(c, first=False):
                q_pair(c, 0, first)
                for j in range(HP):
                    if j + 1 < HP:
                        q_pair(c, j + 1, first)
                    qk_pair(c, j, first)

            chunk(0, first=True)
            with pe.Fori(1, NC) as c:
                chunk(c)


def newton_rstd(nc, dve, std, std_done):
    nc.vector.reciprocal(std[:, 2, :], std[:, 1, :]).then_inc(std_done, 1)
    dve.wait_ge(std_done, 2)
    nc.vector.tensor_tensor(std[:, 2, :], std[:, 2, :], std[:, 0, :], ALU.mult).then_inc(std_done, 1)
    dve.wait_ge(std_done, 3)
    nc.vector.tensor_tensor(std[:, 1, :], std[:, 1, :], std[:, 2, :], ALU.add).then_inc(std_done, 1)
    dve.wait_ge(std_done, 4)
    nc.vector.reciprocal(std[:, 2, :], std[:, 1, :]).then_inc(std_done, 1)
    dve.wait_ge(std_done, 5)
    nc.vector.tensor_scalar(std[:, 3, :], std[:, 2, :], 2.0, None, ALU.mult).then_inc(std_done, 1)
    dve.wait_ge(std_done, 6)


def attend(nc, ctx_in, ctxT_in, qk_dram, o_dram):
    KT = -(-NKV // P)
    FULL = KT - 1
    TAIL = NKV - FULL * P
    SB = HQ // P
    STEPS = SB * NB
    QC = 2 * P
    QB = SB // 2
    TG = [range(0, 4), range(4, 8), range(8, 12), range(12, KT)]
    NG = len(TG)
    CW = NKV + NKV % 2
    EDGE = (CW - 2 * 512) // 4 * 2
    CHUNKS = [(0, EDGE), (EDGE, EDGE + 512), (EDGE + 512, EDGE + 1024), (EDGE + 1024, CW)]
    S0 = 512 - EDGE
    FIRST_PART = 7
    SPB = 2
    with ExitStack() as ctx:
        sb = lambda name, shape, dt=F32: ctx.enter_context(nc.sbuf_tensor("p2_" + name, shape, dt))
        pb = lambda name, shape: ctx.enter_context(nc.psum_tensor("p2_" + name, shape, F32))
        sem = lambda name: ctx.enter_context(nc.semaphore("p2_" + name))

        raw = sb("raw", [P, KT, DC])
        nat = [sb(f"nat{i}", [P, KT, 2 * DC], F32R) for i in range(2)]
        ct_raw = sb("ct_raw", [P, CW])
        ct_hi = [sb(f"ct_hi{i}", [P, 2, CW], F32R) for i in range(2)]
        ct_lo = [sb(f"ct_lo{i}", [P, CW], F32R) for i in range(2)]
        qraw = sb("qraw", [P, 2, HQ])
        q_hi = [sb(f"q_hi{i}", [P, 2, HQ], F32R) for i in range(2)]
        q_lo = [sb(f"q_lo{i}", [P, 2, HQ], F32R) for i in range(2)]
        prob = [sb(f"prob{i}", [P, NKV]) for i in range(2)]
        pt_hi = [sb(f"pt_hi{i}", [P, KT, QC], F32R) for i in range(2)]
        pt_lo = [sb(f"pt_lo{i}", [P, KT, QC], F32R) for i in range(2)]
        o_a = [sb(f"o_a{i}", [P, QC]) for i in range(2)]
        o_b = [sb(f"o_b{i}", [P, QC]) for i in range(2)]
        negmax, rowsum, rinv = sb("negmax", [P, 2]), sb("rowsum", [P, 2]), sb("rinv", [P, 2])
        ident, zero = sb("ident", [P, P]), sb("zero", [P, 1])

        scores = pb("scores", [P, 2048])
        work = [pb(f"work{i}", [P, 512]) for i in range(3)]
        acc = pb("acc", [P, 2, QC])
        WORK_OF = (0, 1, 2, 0)

        raw_in, qk_in = sem("raw_in"), sem("qk_in")
        ct_a_in, ct_b_in = sem("ct_a_in"), sem("ct_b_in")
        zero_done = sem("zero_done")
        ident_done, raw_pad, prob_pad = sem("ident"), sem("raw_pad"), sem("prob_pad")
        nat_hi_done, nat_done = sem("nat_hi_done"), sem("nat_done")
        q_hi_done, q_done = sem("q_hi_done"), sem("q_done")
        ct_a_hi_done, ct_a_done = sem("ct_a_hi_done"), sem("ct_a_done")
        ct_b_hi_done, ct_b_done = sem("ct_b_hi_done"), sem("ct_b_done")
        scores_ready, max_done, exp_done = sem("scores_ready"), sem("max_done"), sem("exp_done")
        rinv_done, prob_done = sem("rinv_done"), sem("prob_done")
        pt_ready, pt_hi_done, pt_lo_done = sem("pt_ready"), sem("pt_hi_done"), sem("pt_lo_done")
        acc_ready, acc_act, acc_dve = sem("acc_ready"), sem("acc_act"), sem("acc_dve")
        stored = [sem("stored0"), sem("stored1")]
        block = ctx.enter_context(nc.Block())

        SPP, QPP = SPB * SB, SPB * QB

        def passes(eng, body):
            body(0, True, False)
            with eng.Fori(1, NB // SPB - 1) as r:
                body(r, False, False)
            body(NB // SPB - 1, False, True)

        @block.sync
        def _(sp):
            def load_raw(n):
                src = ctx_in[bass.ds(n, 1), :, :].rearrange("a k c -> (a k) c")
                sp.dma_start(raw[:, 0:FULL, :], src[0:FULL * P, :].rearrange("(t p) c -> p t c", p=P)).then_inc(raw_in, 16)
                sp.dma_start(raw[0:TAIL, FULL, :], src[FULL * P:NKV, :]).then_inc(raw_in, 16)

            def load_ct_a(n):
                src = ctxT_in[bass.ds(n, 1), :, :].rearrange("a c k -> (a c) k")
                sp.dma_start(ct_raw[:, 0:NKV], src[0:P, :]).then_inc(ct_a_in, 16)

            def load_ct_b(n):
                src = ctxT_in[bass.ds(n, 1), :, :].rearrange("a c k -> (a c) k")
                sp.dma_start(ct_raw[0:DCB, 0:NKV], src[P:DC, :]).then_inc(ct_b_in, 16)
                sp.dma_start(ct_raw[DCB:P, 0:NKV], src[P:DC, :]).then_inc(ct_b_in, 16)

            def load_qk(n):
                src = qk_dram[bass.ds(n, 1), :, :].rearrange("a c n -> (a c) n")
                sp.dma_start(qraw[:, 0, :], src[0:P, :]).then_inc(qk_in, 16)
                sp.dma_start(qraw[0:DCB, 1, :], src[P:DC, :]).then_inc(qk_in, 16)
                sp.dma_start(qraw[DCB:P, 1, :], src[P:DC, :]).then_inc(qk_in, 16)

            def store(i, b, quarter, parity):
                sp.wait_ge(acc_act, i + 1)
                sp.wait_ge(acc_dve, i + 1)
                dst = o_dram[bass.ds(b, 1), :, quarter * QC:(quarter + 1) * QC].rearrange("a c n -> (a c) n")
                sp.dma_start(dst[0:P, :], o_a[parity][:, :]).then_inc(stored[parity], 16)
                sp.dma_start(dst[P:DC, :], o_b[parity][0:DCB, :]).then_inc(stored[parity], 16)

            def body(r, first, last):
                for u in range(SPB):
                    b = r * SPB + u
                    i = r * QPP + u * QB
                    final = last and u == SPB - 1
                    if not (first and u == 0):
                        store(i - 2, b - 1, QB - 2, 0)
                    if not final:
                        sp.wait_ge(ct_a_done, b + 2)
                        load_ct_b(b + 1)
                    if not last:
                        sp.wait_ge(q_done, b + 2)
                        load_qk(b + 2)
                    if not (first and u == 0):
                        store(i - 1, b - 1, QB - 1, 1)
                    if not last:
                        sp.wait_ge(ct_b_done, b + 2)
                        load_ct_a(b + 2)
                    store(i, b, 0, 0)
                    if not last:
                        sp.wait_ge(nat_done, b + 2)
                        load_raw(b + 2)
                    store(i + 1, b, 1, 1)

            sp.wait_ge(raw_pad, 2)
            load_ct_a(0)
            load_qk(0)
            load_raw(0)
            sp.wait_ge(ct_a_done, 1)
            load_ct_b(0)
            sp.wait_ge(q_done, 1)
            load_qk(1)
            sp.wait_ge(ct_b_done, 1)
            load_ct_a(1)
            sp.wait_ge(nat_done, 1)
            load_raw(1)
            passes(sp, body)
            store(NB * QB - 2, NB - 1, QB - 2, 0)
            store(NB * QB - 1, NB - 1, QB - 1, 1)
            for s in stored:
                sp.wait_ge(s, 32 * NB * QB // 2)

        @block.gpsimd
        def _(pool):
            nc.gpsimd.memset(raw[:, FULL, :], 0.0).then_inc(raw_pad, 1)
            nc.gpsimd.memset(ct_raw[:, NKV:CW], 0.0).then_inc(raw_pad, 1)
            for i in range(2):
                nc.gpsimd.memset(bits(pt_hi[i][:, FULL, :]), 0.0).then_inc(prob_pad, 1)
                nc.gpsimd.memset(bits(pt_lo[i][:, FULL, :]), 0.0).then_inc(prob_pad, 1)
            nc.gpsimd.memset(zero[:, :], 0.0).then_inc(zero_done, 1)
            pool.wait_ge(zero_done, 1)
            identity(nc, pool, ident, ident_done)

            def round_to(dst, src):
                flat = (zero[:, :] if len(src.shape) == 2 else zero[:, :].unsqueeze(1)).broadcast_to(src.shape)
                return nc.gpsimd.tensor_tensor(dst, src, flat, ALU.add)

            def prepare(n, par, fresh):
                pool.wait_ge(ct_a_in, (n + 1) * 16)
                if not fresh:
                    pool.wait_ge(scores_ready, (n - 1) * SB)
                round_to(ct_hi[par][:, 0, :], ct_raw[:, :]).then_inc(ct_a_hi_done, 1)
                pool.wait_ge(ct_a_hi_done, n + 1)
                nc.gpsimd.tensor_tensor(ct_lo[par][:, :], ct_raw[:, :], bits(ct_hi[par][:, 0, :]),
                                        ALU.subtract).then_inc(ct_a_done, 1)
                pool.wait_ge(qk_in, (n + 1) * 48)
                round_to(q_hi[par][:, :, :], qraw[:, :, :]).then_inc(q_hi_done, 1)
                pool.wait_ge(q_hi_done, n + 1)
                nc.gpsimd.tensor_tensor(q_lo[par][:, :, :], qraw[:, :, :], bits(q_hi[par][:, :, :]),
                                        ALU.subtract).then_inc(q_done, 1)
                lower = slice(DCB, P)
                pool.wait_ge(ct_b_in, (n + 1) * 32)
                round_to(ct_hi[par][:, 1, :], ct_raw[:, :]).then_inc(ct_b_hi_done, 1)
                pool.wait_ge(ct_b_hi_done, n + 1)
                nc.gpsimd.tensor_tensor(ct_hi[par][lower, 1, :], ct_raw[lower, :], bits(ct_hi[par][lower, 1, :]),
                                        ALU.subtract).then_inc(ct_b_done, 1)
                x = nat[par]
                pool.wait_ge(ct_b_done, n + 1)
                pool.wait_ge(raw_in, (n + 1) * 32)
                if not fresh:
                    pool.wait_ge(acc_ready, (n - 1) * QB)
                round_to(x[:, :, 0:DC], raw[:, :, :]).then_inc(nat_hi_done, 1)
                pool.wait_ge(nat_hi_done, n + 1)
                nc.gpsimd.tensor_tensor(x[:, :, DC:DC + DCB], raw[:, :, P:DC], bits(x[:, :, P:DC]), ALU.subtract)
                nc.gpsimd.tensor_tensor(x[:, :, DC + DCB:2 * DC], raw[:, :, 0:P], bits(x[:, :, 0:P]),
                                        ALU.subtract).then_inc(nat_done, 1)

            def body(r, first, last):
                for u in range(SPB):
                    if not (last and u == SPB - 1):
                        prepare(r * SPB + (u + 1), (u + 1) % 2, first and u == 0)

            prepare(0, 0, True)
            passes(pool, body)

        def transposed(buf, slot, g, half):
            tiles, rows = TG[g], slice(0, TAIL if g == NG - 1 else P)
            src = work[WORK_OF[g]][rows, 0:len(tiles) * P].rearrange("p (t n) -> p t n", n=P)
            return src, buf[slot][rows, tiles[0]:tiles[-1] + 1, half * P:(half + 1) * P]

        @block.scalar
        def _(act):
            def pt_copy(s, g, slot, half):
                act.wait_ge(pt_ready, s * NG + (g + 1))
                src, dst = transposed(pt_hi, slot, g, half)
                nc.scalar.activation(dst, src, ACT.Copy).then_inc(pt_hi_done, 1)

            def acc_copy(i, parity, fresh):
                if not fresh:
                    act.wait_ge(stored[parity], (i - parity) * 16)
                act.wait_ge(acc_ready, i + 1)
                nc.scalar.activation(o_a[parity][:, :], acc[:, 0, :], ACT.Copy)
                nc.scalar.activation(o_b[parity][DCB:P, :], acc[DCB:P, 1, :], ACT.Copy).then_inc(acc_act, 1)

            def step(r, j, first, last):
                s = r * SPP + j
                prev = not (first and j == 0)
                if prev:
                    slot, half = ((j - 1) // 2) % 2, (j - 1) % 2
                    if first and j == 1:
                        act.wait_ge(prob_pad, 4)
                    if not (first and j < 5):
                        act.wait_ge(acc_ready, r * QPP + ((j - 1) // 2 - 1))
                    pt_copy(s - 1, 0, slot, half)
                    pt_copy(s - 1, 1, slot, half)
                act.wait_ge(max_done, s + 1)
                nc.scalar.activation(prob[j % 2][:, 0:NKV], scores[:, S0:S0 + NKV], ACT.Exp, bias=negmax[:, j % 2:j % 2 + 1],
                                     accum_out=rowsum[:, j % 2:j % 2 + 1]).then_inc(exp_done, 1)
                if prev:
                    pt_copy(s - 1, 2, slot, half)
                act.wait_ge(rinv_done, s + 1)
                nc.scalar.activation(prob[j % 2][:, 0:NKV], prob[j % 2][:, 0:NKV], ACT.Copy,
                                     scale=rinv[:, j % 2:j % 2 + 1]).then_inc(prob_done, 1)
                if prev:
                    pt_copy(s - 1, 3, slot, half)
                if j % 2 == 0 and not (first and j < 4):
                    acc_copy(r * QPP + (j // 2 - 2), (j // 2) % 2, first and j < 8)

            def body(r, first, last):
                for j in range(SPP):
                    step(r, j, first, last)

            passes(act, body)
            act.wait_ge(acc_ready, STEPS // 2 - 2)
            for g in range(NG):
                pt_copy(STEPS - 1, g, 1, 1)
            acc_copy(NB * QB - 2, 0, False)
            acc_copy(NB * QB - 1, 1, False)

        @block.vector
        def _(dve):
            def pt_sub(s, g, slot, half):
                dve.wait_ge(pt_hi_done, s * NG + (g + 1))
                src, lo = transposed(pt_lo, slot, g, half)
                _, hi = transposed(pt_hi, slot, g, half)
                nc.vector.tensor_tensor(lo, src, bits(hi), ALU.subtract).then_inc(pt_lo_done, 1)

            def acc_add(i, parity):
                dve.wait_ge(acc_act, i + 1)
                nc.vector.tensor_tensor(o_b[parity][0:DCB, :], acc[0:DCB, 1, :], o_b[parity][DCB:P, :],
                                        ALU.add).then_inc(acc_dve, 1)

            def step(r, j, first, last):
                s = r * SPP + j
                prev = not (first and j == 0)
                slot, half = ((j - 1) // 2) % 2, (j - 1) % 2
                dve.wait_ge(scores_ready, s + 1)
                nc.vector.tensor_reduce(negmax[:, j % 2:j % 2 + 1], scores[:, S0:S0 + NKV], AX.X, ALU.max,
                                        negate=True).then_inc(max_done, 1)
                if prev:
                    pt_sub(s - 1, 0, slot, half)
                    pt_sub(s - 1, 1, slot, half)
                dve.wait_ge(exp_done, s + 1)
                nc.vector.reciprocal(rinv[:, j % 2:j % 2 + 1], rowsum[:, j % 2:j % 2 + 1]).then_inc(rinv_done, 1)
                if prev:
                    pt_sub(s - 1, 2, slot, half)
                    pt_sub(s - 1, 3, slot, half)
                if j % 2 == 0 and not (first and j < 4):
                    acc_add(r * QPP + (j // 2 - 2), (j // 2) % 2)

            def body(r, first, last):
                for j in range(SPP):
                    step(r, j, first, last)

            passes(dve, body)
            for g in range(NG):
                pt_sub(STEPS - 1, g, 1, 1)
            acc_add(NB * QB - 2, 0)
            acc_add(NB * QB - 1, 1)

        @block.tensor
        def _(pe):
            def step_scores(r, j, par, first):
                s, b = r * SPP + j, r * SPB + j // SB
                if j % SB == 0:
                    pe.wait_ge(ct_b_done, b + 1)
                    pe.wait_ge(q_done, b + 1)
                if not (first and j == 0):
                    pe.wait_ge(exp_done, s)
                rows = slice((j % SB) * P, (j % SB + 1) * P)
                q_a, q_b = (slice(None), 0, rows), (slice(None), 1, rows)
                for lo, hi in CHUNKS:
                    ct_a, ct_b, ct_al = (t[:, lo:hi] for t in (ct_hi[par][:, 0, :], ct_hi[par][:, 1, :], ct_lo[par]))
                    terms = ((q_hi[par][q_a], ct_a), (q_lo[par][q_a], ct_a), (q_hi[par][q_a], ct_al),
                             (q_hi[par][q_b], ct_b), (q_lo[par][q_b], ct_b))
                    for m, (w, c) in enumerate(terms):
                        last = nc.tensor.matmul(scores[:, S0 + lo:S0 + hi], w, c, start=m == 0, stop=m == len(terms) - 1)
                last.then_inc(scores_ready, 1)

            def pt_transpose(s, g, j):
                for k, t in enumerate(TG[g]):
                    width = min(P, NKV - t * P)
                    last = nc.tensor.transpose(work[WORK_OF[g]][0:width, k * P:(k + 1) * P],
                                               prob[(j - 1) % 2][:, t * P:t * P + width], ident[:, :])
                last.then_inc(pt_ready, 1)

            def product(slot, par, tiles):
                x = nat[par]
                for k in tiles:
                    a_hi, b_both, a_lo = x[:, k, 0:P], x[:, k, P:P + 2 * DCB], x[:, k, DC + DCB:2 * DC]
                    terms = ((0, a_hi, pt_hi), (0, a_hi, pt_lo), (0, a_lo, pt_hi), (1, b_both, pt_hi), (1, b_both, pt_lo))
                    for m, (blk, w, pt) in enumerate(terms):
                        last = nc.tensor.matmul(acc[:, blk, :], w, pt[slot][:, k, :], start=k == 0 and m == 0,
                                                stop=k == KT - 1 and m in (2, 4), skip_group_check=True)
                if tiles[-1] == KT - 1:
                    last.then_inc(acc_ready, 1)

            def step(r, j, first, last):
                s = r * SPP + j
                prev = not (first and j == 0)
                step_scores(r, j, (j // SB) % 2, first)
                work_left, q_at = [], None
                if j % 2 == 1 and not (first and j < 3):
                    q_at, work_left = (j - 3) // 2, list(range(0, FIRST_PART))
                elif j % 2 == 0 and not (first and j < 4):
                    q_at, work_left = (j - 4) // 2, list(range(FIRST_PART, KT))
                slot, par = (q_at % 2, (q_at // QB) % 2) if q_at is not None else (0, 0)
                if work_left and j % 2 == 1:
                    i = r * QPP + (j - 3) // 2
                    if (j - 3) // 2 % QB == 0:
                        pe.wait_ge(nat_done, r * SPB + (j - 3) // SB + 1)
                    pe.wait_ge(pt_lo_done, (i + 1) * 2 * NG)
                    if not (first and j == 3):
                        pe.wait_ge(acc_dve, i)
                if prev:
                    pe.wait_ge(prob_done, s)
                    if not (first and j == 1):
                        pe.wait_ge(pt_lo_done, (s - 1) * NG)
                    pt_transpose(s - 1, 0, j)
                    pt_transpose(s - 1, 1, j)
                if work_left:
                    product(slot, par, work_left[0:4])
                if prev:
                    pt_transpose(s - 1, 2, j)
                if work_left:
                    product(slot, par, work_left[4:6])
                if prev:
                    pe.wait_ge(pt_lo_done, (s - 1) * NG + 1)
                    pt_transpose(s - 1, 3, j)
                if work_left[6:]:
                    product(slot, par, work_left[6:])

            def body(r, first, last):
                for j in range(SPP):
                    step(r, j, first, last)

            pe.wait_ge(ident_done, 2)
            passes(pe, body)
            pe.wait_ge(prob_done, STEPS)
            pe.wait_ge(pt_lo_done, (STEPS - 1) * NG)
            for g in range(3):
                pt_transpose(STEPS - 1, g, 2)
            pe.wait_ge(pt_lo_done, (STEPS - 1) * NG + 1)
            pt_transpose(STEPS - 1, 3, 2)
            product(0, 1, list(range(FIRST_PART, KT)))
            pe.wait_ge(pt_lo_done, STEPS * NG)
            pe.wait_ge(acc_dve, NB * QB - 1)
            product(1, 1, list(range(KT)))


def attention_output(nc, w_kv, w_out, b_out, x, o_dram, resid):
    NC, CT = 4, TOK // 4
    CB, CTT = CT // NQ, CT // P
    HP = NH // 2
    PL = 2
    NL = HP // PL
    W = PL * 2 * NQ
    with ExitStack() as ctx:
        sb = lambda name, shape, dt=F32: ctx.enter_context(nc.sbuf_tensor("p3_" + name, shape, dt))
        pb = lambda name, shape: ctx.enter_context(nc.psum_tensor("p3_" + name, shape, F32))
        sem = lambda name: ctx.enter_context(nc.semaphore("p3_" + name))

        wv = sb("wv", [P, 2, INNER])
        wo = sb("wo", [P, HP, DM])
        wv_hi, wv_lo = sb("wv_hi", [P, 2, HP, 2, P], F32R), sb("wv_lo", [P, 2, HP, 2, P], F32R)
        wo_hi, wo_lo = sb("wo_hi", [P, HP, DM], F32R), sb("wo_lo", [P, HP, DM], F32R)
        bias = sb("bias", [P, DM])
        oa = [sb(f"oa{i}", [P, CB, W]) for i in range(2)]
        ob = [sb(f"ob{i}", [P, CB, W]) for i in range(2)]
        oa_hi = [sb(f"oa_hi{i}", [P, CB, W], F32R) for i in range(2)]
        oa_lo = [sb(f"oa_lo{i}", [P, CB, W], F32R) for i in range(2)]
        ob_both = [sb(f"ob_both{i}", [P, CB, W], F32R) for i in range(2)]
        at_hi, at_lo = sb("at_hi", [P, HP, CT], F32R), sb("at_lo", [P, HP, CT], F32R)
        vp = [pb(f"vp{i}", [P, CT]) for i in range(2)]
        yp = [pb(f"yp{i}", [P, 512]) for i in range(2)]

        w_in, x_in, b_in = sem("w_in"), sem("x_in"), sem("b_in")
        o_in = [sem("o_in0"), sem("o_in1")]
        zeroed, w_hi_done, w_lo_done, biased = sem("zeroed"), sem("w_hi"), sem("w_lo"), sem("biased")
        o_hi, o_lo = sem("o_hi"), sem("o_lo")
        v_ready, at_hi_done, at_lo_done = sem("v_ready"), sem("at_hi"), sem("at_lo")
        y_ready, y_added = sem("y_ready"), sem("y_added")
        block = ctx.enter_context(nc.Block())

        @block.sync
        def _(sp):
            sp.dma_start(wv[:, 0, :], w_kv[0:P, INNER:2 * INNER]).then_inc(w_in, 16)
            for half in (slice(0, DCB), slice(DCB, P)):
                sp.dma_start(wv[half, 1, :], w_kv[P:DC, INNER:2 * INNER]).then_inc(w_in, 16)
            sp.dma_start(wo[:, :, :], w_out.rearrange("(j p) n -> p j n", p=P)).then_inc(w_in, 16)

            def load(c, l, fresh):
                if not fresh:
                    sp.wait_ge(o_lo, c * NL + (l - 1))
                src = o_dram[bass.ds(c * CB, CB), :, l * W:(l + 1) * W]
                for dst, rows in ((oa[l % 2][:, :, :], slice(0, P)), (ob[l % 2][0:DCB], slice(P, DC)), (ob[l % 2][DCB:P], slice(P, DC))):
                    sp.dma_start(dst, src[:, rows, :].rearrange("b c n -> c b n")).then_inc(o_in[l % 2], 16)

            for l in range(2):
                load(0, l, True)
            sp.dma_start(resid[:, :, :], x.rearrange("(t b) q d -> (b q) t d", b=P // NQ)).then_inc(x_in, 16)
            sp.dma_start(bias[:, :], b_out.rearrange("(a n) -> a n", a=1).partition_broadcast(P)).then_inc(b_in, 16)
            for l in range(2, NL):
                load(0, l, False)
            with sp.Fori(1, NC) as c:
                for l in range(NL):
                    load(c, l, False)

        @block.gpsimd
        def _(pool):
            nc.gpsimd.memset(bits(wv_hi[:, :, :, :, :]), 0.0).then_inc(zeroed, 1)
            nc.gpsimd.memset(bits(wv_lo[:, :, :, :, :]), 0.0).then_inc(zeroed, 1)
            pool.wait_ge(x_in, 16)
            pool.wait_ge(b_in, 16)
            for t in range(TT):
                nc.gpsimd.tensor_tensor(resid[:, t, :], resid[:, t, :], bias[:, :], ALU.add).then_inc(biased, 1)

        def wv_place(dst, blk, r):
            half = slice(r * DH, (r + 1) * DH)
            return dst[:, blk, :, r, half], wv[:, blk, :].rearrange("p (j r d) -> p j r d", r=2, d=DH)[:, :, r, :]

        @block.scalar
        def _(act):
            act.wait_ge(w_in, 64)
            act.wait_ge(zeroed, 2)
            for blk in range(2):
                for r in range(2):
                    dst, src = wv_place(wv_hi, blk, r)
                    nc.scalar.activation(dst, src, ACT.Copy).then_inc(w_hi_done, 1)

            def split(c, l, fresh):
                act.wait_ge(o_in[l % 2], c * (NL // 2 * 48) + (l // 2 + 1) * 48)
                if not fresh:
                    act.wait_ge(v_ready, c * HP + (l - 1) * PL)
                nc.scalar.activation(oa_hi[l % 2][:, :, :], oa[l % 2][:, :, :], ACT.Copy)
                nc.scalar.activation(ob_both[l % 2][:, :, :], ob[l % 2][:, :, :], ACT.Copy).then_inc(o_hi, 1)

            def chunk(c, first):
                for l in range(NL):
                    if l + 1 < NL:
                        split(c, l + 1, first and l == 0)
                    for j in range(l * PL, (l + 1) * PL):
                        act.wait_ge(v_ready, c * HP + (j + 1))
                        if j == 0 and not first:
                            act.wait_ge(y_ready, c * CTT)
                        nc.scalar.activation(at_hi[:, j, :], vp[j % 2][:, :], ACT.Copy).then_inc(at_hi_done, 1)

            split(0, 0, True)
            nc.scalar.activation(wo_hi[:, :, :], wo[:, :, :], ACT.Copy).then_inc(w_hi_done, 1)
            chunk(0, True)
            with act.Fori(1, NC) as c:
                split(c, 0, False)
                chunk(c, False)

        @block.vector
        def _(dve):
            for blk in range(2):
                for r in range(2):
                    dst, src = wv_place(wv_lo, blk, r)
                    hi, _ = wv_place(wv_hi, blk, r)
                    dve.wait_ge(w_hi_done, blk * 2 + r + 1)
                    nc.vector.tensor_tensor(dst, src, bits(hi), ALU.subtract).then_inc(w_lo_done, 1)

            def split(c, l):
                dve.wait_ge(o_hi, c * NL + (l + 1))
                lower = slice(DCB, P)
                nc.vector.tensor_tensor(oa_lo[l % 2][:, :, :], oa[l % 2][:, :, :], bits(oa_hi[l % 2][:, :, :]), ALU.subtract)
                nc.vector.tensor_tensor(ob_both[l % 2][lower], ob[l % 2][lower], bits(ob_both[l % 2][lower]),
                                        ALU.subtract).then_inc(o_lo, 1)

            def chunk(c, first):
                for l in range(NL):
                    if l + 1 < NL:
                        split(c, l + 1)
                    for j in range(l * PL, (l + 1) * PL):
                        dve.wait_ge(at_hi_done, c * HP + (j + 1))
                        nc.vector.tensor_tensor(at_lo[:, j, :], vp[j % 2][:, :], bits(at_hi[:, j, :]),
                                                ALU.subtract).then_inc(at_lo_done, 1)
                for t in range(CTT):
                    if t == 0 and first:
                        dve.wait_ge(biased, TT)
                    dve.wait_ge(y_ready, c * CTT + (t + 1))
                    tile = resid[:, bass.ds(c * CTT + t, 1), :].rearrange("p a d -> p (a d)")
                    nc.vector.tensor_tensor(tile, yp[t % 2][:, 0:DM], tile, ALU.add).then_inc(y_added, 1)

            split(0, 0)
            dve.wait_ge(w_hi_done, 5)
            nc.vector.tensor_tensor(wo_lo[:, :, :], wo[:, :, :], bits(wo_hi[:, :, :]), ALU.subtract).then_inc(w_lo_done, 1)
            chunk(0, True)
            with dve.Fori(1, NC) as c:
                split(c, 0)
                chunk(c, False)

        @block.tensor
        def _(pe):
            def values(c, l, first):
                pe.wait_ge(o_lo, c * NL + (l + 1))
                for j in range(l * PL, (l + 1) * PL):
                    if not (first and j < 2):
                        pe.wait_ge(at_lo_done, c * HP + (j - 1))
                    terms = []
                    for r in range(2):
                        h = slice((2 * (j - l * PL) + r) * NQ, (2 * (j - l * PL) + r + 1) * NQ)
                        a_hi, a_lo, b_both = oa_hi[l % 2][:, :, h], oa_lo[l % 2][:, :, h], ob_both[l % 2][:, :, h]
                        terms += [(wv_hi[:, 0, j, r, :], a_hi), (wv_lo[:, 0, j, r, :], a_hi), (wv_hi[:, 0, j, r, :], a_lo),
                                  (wv_hi[:, 1, j, r, :], b_both), (wv_lo[:, 1, j, r, :], b_both)]
                    for m, (w, o) in enumerate(terms):
                        last = nc.tensor.matmul(vp[j % 2][:, :].rearrange("p (b q) -> p b q", q=NQ), w, o,
                                                start=m == 0, stop=m == len(terms) - 1)
                    last.then_inc(v_ready, 1)

            def output(c, t, first):
                if t == 0:
                    pe.wait_ge(at_lo_done, (c + 1) * HP)
                if not (first and t < 2):
                    pe.wait_ge(y_added, c * CTT + (t - 1))
                tok = slice(t * P, (t + 1) * P)
                terms = [(a[:, j, tok], w[:, j, :]) for j in range(HP)
                         for a, w in ((at_hi, wo_hi), (at_hi, wo_lo), (at_lo, wo_hi))]
                for m, (a, w) in enumerate(terms):
                    last = nc.tensor.matmul(yp[t % 2][:, 0:DM], a, w, start=m == 0, stop=m == len(terms) - 1)
                last.then_inc(y_ready, 1)

            def chunk(c, first):
                for l in range(NL):
                    values(c, l, first)
                if first:
                    pe.wait_ge(w_lo_done, 5)
                for t in range(CTT):
                    output(c, t, first)

            pe.wait_ge(w_lo_done, 4)
            chunk(0, True)
            with pe.Fori(1, NC) as c:
                chunk(c, False)


def mix_and_feed(nc, channels, squares, bo, w1, b1_cols, w2, b2, resid, out):
    NC, CT = 4, TOK // 4
    CB, CTT = CT // NQ, CT // P
    KB = DM // P
    WIDTH = w1.shape[1]
    FB = WIDTH // P
    with ExitStack() as ctx:
        sb = lambda name, shape, dt=F32: ctx.enter_context(nc.sbuf_tensor("p4_" + name, shape, dt))
        pb = lambda name, shape: ctx.enter_context(nc.psum_tensor("p4_" + name, shape, F32))
        sem = lambda name: ctx.enter_context(nc.semaphore("p4_" + name))

        square = sb("square", [P, 4, KB, DM])
        sqT_hi, sqT_lo = sb("sqT_hi", [P, 4, KB, DM], F32R), sb("sqT_lo", [P, 4, KB, DM], F32R)
        w1_raw, w2_raw = sb("w1_raw", [P, KB, WIDTH]), sb("w2_raw", [P, FB, DM])
        w1_hi, w1_lo = sb("w1_hi", [P, KB, WIDTH], F32R), sb("w1_lo", [P, KB, WIDTH], F32R)
        w2_hi, w2_lo = sb("w2_hi", [P, FB, DM], F32R), sb("w2_lo", [P, FB, DM], F32R)
        channel = sb("channel", [P, 5, KB])
        td = sb("td", [P, 2, KB])
        tdm = sb("tdm", [P, KB, CB, NQ])
        b1_col = sb("b1_col", [P, FB])
        bo_row, b2_row = sb("bo_row", [P, DM]), sb("b2_row", [P, DM])
        ident = sb("ident", [P, P])
        stats, parts = sb("stats", [P, CTT, 6]), sb("parts", [P, 3, CTT])
        mean, std = sb("mean", [P, CTT]), sb("std", [P, 4, CTT])
        xn = sb("xn", [P, CTT, DM])
        mid = sb("mid", [P, CTT, DM])
        xnT = sb("xnT", [P, KB, CB, NQ + 1])
        diff = sb("diff", [P, KB, CB, NQ])
        mixed = xn[:, :, :].rearrange("p t (b q) -> p (t b) q", q=NQ).rearrange("p (k b) q -> p k b q", b=CB)
        mixed_hi = sb("mixed_hi", [P, 3, KB, CT], F32R)
        mixed_lo = sb("mixed_lo", [P, 3, KB, CT], F32R)
        ek, ekv = sb("ek", [P, CB, NQ]), sb("ekv", [P, CB, NQ])
        num, den = sb("num", [P, CT]), sb("den", [P, CT])
        eb, er, prod = sb("eb", [P, CT]), sb("er", [P, CT]), sb("prod", [P, CT])
        wkv = sb("wkv", [P, CT])
        wkv_hi, wkv_lo = sb("wkv_hi", [P, KB, CT], F32R), sb("wkv_lo", [P, KB, CT], F32R)
        zT_hi, zT_lo = sb("zT_hi", [P, KB, CT], F32R), sb("zT_lo", [P, KB, CT], F32R)
        hid = [sb(f"hid{i}", [P, CT]) for i in range(2)]
        hid_hi, hid_lo = sb("hid_hi", [P, FB, CT], F32R), sb("hid_lo", [P, FB, CT], F32R)
        staged = sb("staged", [P, CTT, DM])

        tp = pb("tp", [P, 512])
        rp = [pb(f"rp{i}", [P, CT]) for i in range(3)]
        fp = [pb(f"fp{i}", [P, CT]) for i in range(2)]
        yp = [pb(f"yp{i}", [P, 512]) for i in range(2)]

        sq_in, ch_in, w1_in, w2_in = sem("sq_in"), sem("ch_in"), sem("w1_in"), sem("w2_in")
        ident_done, zeroed, td_act, td_dve = sem("ident"), sem("zeroed"), sem("td_act"), sem("td_dve")
        sq_hi_done, sq_lo_done = sem("sq_hi"), sem("sq_lo")
        w1_hi_done, w1_lo_done, w2_hi_done, w2_lo_done = sem("w1_hi"), sem("w1_lo"), sem("w2_hi"), sem("w2_lo")
        ln_step, xn_done, biased, mid_done = sem("ln_step"), sem("xn_done"), sem("biased"), sem("mid_done")
        tp_ready, tp_act, tp_free = sem("tp_ready"), sem("tp_act"), sem("tp_free")
        mix_step, mix_done, mix_hi, mix_lo = sem("mix_step"), sem("mix_done"), sem("mix_hi"), sem("mix_lo")
        r_ready, exps_done, wkv_step = sem("r_ready"), sem("exps_done"), sem("wkv_step")
        wkv_hi_done, wkv_lo_done = sem("wkv_hi_done"), sem("wkv_lo_done")
        g_ready, g_added = sem("g_ready"), sem("g_added")
        f_ready, hid_done, hid_hi_done, hid_lo_done = sem("f_ready"), sem("hid_done"), sem("hid_hi_done"), sem("hid_lo_done")
        y_ready, y_added, stored = sem("y_ready"), sem("y_added"), sem("stored")
        block = ctx.enter_context(nc.Block())

        LN = CTT + 7 + 1 + 5
        MIX = 1 + 3
        WS = 9
        TPC = 2 * KB

        def tile_of(c, t):
            return resid[:, bass.ds(c * CTT + t, 1), :].rearrange("p a d -> p (a d)")

        def pipeline(eng, front, ahead, interleaved):
            front(0, True)
            interleaved(0, True)
            with eng.Fori(1, NC - 1) as c:
                interleaved(c, False)
            ahead(NC - 1)

        @block.sync
        def _(sp):
            sp.dma_start(channel[:, :, :], channels).then_inc(ch_in, 16)
            sp.dma_start(b1_col[:, :], b1_cols).then_inc(ch_in, 16)
            for m in range(4):
                sp.dma_start(square[:, m, :, :], squares[m, :, :].rearrange("(k p) n -> p k n", p=P)).then_inc(sq_in, 16)
            for dst, v in ((bo_row, bo), (b2_row, b2)):
                sp.dma_start(dst[:, :], v.rearrange("(a n) -> a n", a=1).partition_broadcast(P)).then_inc(ch_in, 16)
            sp.dma_start(w1_raw[:, :, :], w1.rearrange("(k p) n -> p k n", p=P)).then_inc(w1_in, 16)
            sp.dma_start(w2_raw[:, :, :], w2.rearrange("(k p) n -> p k n", p=P)).then_inc(w2_in, 16)
            out_v = out.rearrange("(c u b) q d -> (b q) (c u) d", b=P // NQ, u=CTT)
            with sp.Fori(0, NC) as c:
                sp.wait_ge(y_added, (c + 1) * CTT)
                sp.dma_start(out_v[:, bass.ds(c * CTT, CTT), :], staged[:, :, :]).then_inc(stored, 16)
            sp.wait_ge(stored, NC * 16)

        @block.gpsimd
        def _(pool):
            identity(nc, pool, ident, ident_done)
            nc.gpsimd.memset(xnT[:, :, :, 0:1], 0.0).then_inc(zeroed, 1)
            nc.gpsimd.memset(ek[:, :, 0:1], 0.0).then_inc(zeroed, 1)
            nc.gpsimd.memset(ekv[:, :, 0:1], 0.0).then_inc(zeroed, 1)
            nc.gpsimd.memset(tdm[:, :, :, :], 1.0).then_inc(zeroed, 1)
            pool.wait_ge(zeroed, 4)
            nc.gpsimd.memset(tdm[:, :, :, 0:1], 0.0).then_inc(zeroed, 1)
            pool.wait_ge(ch_in, 4 * 16)
            with pool.Fori(0, NC) as c:
                for t in range(CTT):
                    pool.wait_ge(xn_done, c * 2 * CTT + (CTT + t + 1))
                    nc.gpsimd.tensor_tensor(mid[:, t, :], mid[:, t, :], b2_row[:, :], ALU.add).then_inc(biased, 1)

        @block.scalar
        def _(act):
            act.wait_ge(ch_in, 4 * 16)
            nc.scalar.activation(td[:, 0, :], channel[:, 0, :], ACT.Exp).then_inc(td_act, 1)
            act.wait_ge(td_act, 1)
            nc.scalar.activation(td[:, 1, :], td[:, 0, :], ACT.Exp, scale=-1.0).then_inc(td_act, 1)
            act.wait_ge(sq_in, 64)
            nc.scalar.activation(sqT_hi[:, :, :, :], square[:, :, :, :], ACT.Copy).then_inc(sq_hi_done, 1)
            act.wait_ge(w1_in, 16)
            nc.scalar.activation(w1_hi[:, :, :], w1_raw[:, :, :], ACT.Copy).then_inc(w1_hi_done, 1)
            act.wait_ge(w2_in, 16)
            nc.scalar.activation(w2_hi[:, :, :], w2_raw[:, :, :], ACT.Copy).then_inc(w2_hi_done, 1)

            def root(c, m):
                base = c * (2 * LN) + m * LN
                act.wait_ge(ln_step, base + (CTT + 7))
                nc.scalar.activation(std[:, 1, :], std[:, 0, :], ACT.Sqrt).then_inc(ln_step, 1)

            def normed(c, m, first):
                for k in range(KB):
                    act.wait_ge(tp_ready, c * TPC + (m * KB + k + 1))
                    if m == 0:
                        if first and k == 0:
                            act.wait_ge(zeroed, 5)
                        if not first and k == 0:
                            act.wait_ge(mix_step, c * (KB * MIX))
                        nc.scalar.activation(xnT[:, k, :, 1:NQ + 1], tp[:, :].rearrange("p (b q) -> p b q", q=NQ),
                                             ACT.Copy).then_inc(tp_act, 1)
                    else:
                        if not first and k == 0:
                            act.wait_ge(f_ready, c * FB)
                        nc.scalar.activation(zT_hi[:, k, :], tp[:, :], ACT.Copy).then_inc(tp_act, 1)

            def mix_round(c, first):
                for k in range(KB):
                    for m in range(3):
                        act.wait_ge(mix_done, c * (3 * KB) + (3 * k + m + 1))
                        if not first and k == 0 and m == 0:
                            act.wait_ge(r_ready, c * (3 * KB))
                        nc.scalar.activation(mixed_hi[:, m, k, :], mixed[:, k, :, :].rearrange("p b q -> p (b q)"),
                                             ACT.Copy).then_inc(mix_hi, 1)

            def exps(c, o, first):
                act.wait_ge(r_ready, c * (3 * KB) + 3 * (o + 1))
                if not (first and o == 0):
                    act.wait_ge(wkv_step, c * (KB * WS) + o * WS)
                kp = rp[0][:, :].rearrange("p (b q) -> p b q", q=NQ)
                nc.scalar.activation(ek[:, :, 1:NQ], kp[:, :, 0:NQ - 1], ACT.Exp)
                nc.scalar.activation(eb[:, :], rp[0][:, :], ACT.Exp, bias=channel[:, 1, o:o + 1])
                nc.scalar.activation(er[:, :], rp[2][:, :], ACT.Exp, scale=-1.0).then_inc(exps_done, 1)

            def wkv_round(c, o, first):
                act.wait_ge(wkv_step, c * (KB * WS) + (o + 1) * WS)
                if not first and o == 0:
                    act.wait_ge(g_ready, c * CTT)
                nc.scalar.activation(wkv_hi[:, o, :], wkv[:, :], ACT.Copy).then_inc(wkv_hi_done, 1)

            def relus(c, blocks, first):
                for f in blocks:
                    act.wait_ge(f_ready, c * FB + (f + 1))
                    if not (first and f < 2):
                        act.wait_ge(hid_lo_done, c * FB + (f - 1))
                    nc.scalar.activation(hid[f % 2][:, :], fp[f % 2][:, :], ACT.Relu, bias=b1_col[:, f:f + 1]).then_inc(hid_done, 1)

            def front(c, first):
                root(c, 0)
                normed(c, 0, first)
                mix_round(c, first)
                for o in range(KB):
                    exps(c, o, first)
                    wkv_round(c, o, first)
                root(c, 1)
                normed(c, 1, first)

            def interleaved(c, first):
                root(c + 1, 0)
                normed(c + 1, 0, False)
                relus(c, range(0, 2), first)
                mix_round(c + 1, False)
                relus(c, range(2, 4), first)
                exps(c + 1, 0, False)
                relus(c, range(4, 6), first)
                wkv_round(c + 1, 0, False)
                exps(c + 1, 1, False)
                relus(c, range(6, 8), first)
                wkv_round(c + 1, 1, False)
                root(c + 1, 1)
                normed(c + 1, 1, False)

            pipeline(act, front, lambda c: relus(c, range(FB), False), interleaved)

        @block.vector
        def _(dve):
            dve.wait_ge(td_act, 2)
            dve.wait_ge(zeroed, 5)
            for k in range(KB):
                nc.vector.tensor_scalar(tdm[:, k, :, :], tdm[:, k, :, :], td[:, 1, k:k + 1], None, ALU.mult).then_inc(td_dve, 1)
            def split_weights():
                dve.wait_ge(sq_hi_done, 1)
                nc.vector.tensor_tensor(sqT_lo[:, :, :, :], square[:, :, :, :], bits(sqT_hi[:, :, :, :]),
                                        ALU.subtract).then_inc(sq_lo_done, 1)
                dve.wait_ge(w1_hi_done, 1)
                nc.vector.tensor_tensor(w1_lo[:, :, :], w1_raw[:, :, :], bits(w1_hi[:, :, :]), ALU.subtract).then_inc(w1_lo_done, 1)
                dve.wait_ge(w2_hi_done, 1)
                nc.vector.tensor_tensor(w2_lo[:, :, :], w2_raw[:, :, :], bits(w2_hi[:, :, :]), ALU.subtract).then_inc(w2_lo_done, 1)

            def source(c, m, t):
                return tile_of(c, t) if m == 0 else mid[:, t, :]

            def norm(c, m, first):
                base = c * (2 * LN) + m * LN
                for t in range(CTT):
                    if m == 1:
                        dve.wait_ge(g_added, c * CTT + (t + 1))
                    nc.vector.bn_stats(stats[:, t, :], source(c, m, t)).then_inc(ln_step, 1)
                even_mean, even_sq, odd_mean, odd_sq = (stats[:, :, n] for n in (1, 2, 4, 5))
                dve.wait_ge(ln_step, base + CTT)
                nc.vector.tensor_tensor(parts[:, 0, :], even_mean, odd_mean, ALU.add).then_inc(ln_step, 1)
                nc.vector.tensor_tensor(parts[:, 1, :], even_mean, odd_mean, ALU.subtract).then_inc(ln_step, 1)
                nc.vector.tensor_tensor(parts[:, 2, :], even_sq, odd_sq, ALU.add).then_inc(ln_step, 1)
                dve.wait_ge(ln_step, base + (CTT + 3))
                nc.vector.tensor_scalar(mean[:, :], parts[:, 0, :], 0.5, None, ALU.mult).then_inc(ln_step, 1)
                nc.vector.scalar_tensor_tensor(parts[:, 1, :], parts[:, 1, :], 0.25, parts[:, 1, :], ALU.mult, ALU.mult).then_inc(ln_step, 1)
                nc.vector.tensor_scalar(parts[:, 2, :], parts[:, 2, :], 1.0 / DM, EPS, ALU.mult, ALU.add).then_inc(ln_step, 1)
                dve.wait_ge(ln_step, base + (CTT + 6))
                nc.vector.tensor_tensor(std[:, 0, :], parts[:, 1, :], parts[:, 2, :], ALU.add).then_inc(ln_step, 1)
                dve.wait_ge(ln_step, base + (CTT + 8))
                nc.vector.reciprocal(std[:, 2, :], std[:, 1, :]).then_inc(ln_step, 1)
                dve.wait_ge(ln_step, base + (CTT + 9))
                nc.vector.tensor_tensor(std[:, 2, :], std[:, 2, :], std[:, 0, :], ALU.mult).then_inc(ln_step, 1)
                dve.wait_ge(ln_step, base + (CTT + 10))
                nc.vector.tensor_tensor(std[:, 1, :], std[:, 1, :], std[:, 2, :], ALU.add).then_inc(ln_step, 1)
                dve.wait_ge(ln_step, base + (CTT + 11))
                nc.vector.reciprocal(std[:, 2, :], std[:, 1, :]).then_inc(ln_step, 1)
                dve.wait_ge(ln_step, base + (CTT + 12))
                nc.vector.tensor_scalar(std[:, 3, :], std[:, 2, :], 2.0, None, ALU.mult).then_inc(ln_step, 1)
                dve.wait_ge(ln_step, base + LN)
                if not (first and m == 0):
                    dve.wait_ge(tp_ready, c * TPC + m * KB)
                for t in range(CTT):
                    nc.vector.tensor_scalar(xn[:, t, :], source(c, m, t), mean[:, t:t + 1], std[:, 3, t:t + 1],
                                            ALU.subtract, ALU.mult).then_inc(xn_done, 1)

            def feed_lo(c, first):
                for k in range(KB):
                    dve.wait_ge(tp_act, c * TPC + (KB + k + 1))
                    nc.vector.tensor_tensor(zT_lo[:, k, :], tp[:, :], bits(zT_hi[:, k, :]), ALU.subtract).then_inc(tp_free, 1)

            def mix(c, first):
                for k in range(KB):
                    now, before = xnT[:, k, :, 1:NQ + 1], xnT[:, k, :, 0:NQ]
                    if k == 0:
                        dve.wait_ge(tp_act, c * TPC + KB)
                    nc.vector.tensor_tensor(diff[:, k, :, :], now, before, ALU.subtract).then_inc(mix_step, 1)
                    dve.wait_ge(mix_step, c * (KB * MIX) + (k * MIX + 1))
                    for m in range(3):
                        nc.vector.scalar_tensor_tensor(mixed[:, k, :, :], diff[:, k, :, :], channel[:, 2 + m, k:k + 1],
                                                       before, ALU.mult, ALU.add).then_inc(mix_done, 1)
                        dve.wait_ge(mix_hi, c * (3 * KB) + (3 * k + m + 1))
                        nc.vector.tensor_tensor(mixed_lo[:, m, k, :], mixed[:, k, :, :].rearrange("p b q -> p (b q)"),
                                                bits(mixed_hi[:, m, k, :]), ALU.subtract).then_inc(mix_step, 1)
                        dve.wait_ge(mix_step, c * (KB * MIX) + (k * MIX + m + 2))

            def recur(c, o, first):
                base = c * (KB * WS) + o * WS
                vp = rp[1][:, :].rearrange("p (b q) -> p b q", q=NQ)
                flat = lambda ap: ap.rearrange("p b q -> p (b q)")
                decays = flat(tdm[:, o, :, :])
                dve.wait_ge(exps_done, c * KB + (o + 1))
                if first and o == 0:
                    dve.wait_ge(td_dve, KB)
                nc.vector.tensor_tensor(ekv[:, :, 1:NQ], vp[:, :, 0:NQ - 1], ek[:, :, 1:NQ], ALU.mult).then_inc(wkv_step, 1)
                nc.vector.tensor_tensor(prod[:, :], rp[1][:, :], eb[:, :], ALU.mult).then_inc(wkv_step, 1)
                nc.vector.tensor_tensor_scan(den[:, :], decays, flat(ek[:, :, :]), 0.0, ALU.mult, ALU.add).then_inc(wkv_step, 1)
                dve.wait_ge(wkv_step, base + 1)
                nc.vector.tensor_tensor_scan(num[:, :], decays, flat(ekv[:, :, :]), 0.0, ALU.mult, ALU.add).then_inc(wkv_step, 1)
                dve.wait_ge(wkv_step, base + 3)
                nc.vector.tensor_tensor(den[:, :], den[:, :], eb[:, :], ALU.add).then_inc(wkv_step, 1)
                dve.wait_ge(wkv_step, base + 4)
                nc.vector.tensor_tensor(num[:, :], num[:, :], prod[:, :], ALU.add).then_inc(wkv_step, 1)
                dve.wait_ge(wkv_step, base + 5)
                nc.vector.scalar_tensor_tensor(er[:, :], er[:, :], 1.0, den[:, :], ALU.add, ALU.mult).then_inc(wkv_step, 1)
                dve.wait_ge(wkv_step, base + 7)
                nc.vector.reciprocal(er[:, :], er[:, :]).then_inc(wkv_step, 1)
                dve.wait_ge(wkv_step, base + 8)
                if not (first and o == 0):
                    dve.wait_ge(wkv_lo_done, c * KB + o)
                nc.vector.tensor_tensor(wkv[:, :], num[:, :], er[:, :], ALU.mult).then_inc(wkv_step, 1)

            def wkv_sub(c, o):
                dve.wait_ge(wkv_hi_done, c * KB + (o + 1))
                nc.vector.tensor_tensor(wkv_lo[:, o, :], wkv[:, :], bits(wkv_hi[:, o, :]), ALU.subtract).then_inc(wkv_lo_done, 1)

            def mixed_add(c, first):
                for t in range(CTT):
                    if t == 0 and not first:
                        dve.wait_ge(y_added, c * CTT)
                    nc.vector.tensor_tensor(mid[:, t, :], tile_of(c, t), bo_row[:, :], ALU.add).then_inc(mid_done, 1)
                for t in range(CTT):
                    dve.wait_ge(mid_done, c * CTT + (t + 1))
                    dve.wait_ge(g_ready, c * CTT + (t + 1))
                    nc.vector.tensor_tensor(mid[:, t, :], yp[t % 2][:, 0:DM], mid[:, t, :], ALU.add).then_inc(g_added, 1)

            def hidden(c, blocks, first):
                for f in blocks:
                    dve.wait_ge(hid_done, c * FB + (f + 1))
                    if not first and f == 0:
                        dve.wait_ge(y_ready, c * CTT)
                    nc.vector.tensor_copy(hid_hi[:, f, :], hid[f % 2][:, :]).then_inc(hid_hi_done, 1)
                    dve.wait_ge(hid_hi_done, c * FB + (f + 1))
                    nc.vector.tensor_tensor(hid_lo[:, f, :], hid[f % 2][:, :], bits(hid_hi[:, f, :]), ALU.subtract).then_inc(hid_lo_done, 1)

            def finish(c, first):
                for t in range(CTT):
                    dve.wait_ge(y_ready, c * CTT + (t + 1))
                    dve.wait_ge(biased, c * CTT + (t + 1))
                    if not first and t == 0:
                        dve.wait_ge(stored, c * 16)
                    nc.vector.tensor_tensor(staged[:, t, :], yp[t % 2][:, 0:DM], mid[:, t, :], ALU.add).then_inc(y_added, 1)

            def front(c, first):
                norm(c, 0, first)
                mix(c, first)
                split_weights()
                for o in range(KB):
                    recur(c, o, first)
                    wkv_sub(c, o)
                mixed_add(c, first)
                norm(c, 1, first)
                feed_lo(c, first)

            def interleaved(c, first):
                norm(c + 1, 0, False)
                hidden(c, range(0, 2), first)
                mix(c + 1, False)
                hidden(c, range(2, 4), first)
                recur(c + 1, 0, False)
                hidden(c, range(4, 6), first)
                wkv_sub(c + 1, 0)
                recur(c + 1, 1, False)
                hidden(c, range(6, 8), first)
                wkv_sub(c + 1, 1)
                finish(c, first)
                mixed_add(c + 1, False)
                norm(c + 1, 1, False)
                feed_lo(c + 1, False)

            def last_back(c):
                hidden(c, range(FB), False)
                finish(c, False)

            pipeline(dve, front, last_back, interleaved)

        @block.tensor
        def _(pe):
            pe.wait_ge(ident_done, 2)

            def transposes(c, m, first):
                pe.wait_ge(xn_done, c * (2 * CTT) + (m + 1) * CTT)
                for k in range(KB):
                    if not (first and (m, k) == (0, 0)):
                        pe.wait_ge(tp_act, c * TPC + (m * KB + k))
                    if (m, k) == (0, 0) and not first:
                        pe.wait_ge(tp_free, c * KB)
                    if (m, k) == (1, 1):
                        pe.wait_ge(tp_free, c * KB + 1)
                    for t in range(CTT):
                        last = nc.tensor.transpose(tp[:, t * P:(t + 1) * P], xn[:, t, k * P:(k + 1) * P], ident[:, :])
                    last.then_inc(tp_ready, 1)

            def split_terms(w_hi, w_lo, a_hi, a_lo):
                return ((w_hi, a_hi), (w_lo, a_hi), (w_hi, a_lo))

            def mixing(c, o, first):
                pe.wait_ge(mix_step, (c + 1) * (KB * MIX))
                if first and o == 0:
                    pe.wait_ge(sq_lo_done, 1)
                if not (first and o == 0):
                    pe.wait_ge(wkv_step, c * (KB * WS) + o * WS)
                cols = slice(o * P, (o + 1) * P)
                for m in range(3):
                    terms = [t for k in range(KB) for t in split_terms(sqT_hi[:, m, k, cols], sqT_lo[:, m, k, cols],
                                                                      mixed_hi[:, m, k, :], mixed_lo[:, m, k, :])]
                    for n, (w, a) in enumerate(terms):
                        last = nc.tensor.matmul(rp[m][:, :], w, a, start=n == 0, stop=n == len(terms) - 1)
                    last.then_inc(r_ready, 1)

            def mixed_out(c, first):
                pe.wait_ge(wkv_lo_done, (c + 1) * KB)
                for t in range(CTT):
                    if t >= 2:
                        pe.wait_ge(g_added, c * CTT + (t - 1))
                    elif not first:
                        pe.wait_ge(y_added, c * CTT)
                    tok = slice(t * P, (t + 1) * P)
                    terms = [x for k in range(KB) for x in ((wkv_hi[:, k, tok], sqT_hi[:, 3, k, :]),
                                                            (wkv_hi[:, k, tok], sqT_lo[:, 3, k, :]),
                                                            (wkv_lo[:, k, tok], sqT_hi[:, 3, k, :]))]
                    for n, (a, w) in enumerate(terms):
                        last = nc.tensor.matmul(yp[t % 2][:, 0:DM], a, w, start=n == 0, stop=n == len(terms) - 1)
                    last.then_inc(g_ready, 1)

            def feed_in(c, blocks, first):
                for f in blocks:
                    if f == 0:
                        pe.wait_ge(tp_free, (c + 1) * KB)
                        if first:
                            pe.wait_ge(w1_lo_done, 1)
                    if not (first and f < 2):
                        pe.wait_ge(hid_done, c * FB + (f - 1))
                    cols = slice(f * P, (f + 1) * P)
                    terms = [t for k in range(KB) for t in split_terms(w1_hi[:, k, cols], w1_lo[:, k, cols],
                                                                      zT_hi[:, k, :], zT_lo[:, k, :])]
                    for n, (w, a) in enumerate(terms):
                        last = nc.tensor.matmul(fp[f % 2][:, :], w, a, start=n == 0, stop=n == len(terms) - 1)
                    last.then_inc(f_ready, 1)

            def feed_out(c, first):
                pe.wait_ge(hid_lo_done, (c + 1) * FB)
                if first:
                    pe.wait_ge(w2_lo_done, 1)
                for t in range(CTT):
                    if t >= 2:
                        pe.wait_ge(y_added, c * CTT + (t - 1))
                    else:
                        pe.wait_ge(g_added, (c + 1) * CTT)
                    tok = slice(t * P, (t + 1) * P)
                    terms = [x for f in range(FB) for x in ((hid_hi[:, f, tok], w2_hi[:, f, :]),
                                                            (hid_hi[:, f, tok], w2_lo[:, f, :]),
                                                            (hid_lo[:, f, tok], w2_hi[:, f, :]))]
                    for n, (a, w) in enumerate(terms):
                        last = nc.tensor.matmul(yp[t % 2][:, 0:DM], a, w, start=n == 0, stop=n == len(terms) - 1)
                    last.then_inc(y_ready, 1)

            def front(c, first):
                transposes(c, 0, first)
                for o in range(KB):
                    mixing(c, o, first)
                mixed_out(c, first)
                transposes(c, 1, first)

            def interleaved(c, first):
                feed_in(c, range(0, 2), first)
                transposes(c + 1, 0, False)
                feed_in(c, range(2, 4), first)
                mixing(c + 1, 0, False)
                feed_in(c, range(4, 6), first)
                mixing(c + 1, 1, False)
                feed_in(c, range(6, 8), first)
                feed_out(c, first)
                mixed_out(c + 1, False)
                transposes(c + 1, 1, False)

            def last_back(c):
                feed_in(c, range(FB), False)
                feed_out(c, False)

            pipeline(pe, front, last_back, interleaved)


def kernel(x, ctx_768, L0_xattn_w_q, L0_xattn_w_kv, L0_xattn_w_out, L0_xattn_b_out, L0_attn_time_decay,
           L0_attn_time_first, L0_attn_time_mix_key, L0_attn_time_mix_value, L0_attn_time_mix_receptance,
           L0_attn_Wk, L0_attn_Wv, L0_attn_Wr, L0_attn_Wo, L0_attn_bo, L0_ffn_w1, L0_ffn_b1, L0_ffn_w2, L0_ffn_b2):
    import concourse.bacc as bacc
    from concourse.bass_utils import run_bass_kernel_spmd

    nc = bacc.Bacc("TRN2", target_bir_lowering=False, num_devices=1)
    columns = lambda vectors: np.stack([np.asarray(v).reshape(-1, P) for v in vectors]).transpose(2, 0, 1)
    data = {
        "x": x, "ctx": ctx_768, "ctxT": np.asarray(ctx_768).transpose(0, 2, 1), "w_q": L0_xattn_w_q, "w_kv": L0_xattn_w_kv, "w_out": L0_xattn_w_out, "b_out": L0_xattn_b_out,
        "channels": columns([L0_attn_time_decay, L0_attn_time_first, L0_attn_time_mix_key, L0_attn_time_mix_value,
                             L0_attn_time_mix_receptance]),
        "squares": np.stack([np.asarray(w).T for w in (L0_attn_Wk, L0_attn_Wv, L0_attn_Wr, L0_attn_Wo)]),
        "bo": L0_attn_bo, "w1": L0_ffn_w1, "b1": np.asarray(L0_ffn_b1).reshape(-1, P).T, "w2": L0_ffn_w2, "b2": L0_ffn_b2,
    }
    data = {name: np.ascontiguousarray(a) for name, a in data.items()}
    t = {name: nc.dram_tensor(f"in_{name}", a.shape, F32, kind="ExternalInput").ap() for name, a in data.items()}
    out = nc.dram_tensor("out_x", (NB, NQ, DM), F32, kind="ExternalOutput").ap()
    qk_dram = nc.dram_tensor("qk_scratch", (NB, DC, HQ), F32).ap()
    o_dram = nc.dram_tensor("o_scratch", (NB, DC, HQ), F32).ap()
    perceiver_layer(nc, t, qk_dram, o_dram, out)
    result = run_bass_kernel_spmd(nc, [{f"in_{name}": a for name, a in data.items()}], core_ids=[0])
    return result.results[0]["out_x"]


def perceiver_layer(nc, t, qk_dram, o_dram, out):
    project_queries(nc, t["x"], t["w_q"], t["w_kv"], qk_dram)
    attend(nc, t["ctx"], t["ctxT"], qk_dram, o_dram)
    with nc.sbuf_tensor("resid", [P, TT, DM], F32) as resid:
        attention_output(nc, t["w_kv"], t["w_out"], t["b_out"], t["x"], o_dram, resid)
        mix_and_feed(nc, t["channels"], t["squares"], t["bo"], t["w1"], t["b1"], t["w2"], t["b2"], resid, out)
```

```python
import numpy as np
import concourse.bass as bass
from concourse import mybir
from contextlib import ExitStack

F32 = mybir.dt.float32
F32R = mybir.dt.float32r
ALU = mybir.AluOpType
ACT = mybir.ActivationFunctionType
AX = mybir.AxisListType

P = 128
NB, NQ, DM = 32, 64, 256
NKV, DC = 1601, 192
NH, DH = 16, 64
INNER = NH * DH
HQ = NH * NQ
TOK = NB * NQ
TT = TOK // P
DCB = DC - P
SCALE = DH ** -0.5
EPS = 1e-5


def bits(ap):
    return ap.bitcast(F32)


def identity(nc, pool, ident, ident_done):
    nc.gpsimd.memset(ident[:, :], 0.0).then_inc(ident_done, 1)
    pool.wait_ge(ident_done, 1)
    nc.gpsimd.affine_select(out=ident[:, :], in_=ident[:, :], compare_op=ALU.not_equal, fill=1.0,
                            base=0, pattern=[[-1, P]], channel_multiplier=1).then_inc(ident_done, 1)


def project_queries(nc, x, w_q, w_kv, qk_dram):
    KB = DM // P
    NC, CT = 4, TOK // 4
    CB = CT // NQ
    HP = NH // 2
    HALF = HP // 2
    with ExitStack() as ctx:
        sb = lambda name, shape, dt=F32: ctx.enter_context(nc.sbuf_tensor("p1_" + name, shape, dt))
        pb = lambda name, shape: ctx.enter_context(nc.psum_tensor("p1_" + name, shape, F32))
        sem = lambda name: ctx.enter_context(nc.semaphore("p1_" + name))

        xt = sb("x", [P, TT, DM])
        stats = sb("stats", [P, TT, 6])
        mv = sb("mv", [P, TT, 2])
        std = sb("std", [P, 4, TT])
        wq = sb("wq", [P, KB, INNER])
        wq_hi, wq_lo = sb("wq_hi", [P, KB, INNER], F32R), sb("wq_lo", [P, KB, INNER], F32R)
        wk_a, wk_b = sb("wk_a", [P, INNER]), sb("wk_b", [DCB, INNER])
        wk2 = sb("wk2", [P, INNER // DH, 2, DH])
        wk2_b = sb("wk2_b", [DCB, INNER // DH, 2, DH])
        wks_hi, wks_lo = sb("wks_hi", [P, NH, DC], F32R), sb("wks_lo", [P, NH, DC], F32R)
        xT_hi, xT_lo = sb("xT_hi", [P, KB, TOK], F32R), sb("xT_lo", [P, KB, TOK], F32R)
        stack = sb("stack", [P, 2, 2, CT], F32R)
        out_a, out_b = sb("out_a", [P, CB, HALF * 2, NQ]), sb("out_b", [DCB, CB, HALF * 2, NQ])
        out_a2, out_b2 = sb("out_a2", [P, CB, HALF * 2, NQ]), sb("out_b2", [DCB, CB, HALF * 2, NQ])
        staged = ((out_a, out_b), (out_a2, out_b2))
        ident = sb("ident", [P, P])

        tp = [pb(f"tp{i}", [P, 512]) for i in range(2)]
        qp = [pb(f"qp{i}", [P, 512]) for i in range(2)]
        ap = [pb(f"ap{i}", [P, 512]) for i in range(2)]
        bp = [pb(f"bp{i}", [DCB, 512]) for i in range(2)]

        x_in, wq_in, wk_in = sem("x_in"), sem("wq_in"), sem("wk_in")
        ident_done, wq_hi_done, wq_lo_done, wk2_done = sem("ident"), sem("wqh"), sem("wql"), sem("wk2")
        stat_done, std_done, xn_done = sem("stat"), sem("std"), sem("xn")
        tp_ready, tp_hi, tp_lo = sem("tp_ready"), sem("tp_hi"), sem("tp_lo")
        q_ready, stack_hi, stack_lo = sem("q_ready"), sem("stack_hi"), sem("stack_lo")
        qk_ready, evac_act, evac_dve = sem("qk_ready"), sem("evac_act"), sem("evac_dve")
        stored = [sem("stored0"), sem("stored1")]
        block = ctx.enter_context(nc.Block())

        NT = NC * KB + NH // 2

        @block.sync
        def _(sp):
            sp.dma_start(xt[:, :, :], x.rearrange("(t b) q d -> (b q) t d", b=P // NQ)).then_inc(x_in, 16)
            sp.dma_start(wk_a[:, :], w_kv[0:P, 0:INNER]).then_inc(wk_in, 16)
            sp.dma_start(wk_b[:, :], w_kv[P:DC, 0:INNER]).then_inc(wk_in, 16)
            sp.dma_start(wq[:, :, :], w_q.rearrange("(k p) n -> p k n", p=P)).then_inc(wq_in, 16)
            with sp.Fori(0, NC) as c:
                for half in range(2):
                    sp.wait_ge(evac_act, c * (2 * HP) + (half + 1) * HP)
                    sp.wait_ge(evac_dve, c * (2 * HP) + (half + 1) * HP)
                    cols = slice(half * HALF * 2 * NQ, (half + 1) * HALF * 2 * NQ)
                    for buf, rows in zip(staged[half], (slice(0, P), slice(P, DC))):
                        dst = qk_dram[bass.ds(c * CB, CB), rows, cols].rearrange("b c n -> c b n")
                        sp.dma_start(dst, buf[:, :, :, :].rearrange("p b h q -> p b (h q)")).then_inc(stored[half], 16)
            sp.wait_ge(stored[0], 32 * NC)
            sp.wait_ge(stored[1], 32 * NC)

        @block.gpsimd
        def _(pool):
            identity(nc, pool, ident, ident_done)
            pool.wait_ge(wk_in, 32)
            for r in range(2):
                nc.gpsimd.tensor_copy(wk2[:, :, r, :], wk_a[:, :].rearrange("p (h d) -> p h d", d=DH)).then_inc(wk2_done, 1)
                nc.gpsimd.tensor_copy(wk2_b[:, :, r, :], wk_b[:, :].rearrange("p (h d) -> p h d", d=DH)).then_inc(wk2_done, 1)

        def evacuate(eng, scalar, c, j, first):
            half, jj = divmod(j, HALF)
            buf_a, buf_b = staged[half]
            for r in range(2):
                eng.wait_ge(qk_ready, c * NH + (2 * j + r + 1))
                if not first and jj == 0 and r == 0:
                    eng.wait_ge(stored[half], c * 32)
                first = (r == 0) == scalar
                dst = (buf_a if first else buf_b)[:, :, 2 * jj + r, :]
                src = (ap if first else bp)[r][:, :].rearrange("p (b q) -> p b q", q=NQ)
                if scalar:
                    nc.scalar.activation(dst, src, ACT.Copy).then_inc(evac_act, 1)
                else:
                    nc.vector.tensor_copy(dst, src).then_inc(evac_dve, 1)

        @block.scalar
        def _(act):
            act.wait_ge(stat_done, TT + TT + 1)
            nc.scalar.activation(std[:, 1, :], std[:, 0, :], ACT.Sqrt).then_inc(std_done, 1)
            act.wait_ge(wq_in, 16)
            nc.scalar.activation(wq_hi[:, :, :], wq[:, :, :], ACT.Copy).then_inc(wq_hi_done, 1)
            for n in range(NT):
                act.wait_ge(tp_ready, n + 1)
                if n < NC * KB:
                    c, k = divmod(n, KB)
                    nc.scalar.activation(xT_hi[:, k, c * CT:(c + 1) * CT], tp[n % 2][:, :], ACT.Copy).then_inc(tp_hi, 1)
                else:
                    h = 2 * (n - NC * KB)
                    nc.scalar.activation(wks_hi[:, h:h + 2, :], tp[n % 2][:, 0:2 * DC].rearrange("p (h c) -> p h c", c=DC),
                                         ACT.Copy).then_inc(tp_hi, 1)

            def chunk(c, first=False):
                for j in range(HP):
                    act.wait_ge(q_ready, c * HP + (j + 1))
                    if not first or j >= 2:
                        act.wait_ge(qk_ready, c * NH + 2 * (j - 1))
                    s = stack[:, j % 2]
                    nc.scalar.activation(s[0:DH, 0, :], qp[j % 2][0:DH, :], ACT.Copy, scale=SCALE)
                    nc.scalar.activation(s[DH:P, 1, :], qp[j % 2][DH:P, :], ACT.Copy, scale=SCALE).then_inc(stack_hi, 1)
                    if j >= 1:
                        evacuate(act, True, c, j - 1, first)
                evacuate(act, True, c, HP - 1, first)

            chunk(0, first=True)
            with act.Fori(1, NC) as c:
                chunk(c)

        @block.vector
        def _(dve):
            dve.wait_ge(x_in, 16)
            for t in range(TT):
                nc.vector.bn_stats(stats[:, t, :], xt[:, t, :]).then_inc(stat_done, 1)
            for t in range(TT):
                dve.wait_ge(stat_done, t + 1)
                nc.vector.bn_aggr(mv[:, t, :], stats[:, t, :]).then_inc(stat_done, 1)
            dve.wait_ge(stat_done, 2 * TT)
            nc.vector.tensor_scalar(std[:, 0, :], mv[:, :, 1], EPS, None, ALU.add).then_inc(stat_done, 1)
            dve.wait_ge(std_done, 1)
            newton_rstd(nc, dve, std, std_done)
            for t in range(TT):
                nc.vector.tensor_scalar(xt[:, t, :], xt[:, t, :], mv[:, t, 0:1], std[:, 3, t:t + 1],
                                        ALU.subtract, ALU.mult).then_inc(xn_done, 1)
            for n in range(NT):
                dve.wait_ge(tp_hi, n + 1)
                if n < NC * KB:
                    c, k = divmod(n, KB)
                    cols = slice(c * CT, (c + 1) * CT)
                    nc.vector.tensor_tensor(xT_lo[:, k, cols], tp[n % 2][:, :], bits(xT_hi[:, k, cols]),
                                            ALU.subtract).then_inc(tp_lo, 1)
                else:
                    h = 2 * (n - NC * KB)
                    nc.vector.tensor_tensor(wks_lo[:, h:h + 2, :], tp[n % 2][:, 0:2 * DC].rearrange("p (h c) -> p h c", c=DC),
                                            bits(wks_hi[:, h:h + 2, :]), ALU.subtract).then_inc(tp_lo, 1)
            dve.wait_ge(wq_hi_done, 1)
            nc.vector.tensor_tensor(wq_lo[:, :, :], wq[:, :, :], bits(wq_hi[:, :, :]), ALU.subtract).then_inc(wq_lo_done, 1)

            def chunk(c, first=False):
                for j in range(HP):
                    dve.wait_ge(stack_hi, c * HP + (j + 1))
                    s, q = stack[:, j % 2], qp[j % 2]
                    nc.vector.scalar_tensor_tensor(s[DH:P, 0, :], q[0:DH, :], SCALE, bits(s[0:DH, 0, :]), ALU.mult, ALU.subtract)
                    nc.vector.scalar_tensor_tensor(s[0:DH, 1, :], q[DH:P, :], SCALE, bits(s[DH:P, 1, :]), ALU.mult,
                                                   ALU.subtract).then_inc(stack_lo, 1)
                    if j >= 1:
                        evacuate(dve, False, c, j - 1, first)
                evacuate(dve, False, c, HP - 1, first)

            chunk(0, first=True)
            with dve.Fori(1, NC) as c:
                chunk(c)

        @block.tensor
        def _(pe):
            pe.wait_ge(ident_done, 2)
            for n in range(NT):
                if n >= 2:
                    pe.wait_ge(tp_lo, n - 1)
                if n < NC * KB:
                    c, k = divmod(n, KB)
                    per = CT // P
                    pe.wait_ge(xn_done, (c + 1) * per)
                    for i in range(per):
                        last = nc.tensor.transpose(tp[n % 2][:, i * P:(i + 1) * P],
                                                   xt[:, c * per + i, k * P:(k + 1) * P], ident[:, :])
                else:
                    h = 2 * (n - NC * KB)
                    pe.wait_ge(wk2_done, 4)
                    for r in range(2):
                        dst = tp[n % 2][:, r * DC:(r + 1) * DC]
                        nc.tensor.transpose(dst[:, 0:P], wk2[:, h + r, :, :].rearrange("p r d -> p (r d)"), ident[:, :])
                        last = nc.tensor.transpose(dst[:, P:DC], wk2_b[:, h + r, :, :].rearrange("p r d -> p (r d)"),
                                                   ident[0:DCB, 0:DCB])
                last.then_inc(tp_ready, 1)
            pe.wait_ge(wq_lo_done, 1)
            pe.wait_ge(tp_lo, NT)

            def q_pair(c, j, first):
                if not first or j >= 2:
                    pe.wait_ge(stack_lo, c * HP + (j - 1))
                terms = [(wh, xh, k) for k in range(KB) for wh, xh in ((wq_hi, xT_hi), (wq_lo, xT_hi), (wq_hi, xT_lo))]
                for n, (w, xv, k) in enumerate(terms):
                    last = nc.tensor.matmul(qp[j % 2][:, :], w[:, k, j * P:(j + 1) * P], xv[:, k, bass.ds(c * CT, CT)],
                                            start=n == 0, stop=n == len(terms) - 1)
                last.then_inc(q_ready, 1)

            def qk_pair(c, j, first):
                pe.wait_ge(stack_lo, c * HP + (j + 1))
                for r in range(2):
                    s = stack[:, j % 2, r, :]
                    if not first or j >= 1:
                        pe.wait_ge(evac_act, c * NH + (2 * (j - 1) + r + 1))
                        pe.wait_ge(evac_dve, c * NH + (2 * (j - 1) + r + 1))
                    h = 2 * j + r
                    for n, w in enumerate((wks_hi, wks_lo)):
                        nc.tensor.matmul(ap[r][:, :], w[:, h, 0:P], s, start=n == 0, stop=n == 1)
                    for n, w in enumerate((wks_hi, wks_lo)):
                        last = nc.tensor.matmul(bp[r][:, :], w[:, h, P:DC], s, start=n == 0, stop=n == 1)
                    last.then_inc(qk_ready, 1)

            def chunk(c, first=False):
                q_pair(c, 0, first)
                for j in range(HP):
                    if j + 1 < HP:
                        q_pair(c, j + 1, first)
                    qk_pair(c, j, first)

            chunk(0, first=True)
            with pe.Fori(1, NC) as c:
                chunk(c)


def newton_rstd(nc, dve, std, std_done):
    nc.vector.reciprocal(std[:, 2, :], std[:, 1, :]).then_inc(std_done, 1)
    dve.wait_ge(std_done, 2)
    nc.vector.tensor_tensor(std[:, 2, :], std[:, 2, :], std[:, 0, :], ALU.mult).then_inc(std_done, 1)
    dve.wait_ge(std_done, 3)
    nc.vector.tensor_tensor(std[:, 1, :], std[:, 1, :], std[:, 2, :], ALU.add).then_inc(std_done, 1)
    dve.wait_ge(std_done, 4)
    nc.vector.reciprocal(std[:, 2, :], std[:, 1, :]).then_inc(std_done, 1)
    dve.wait_ge(std_done, 5)
    nc.vector.tensor_scalar(std[:, 3, :], std[:, 2, :], 2.0, None, ALU.mult).then_inc(std_done, 1)
    dve.wait_ge(std_done, 6)


def attend(nc, ctx_in, ctxT_in, qk_dram, o_dram):
    KT = -(-NKV // P)
    FULL = KT - 1
    TAIL = NKV - FULL * P
    SB = HQ // P
    STEPS = SB * NB
    QC = 2 * P
    QB = SB // 2
    TG = [range(0, 4), range(4, 8), range(8, 12), range(12, KT)]
    NG = len(TG)
    CW = NKV + NKV % 2
    EDGE = (CW - 2 * 512) // 4 * 2
    CHUNKS = [(0, EDGE), (EDGE, EDGE + 512), (EDGE + 512, EDGE + 1024), (EDGE + 1024, CW)]
    S0 = 512 - EDGE
    FIRST_PART = 7
    SPB = 2
    with ExitStack() as ctx:
        sb = lambda name, shape, dt=F32: ctx.enter_context(nc.sbuf_tensor("p2_" + name, shape, dt))
        pb = lambda name, shape: ctx.enter_context(nc.psum_tensor("p2_" + name, shape, F32))
        sem = lambda name: ctx.enter_context(nc.semaphore("p2_" + name))

        raw = sb("raw", [P, KT, DC])
        nat = [sb(f"nat{i}", [P, KT, 2 * DC], F32R) for i in range(2)]
        ct_raw = sb("ct_raw", [P, CW])
        ct_hi = [sb(f"ct_hi{i}", [P, 2, CW], F32R) for i in range(2)]
        ct_lo = [sb(f"ct_lo{i}", [P, CW], F32R) for i in range(2)]
        qraw = sb("qraw", [P, 2, HQ])
        q_hi = [sb(f"q_hi{i}", [P, 2, HQ], F32R) for i in range(2)]
        q_lo = [sb(f"q_lo{i}", [P, 2, HQ], F32R) for i in range(2)]
        prob = [sb(f"prob{i}", [P, NKV]) for i in range(2)]
        pt_hi = [sb(f"pt_hi{i}", [P, KT, QC], F32R) for i in range(2)]
        pt_lo = [sb(f"pt_lo{i}", [P, KT, QC], F32R) for i in range(2)]
        o_a = [sb(f"o_a{i}", [P, QC]) for i in range(2)]
        o_b = [sb(f"o_b{i}", [P, QC]) for i in range(2)]
        negmax, rowsum, rinv = sb("negmax", [P, 2]), sb("rowsum", [P, 2]), sb("rinv", [P, 2])
        ident, zero = sb("ident", [P, P]), sb("zero", [P, 1])

        scores = pb("scores", [P, 2048])
        work = [pb(f"work{i}", [P, 512]) for i in range(3)]
        acc = pb("acc", [P, 2, QC])
        WORK_OF = (0, 1, 2, 0)

        raw_in, qk_in = sem("raw_in"), sem("qk_in")
        ct_a_in, ct_b_in = sem("ct_a_in"), sem("ct_b_in")
        zero_done = sem("zero_done")
        ident_done, raw_pad, prob_pad = sem("ident"), sem("raw_pad"), sem("prob_pad")
        nat_hi_done, nat_done = sem("nat_hi_done"), sem("nat_done")
        q_hi_done, q_done = sem("q_hi_done"), sem("q_done")
        ct_a_hi_done, ct_a_done = sem("ct_a_hi_done"), sem("ct_a_done")
        ct_b_hi_done, ct_b_done = sem("ct_b_hi_done"), sem("ct_b_done")
        scores_ready, max_done, exp_done = sem("scores_ready"), sem("max_done"), sem("exp_done")
        rinv_done, prob_done = sem("rinv_done"), sem("prob_done")
        pt_ready, pt_hi_done, pt_lo_done = sem("pt_ready"), sem("pt_hi_done"), sem("pt_lo_done")
        acc_ready, acc_act, acc_dve = sem("acc_ready"), sem("acc_act"), sem("acc_dve")
        stored = [sem("stored0"), sem("stored1")]
        block = ctx.enter_context(nc.Block())

        SPP, QPP = SPB * SB, SPB * QB

        def passes(eng, body):
            body(0, True, False)
            with eng.Fori(1, NB // SPB - 1) as r:
                body(r, False, False)
            body(NB // SPB - 1, False, True)

        @block.sync
        def _(sp):
            def load_raw(n):
                src = ctx_in[bass.ds(n, 1), :, :].rearrange("a k c -> (a k) c")
                sp.dma_start(raw[:, 0:FULL, :], src[0:FULL * P, :].rearrange("(t p) c -> p t c", p=P)).then_inc(raw_in, 16)
                sp.dma_start(raw[0:TAIL, FULL, :], src[FULL * P:NKV, :]).then_inc(raw_in, 16)

            def load_ct_a(n):
                src = ctxT_in[bass.ds(n, 1), :, :].rearrange("a c k -> (a c) k")
                sp.dma_start(ct_raw[:, 0:NKV], src[0:P, :]).then_inc(ct_a_in, 16)

            def load_ct_b(n):
                src = ctxT_in[bass.ds(n, 1), :, :].rearrange("a c k -> (a c) k")
                sp.dma_start(ct_raw[0:DCB, 0:NKV], src[P:DC, :]).then_inc(ct_b_in, 16)
                sp.dma_start(ct_raw[DCB:P, 0:NKV], src[P:DC, :]).then_inc(ct_b_in, 16)

            def load_qk(n):
                src = qk_dram[bass.ds(n, 1), :, :].rearrange("a c n -> (a c) n")
                sp.dma_start(qraw[:, 0, :], src[0:P, :]).then_inc(qk_in, 16)
                sp.dma_start(qraw[0:DCB, 1, :], src[P:DC, :]).then_inc(qk_in, 16)
                sp.dma_start(qraw[DCB:P, 1, :], src[P:DC, :]).then_inc(qk_in, 16)

            def store(i, b, quarter, parity):
                sp.wait_ge(acc_act, i + 1)
                sp.wait_ge(acc_dve, i + 1)
                dst = o_dram[bass.ds(b, 1), :, quarter * QC:(quarter + 1) * QC].rearrange("a c n -> (a c) n")
                sp.dma_start(dst[0:P, :], o_a[parity][:, :]).then_inc(stored[parity], 16)
                sp.dma_start(dst[P:DC, :], o_b[parity][0:DCB, :]).then_inc(stored[parity], 16)

            def body(r, first, last):
                for u in range(SPB):
                    b = r * SPB + u
                    i = r * QPP + u * QB
                    final = last and u == SPB - 1
                    if not (first and u == 0):
                        store(i - 2, b - 1, QB - 2, 0)
                    if not final:
                        sp.wait_ge(ct_a_done, b + 2)
                        load_ct_b(b + 1)
                    if not last:
                        sp.wait_ge(q_done, b + 2)
                        load_qk(b + 2)
                    if not (first and u == 0):
                        store(i - 1, b - 1, QB - 1, 1)
                    if not last:
                        sp.wait_ge(ct_b_done, b + 2)
                        load_ct_a(b + 2)
                    store(i, b, 0, 0)
                    if not last:
                        sp.wait_ge(nat_done, b + 2)
                        load_raw(b + 2)
                    store(i + 1, b, 1, 1)

            sp.wait_ge(raw_pad, 2)
            load_ct_a(0)
            load_qk(0)
            load_raw(0)
            sp.wait_ge(ct_a_done, 1)
            load_ct_b(0)
            sp.wait_ge(q_done, 1)
            load_qk(1)
            sp.wait_ge(ct_b_done, 1)
            load_ct_a(1)
            sp.wait_ge(nat_done, 1)
            load_raw(1)
            passes(sp, body)
            store(NB * QB - 2, NB - 1, QB - 2, 0)
            store(NB * QB - 1, NB - 1, QB - 1, 1)
            for s in stored:
                sp.wait_ge(s, 32 * NB * QB // 2)

        @block.gpsimd
        def _(pool):
            nc.gpsimd.memset(raw[:, FULL, :], 0.0).then_inc(raw_pad, 1)
            nc.gpsimd.memset(ct_raw[:, NKV:CW], 0.0).then_inc(raw_pad, 1)
            for i in range(2):
                nc.gpsimd.memset(bits(pt_hi[i][:, FULL, :]), 0.0).then_inc(prob_pad, 1)
                nc.gpsimd.memset(bits(pt_lo[i][:, FULL, :]), 0.0).then_inc(prob_pad, 1)
            nc.gpsimd.memset(zero[:, :], 0.0).then_inc(zero_done, 1)
            pool.wait_ge(zero_done, 1)
            identity(nc, pool, ident, ident_done)

            def round_to(dst, src):
                flat = (zero[:, :] if len(src.shape) == 2 else zero[:, :].unsqueeze(1)).broadcast_to(src.shape)
                return nc.gpsimd.tensor_tensor(dst, src, flat, ALU.add)

            def prepare(n, par, fresh):
                pool.wait_ge(ct_a_in, (n + 1) * 16)
                if not fresh:
                    pool.wait_ge(scores_ready, (n - 1) * SB)
                round_to(ct_hi[par][:, 0, :], ct_raw[:, :]).then_inc(ct_a_hi_done, 1)
                pool.wait_ge(ct_a_hi_done, n + 1)
                nc.gpsimd.tensor_tensor(ct_lo[par][:, :], ct_raw[:, :], bits(ct_hi[par][:, 0, :]),
                                        ALU.subtract).then_inc(ct_a_done, 1)
                pool.wait_ge(qk_in, (n + 1) * 48)
                round_to(q_hi[par][:, :, :], qraw[:, :, :]).then_inc(q_hi_done, 1)
                pool.wait_ge(q_hi_done, n + 1)
                nc.gpsimd.tensor_tensor(q_lo[par][:, :, :], qraw[:, :, :], bits(q_hi[par][:, :, :]),
                                        ALU.subtract).then_inc(q_done, 1)
                lower = slice(DCB, P)
                pool.wait_ge(ct_b_in, (n + 1) * 32)
                round_to(ct_hi[par][:, 1, :], ct_raw[:, :]).then_inc(ct_b_hi_done, 1)
                pool.wait_ge(ct_b_hi_done, n + 1)
                nc.gpsimd.tensor_tensor(ct_hi[par][lower, 1, :], ct_raw[lower, :], bits(ct_hi[par][lower, 1, :]),
                                        ALU.subtract).then_inc(ct_b_done, 1)
                x = nat[par]
                pool.wait_ge(ct_b_done, n + 1)
                pool.wait_ge(raw_in, (n + 1) * 32)
                if not fresh:
                    pool.wait_ge(acc_ready, (n - 1) * QB)
                round_to(x[:, :, 0:DC], raw[:, :, :]).then_inc(nat_hi_done, 1)
                pool.wait_ge(nat_hi_done, n + 1)
                nc.gpsimd.tensor_tensor(x[:, :, DC:DC + DCB], raw[:, :, P:DC], bits(x[:, :, P:DC]), ALU.subtract)
                nc.gpsimd.tensor_tensor(x[:, :, DC + DCB:2 * DC], raw[:, :, 0:P], bits(x[:, :, 0:P]),
                                        ALU.subtract).then_inc(nat_done, 1)

            def body(r, first, last):
                for u in range(SPB):
                    if not (last and u == SPB - 1):
                        prepare(r * SPB + (u + 1), (u + 1) % 2, first and u == 0)

            prepare(0, 0, True)
            passes(pool, body)

        def transposed(buf, slot, g, half):
            tiles, rows = TG[g], slice(0, TAIL if g == NG - 1 else P)
            src = work[WORK_OF[g]][rows, 0:len(tiles) * P].rearrange("p (t n) -> p t n", n=P)
            return src, buf[slot][rows, tiles[0]:tiles[-1] + 1, half * P:(half + 1) * P]

        @block.scalar
        def _(act):
            def pt_copy(s, g, slot, half):
                act.wait_ge(pt_ready, s * NG + (g + 1))
                src, dst = transposed(pt_hi, slot, g, half)
                nc.scalar.activation(dst, src, ACT.Copy).then_inc(pt_hi_done, 1)

            def acc_copy(i, parity, fresh):
                if not fresh:
                    act.wait_ge(stored[parity], (i - parity) * 16)
                act.wait_ge(acc_ready, i + 1)
                nc.scalar.activation(o_a[parity][:, :], acc[:, 0, :], ACT.Copy)
                nc.scalar.activation(o_b[parity][DCB:P, :], acc[DCB:P, 1, :], ACT.Copy).then_inc(acc_act, 1)

            def step(r, j, first, last):
                s = r * SPP + j
                prev = not (first and j == 0)
                if prev:
                    slot, half = ((j - 1) // 2) % 2, (j - 1) % 2
                    if first and j == 1:
                        act.wait_ge(prob_pad, 4)
                    if not (first and j < 5):
                        act.wait_ge(acc_ready, r * QPP + ((j - 1) // 2 - 1))
                    pt_copy(s - 1, 0, slot, half)
                    pt_copy(s - 1, 1, slot, half)
                act.wait_ge(max_done, s + 1)
                nc.scalar.activation(prob[j % 2][:, 0:NKV], scores[:, S0:S0 + NKV], ACT.Exp, bias=negmax[:, j % 2:j % 2 + 1],
                                     accum_out=rowsum[:, j % 2:j % 2 + 1]).then_inc(exp_done, 1)
                if prev:
                    pt_copy(s - 1, 2, slot, half)
                act.wait_ge(rinv_done, s + 1)
                nc.scalar.activation(prob[j % 2][:, 0:NKV], prob[j % 2][:, 0:NKV], ACT.Copy,
                                     scale=rinv[:, j % 2:j % 2 + 1]).then_inc(prob_done, 1)
                if prev:
                    pt_copy(s - 1, 3, slot, half)
                if j % 2 == 0 and not (first and j < 4):
                    acc_copy(r * QPP + (j // 2 - 2), (j // 2) % 2, first and j < 8)

            def body(r, first, last):
                for j in range(SPP):
                    step(r, j, first, last)

            passes(act, body)
            act.wait_ge(acc_ready, STEPS // 2 - 2)
            for g in range(NG):
                pt_copy(STEPS - 1, g, 1, 1)
            acc_copy(NB * QB - 2, 0, False)
            acc_copy(NB * QB - 1, 1, False)

        @block.vector
        def _(dve):
            def pt_sub(s, g, slot, half):
                dve.wait_ge(pt_hi_done, s * NG + (g + 1))
                src, lo = transposed(pt_lo, slot, g, half)
                _, hi = transposed(pt_hi, slot, g, half)
                nc.vector.tensor_tensor(lo, src, bits(hi), ALU.subtract).then_inc(pt_lo_done, 1)

            def acc_add(i, parity):
                dve.wait_ge(acc_act, i + 1)
                nc.vector.tensor_tensor(o_b[parity][0:DCB, :], acc[0:DCB, 1, :], o_b[parity][DCB:P, :],
                                        ALU.add).then_inc(acc_dve, 1)

            def step(r, j, first, last):
                s = r * SPP + j
                prev = not (first and j == 0)
                slot, half = ((j - 1) // 2) % 2, (j - 1) % 2
                dve.wait_ge(scores_ready, s + 1)
                nc.vector.tensor_reduce(negmax[:, j % 2:j % 2 + 1], scores[:, S0:S0 + NKV], AX.X, ALU.max,
                                        negate=True).then_inc(max_done, 1)
                if prev:
                    pt_sub(s - 1, 0, slot, half)
                    pt_sub(s - 1, 1, slot, half)
                dve.wait_ge(exp_done, s + 1)
                nc.vector.reciprocal(rinv[:, j % 2:j % 2 + 1], rowsum[:, j % 2:j % 2 + 1]).then_inc(rinv_done, 1)
                if prev:
                    pt_sub(s - 1, 2, slot, half)
                    pt_sub(s - 1, 3, slot, half)
                if j % 2 == 0 and not (first and j < 4):
                    acc_add(r * QPP + (j // 2 - 2), (j // 2) % 2)

            def body(r, first, last):
                for j in range(SPP):
                    step(r, j, first, last)

            passes(dve, body)
            for g in range(NG):
                pt_sub(STEPS - 1, g, 1, 1)
            acc_add(NB * QB - 2, 0)
            acc_add(NB * QB - 1, 1)

        @block.tensor
        def _(pe):
            def step_scores(r, j, par, first):
                s, b = r * SPP + j, r * SPB + j // SB
                if j % SB == 0:
                    pe.wait_ge(ct_b_done, b + 1)
                    pe.wait_ge(q_done, b + 1)
                if not (first and j == 0):
                    pe.wait_ge(exp_done, s)
                rows = slice((j % SB) * P, (j % SB + 1) * P)
                q_a, q_b = (slice(None), 0, rows), (slice(None), 1, rows)
                for lo, hi in CHUNKS:
                    ct_a, ct_b, ct_al = (t[:, lo:hi] for t in (ct_hi[par][:, 0, :], ct_hi[par][:, 1, :], ct_lo[par]))
                    terms = ((q_hi[par][q_a], ct_a), (q_lo[par][q_a], ct_a), (q_hi[par][q_a], ct_al),
                             (q_hi[par][q_b], ct_b), (q_lo[par][q_b], ct_b))
                    for m, (w, c) in enumerate(terms):
                        last = nc.tensor.matmul(scores[:, S0 + lo:S0 + hi], w, c, start=m == 0, stop=m == len(terms) - 1)
                last.then_inc(scores_ready, 1)

            def pt_transpose(s, g, j):
                for k, t in enumerate(TG[g]):
                    width = min(P, NKV - t * P)
                    last = nc.tensor.transpose(work[WORK_OF[g]][0:width, k * P:(k + 1) * P],
                                               prob[(j - 1) % 2][:, t * P:t * P + width], ident[:, :])
                last.then_inc(pt_ready, 1)

            def product(slot, par, tiles):
                x = nat[par]
                for k in tiles:
                    a_hi, b_both, a_lo = x[:, k, 0:P], x[:, k, P:P + 2 * DCB], x[:, k, DC + DCB:2 * DC]
                    terms = ((0, a_hi, pt_hi), (0, a_hi, pt_lo), (0, a_lo, pt_hi), (1, b_both, pt_hi), (1, b_both, pt_lo))
                    for m, (blk, w, pt) in enumerate(terms):
                        last = nc.tensor.matmul(acc[:, blk, :], w, pt[slot][:, k, :], start=k == 0 and m == 0,
                                                stop=k == KT - 1 and m in (2, 4), skip_group_check=True)
                if tiles[-1] == KT - 1:
                    last.then_inc(acc_ready, 1)

            def step(r, j, first, last):
                s = r * SPP + j
                prev = not (first and j == 0)
                step_scores(r, j, (j // SB) % 2, first)
                work_left, q_at = [], None
                if j % 2 == 1 and not (first and j < 3):
                    q_at, work_left = (j - 3) // 2, list(range(0, FIRST_PART))
                elif j % 2 == 0 and not (first and j < 4):
                    q_at, work_left = (j - 4) // 2, list(range(FIRST_PART, KT))
                slot, par = (q_at % 2, (q_at // QB) % 2) if q_at is not None else (0, 0)
                if work_left and j % 2 == 1:
                    i = r * QPP + (j - 3) // 2
                    if (j - 3) // 2 % QB == 0:
                        pe.wait_ge(nat_done, r * SPB + (j - 3) // SB + 1)
                    pe.wait_ge(pt_lo_done, (i + 1) * 2 * NG)
                    if not (first and j == 3):
                        pe.wait_ge(acc_dve, i)
                if prev:
                    pe.wait_ge(prob_done, s)
                    if not (first and j == 1):
                        pe.wait_ge(pt_lo_done, (s - 1) * NG)
                    pt_transpose(s - 1, 0, j)
                    pt_transpose(s - 1, 1, j)
                if work_left:
                    product(slot, par, work_left[0:4])
                if prev:
                    pt_transpose(s - 1, 2, j)
                if work_left:
                    product(slot, par, work_left[4:6])
                if prev:
                    pe.wait_ge(pt_lo_done, (s - 1) * NG + 1)
                    pt_transpose(s - 1, 3, j)
                if work_left[6:]:
                    product(slot, par, work_left[6:])

            def body(r, first, last):
                for j in range(SPP):
                    step(r, j, first, last)

            pe.wait_ge(ident_done, 2)
            passes(pe, body)
            pe.wait_ge(prob_done, STEPS)
            pe.wait_ge(pt_lo_done, (STEPS - 1) * NG)
            for g in range(3):
                pt_transpose(STEPS - 1, g, 2)
            pe.wait_ge(pt_lo_done, (STEPS - 1) * NG + 1)
            pt_transpose(STEPS - 1, 3, 2)
            product(0, 1, list(range(FIRST_PART, KT)))
            pe.wait_ge(pt_lo_done, STEPS * NG)
            pe.wait_ge(acc_dve, NB * QB - 1)
            product(1, 1, list(range(KT)))


def attention_output(nc, w_kv, w_out, b_out, x, o_dram, resid):
    NC, CT = 4, TOK // 4
    CB, CTT = CT // NQ, CT // P
    HP = NH // 2
    PL = 2
    NL = HP // PL
    W = PL * 2 * NQ
    with ExitStack() as ctx:
        sb = lambda name, shape, dt=F32: ctx.enter_context(nc.sbuf_tensor("p3_" + name, shape, dt))
        pb = lambda name, shape: ctx.enter_context(nc.psum_tensor("p3_" + name, shape, F32))
        sem = lambda name: ctx.enter_context(nc.semaphore("p3_" + name))

        wv = sb("wv", [P, 2, INNER])
        wo = sb("wo", [P, HP, DM])
        wv_hi, wv_lo = sb("wv_hi", [P, 2, HP, 2, P], F32R), sb("wv_lo", [P, 2, HP, 2, P], F32R)
        wo_hi, wo_lo = sb("wo_hi", [P, HP, DM], F32R), sb("wo_lo", [P, HP, DM], F32R)
        bias = sb("bias", [P, DM])
        oa = [sb(f"oa{i}", [P, CB, W]) for i in range(2)]
        ob = [sb(f"ob{i}", [P, CB, W]) for i in range(2)]
        oa_hi = [sb(f"oa_hi{i}", [P, CB, W], F32R) for i in range(2)]
        oa_lo = [sb(f"oa_lo{i}", [P, CB, W], F32R) for i in range(2)]
        ob_both = [sb(f"ob_both{i}", [P, CB, W], F32R) for i in range(2)]
        at_hi, at_lo = sb("at_hi", [P, HP, CT], F32R), sb("at_lo", [P, HP, CT], F32R)
        vp = [pb(f"vp{i}", [P, CT]) for i in range(2)]
        yp = [pb(f"yp{i}", [P, 512]) for i in range(2)]

        w_in, x_in, b_in = sem("w_in"), sem("x_in"), sem("b_in")
        o_in = [sem("o_in0"), sem("o_in1")]
        zeroed, w_hi_done, w_lo_done, biased = sem("zeroed"), sem("w_hi"), sem("w_lo"), sem("biased")
        o_hi, o_lo = sem("o_hi"), sem("o_lo")
        v_ready, at_hi_done, at_lo_done = sem("v_ready"), sem("at_hi"), sem("at_lo")
        y_ready, y_added = sem("y_ready"), sem("y_added")
        block = ctx.enter_context(nc.Block())

        @block.sync
        def _(sp):
            sp.dma_start(wv[:, 0, :], w_kv[0:P, INNER:2 * INNER]).then_inc(w_in, 16)
            for half in (slice(0, DCB), slice(DCB, P)):
                sp.dma_start(wv[half, 1, :], w_kv[P:DC, INNER:2 * INNER]).then_inc(w_in, 16)
            sp.dma_start(wo[:, :, :], w_out.rearrange("(j p) n -> p j n", p=P)).then_inc(w_in, 16)

            def load(c, l, fresh):
                if not fresh:
                    sp.wait_ge(o_lo, c * NL + (l - 1))
                src = o_dram[bass.ds(c * CB, CB), :, l * W:(l + 1) * W]
                for dst, rows in ((oa[l % 2][:, :, :], slice(0, P)), (ob[l % 2][0:DCB], slice(P, DC)), (ob[l % 2][DCB:P], slice(P, DC))):
                    sp.dma_start(dst, src[:, rows, :].rearrange("b c n -> c b n")).then_inc(o_in[l % 2], 16)

            for l in range(2):
                load(0, l, True)
            sp.dma_start(resid[:, :, :], x.rearrange("(t b) q d -> (b q) t d", b=P // NQ)).then_inc(x_in, 16)
            sp.dma_start(bias[:, :], b_out.rearrange("(a n) -> a n", a=1).partition_broadcast(P)).then_inc(b_in, 16)
            for l in range(2, NL):
                load(0, l, False)
            with sp.Fori(1, NC) as c:
                for l in range(NL):
                    load(c, l, False)

        @block.gpsimd
        def _(pool):
            nc.gpsimd.memset(bits(wv_hi[:, :, :, :, :]), 0.0).then_inc(zeroed, 1)
            nc.gpsimd.memset(bits(wv_lo[:, :, :, :, :]), 0.0).then_inc(zeroed, 1)
            pool.wait_ge(x_in, 16)
            pool.wait_ge(b_in, 16)
            for t in range(TT):
                nc.gpsimd.tensor_tensor(resid[:, t, :], resid[:, t, :], bias[:, :], ALU.add).then_inc(biased, 1)

        def wv_place(dst, blk, r):
            half = slice(r * DH, (r + 1) * DH)
            return dst[:, blk, :, r, half], wv[:, blk, :].rearrange("p (j r d) -> p j r d", r=2, d=DH)[:, :, r, :]

        @block.scalar
        def _(act):
            act.wait_ge(w_in, 64)
            act.wait_ge(zeroed, 2)
            for blk in range(2):
                for r in range(2):
                    dst, src = wv_place(wv_hi, blk, r)
                    nc.scalar.activation(dst, src, ACT.Copy).then_inc(w_hi_done, 1)

            def split(c, l, fresh):
                act.wait_ge(o_in[l % 2], c * (NL // 2 * 48) + (l // 2 + 1) * 48)
                if not fresh:
                    act.wait_ge(v_ready, c * HP + (l - 1) * PL)
                nc.scalar.activation(oa_hi[l % 2][:, :, :], oa[l % 2][:, :, :], ACT.Copy)
                nc.scalar.activation(ob_both[l % 2][:, :, :], ob[l % 2][:, :, :], ACT.Copy).then_inc(o_hi, 1)

            def chunk(c, first):
                for l in range(NL):
                    if l + 1 < NL:
                        split(c, l + 1, first and l == 0)
                    for j in range(l * PL, (l + 1) * PL):
                        act.wait_ge(v_ready, c * HP + (j + 1))
                        if j == 0 and not first:
                            act.wait_ge(y_ready, c * CTT)
                        nc.scalar.activation(at_hi[:, j, :], vp[j % 2][:, :], ACT.Copy).then_inc(at_hi_done, 1)

            split(0, 0, True)
            nc.scalar.activation(wo_hi[:, :, :], wo[:, :, :], ACT.Copy).then_inc(w_hi_done, 1)
            chunk(0, True)
            with act.Fori(1, NC) as c:
                split(c, 0, False)
                chunk(c, False)

        @block.vector
        def _(dve):
            for blk in range(2):
                for r in range(2):
                    dst, src = wv_place(wv_lo, blk, r)
                    hi, _ = wv_place(wv_hi, blk, r)
                    dve.wait_ge(w_hi_done, blk * 2 + r + 1)
                    nc.vector.tensor_tensor(dst, src, bits(hi), ALU.subtract).then_inc(w_lo_done, 1)

            def split(c, l):
                dve.wait_ge(o_hi, c * NL + (l + 1))
                lower = slice(DCB, P)
                nc.vector.tensor_tensor(oa_lo[l % 2][:, :, :], oa[l % 2][:, :, :], bits(oa_hi[l % 2][:, :, :]), ALU.subtract)
                nc.vector.tensor_tensor(ob_both[l % 2][lower], ob[l % 2][lower], bits(ob_both[l % 2][lower]),
                                        ALU.subtract).then_inc(o_lo, 1)

            def chunk(c, first):
                for l in range(NL):
                    if l + 1 < NL:
                        split(c, l + 1)
                    for j in range(l * PL, (l + 1) * PL):
                        dve.wait_ge(at_hi_done, c * HP + (j + 1))
                        nc.vector.tensor_tensor(at_lo[:, j, :], vp[j % 2][:, :], bits(at_hi[:, j, :]),
                                                ALU.subtract).then_inc(at_lo_done, 1)
                for t in range(CTT):
                    if t == 0 and first:
                        dve.wait_ge(biased, TT)
                    dve.wait_ge(y_ready, c * CTT + (t + 1))
                    tile = resid[:, bass.ds(c * CTT + t, 1), :].rearrange("p a d -> p (a d)")
                    nc.vector.tensor_tensor(tile, yp[t % 2][:, 0:DM], tile, ALU.add).then_inc(y_added, 1)

            split(0, 0)
            dve.wait_ge(w_hi_done, 5)
            nc.vector.tensor_tensor(wo_lo[:, :, :], wo[:, :, :], bits(wo_hi[:, :, :]), ALU.subtract).then_inc(w_lo_done, 1)
            chunk(0, True)
            with dve.Fori(1, NC) as c:
                split(c, 0)
                chunk(c, False)

        @block.tensor
        def _(pe):
            def values(c, l, first):
                pe.wait_ge(o_lo, c * NL + (l + 1))
                for j in range(l * PL, (l + 1) * PL):
                    if not (first and j < 2):
                        pe.wait_ge(at_lo_done, c * HP + (j - 1))
                    terms = []
                    for r in range(2):
                        h = slice((2 * (j - l * PL) + r) * NQ, (2 * (j - l * PL) + r + 1) * NQ)
                        a_hi, a_lo, b_both = oa_hi[l % 2][:, :, h], oa_lo[l % 2][:, :, h], ob_both[l % 2][:, :, h]
                        terms += [(wv_hi[:, 0, j, r, :], a_hi), (wv_lo[:, 0, j, r, :], a_hi), (wv_hi[:, 0, j, r, :], a_lo),
                                  (wv_hi[:, 1, j, r, :], b_both), (wv_lo[:, 1, j, r, :], b_both)]
                    for m, (w, o) in enumerate(terms):
                        last = nc.tensor.matmul(vp[j % 2][:, :].rearrange("p (b q) -> p b q", q=NQ), w, o,
                                                start=m == 0, stop=m == len(terms) - 1)
                    last.then_inc(v_ready, 1)

            def output(c, t, first):
                if t == 0:
                    pe.wait_ge(at_lo_done, (c + 1) * HP)
                if not (first and t < 2):
                    pe.wait_ge(y_added, c * CTT + (t - 1))
                tok = slice(t * P, (t + 1) * P)
                terms = [(a[:, j, tok], w[:, j, :]) for j in range(HP)
                         for a, w in ((at_hi, wo_hi), (at_hi, wo_lo), (at_lo, wo_hi))]
                for m, (a, w) in enumerate(terms):
                    last = nc.tensor.matmul(yp[t % 2][:, 0:DM], a, w, start=m == 0, stop=m == len(terms) - 1)
                last.then_inc(y_ready, 1)

            def chunk(c, first):
                for l in range(NL):
                    values(c, l, first)
                if first:
                    pe.wait_ge(w_lo_done, 5)
                for t in range(CTT):
                    output(c, t, first)

            pe.wait_ge(w_lo_done, 4)
            chunk(0, True)
            with pe.Fori(1, NC) as c:
                chunk(c, False)


def mix_and_feed(nc, channels, squares, bo, w1, b1_cols, w2, b2, resid, out):
    NC, CT = 4, TOK // 4
    CB, CTT = CT // NQ, CT // P
    KB = DM // P
    WIDTH = w1.shape[1]
    FB = WIDTH // P
    NM = 3 * KB
    BR = 33
    with ExitStack() as ctx:
        sb = lambda name, shape, dt=F32: ctx.enter_context(nc.sbuf_tensor("p4_" + name, shape, dt))
        pb = lambda name, shape: ctx.enter_context(nc.psum_tensor("p4_" + name, shape, F32))
        sem = lambda name: ctx.enter_context(nc.semaphore("p4_" + name))

        sqT_hi, sqT_lo = sb("sqT_hi", [P, 4, KB, DM], F32R), sb("sqT_lo", [P, 4, KB, DM], F32R)
        w1_hi, w1_lo = sb("w1_hi", [P, KB, WIDTH], F32R), sb("w1_lo", [P, KB, WIDTH], F32R)
        w2_hi, w2_lo = sb("w2_hi", [P, FB, DM], F32R), sb("w2_lo", [P, FB, DM], F32R)
        hid_hi, hid_lo = sb("hid_hi", [P, FB, CT], F32R), sb("hid_lo", [P, FB, CT], F32R)
        area = sb("area", [P, 13, CT])
        slot = lambda n: area[:, n, :]
        eb, er, wkv = [slot(0), slot(1)], [slot(2), slot(3)], [slot(4), slot(5)]
        num, den, prod = slot(6), slot(7), slot(8)
        hid = [slot(9), slot(10)]
        zT = area[:, 11:13, :]
        weights = lambda n, inner: area[:, n:n + 4, :].rearrange("p f n -> p (f n)").rearrange("p (k n) -> p k n", n=inner)
        w1_raw, w2_raw = weights(0, WIDTH), weights(8, DM)
        square = area[:, 4:8, :].rearrange("p m (k n) -> p m k n", n=DM)
        bias_raw, bias = sb("bias_raw", [BR, 2, DM]), sb("bias", [BR, 2, DM], F32R)
        ones = sb("ones", [BR, P], F32R)
        channel = sb("channel", [P, 5, KB])
        td = sb("td", [P, 2, KB])
        tdm = sb("tdm", [P, KB, CB, NQ])
        b1_col = sb("b1_col", [P, FB])
        ident = sb("ident", [P, P])
        stats = [sb(f"stats{m}", [P, CTT, 6]) for m in range(2)]
        parts = [sb(f"parts{m}", [P, 3, CTT]) for m in range(2)]
        mean = [sb(f"mean{m}", [P, CTT]) for m in range(2)]
        std = [sb(f"std{m}", [P, 4, CTT]) for m in range(2)]
        xn = [sb(f"xn{m}", [P, CTT, DM]) for m in range(2)]
        xnT = sb("xnT", [P, KB, CB, NQ + 1])
        diff = sb("diff", [P, KB, CB, NQ])
        mixed = sb("mixed", [P, 3, CB, NQ])
        mixed_hi, mixed_lo = sb("mixed_hi", [P, 3, KB, CT], F32R), sb("mixed_lo", [P, 3, KB, CT], F32R)
        ek, ekv = ([sb(f"{n}{o}", [P, CB, NQ]) for o in range(KB)] for n in ("ek", "ekv"))
        wkv_hi, wkv_lo = sb("wkv_hi", [P, KB, CT], F32R), sb("wkv_lo", [P, KB, CT], F32R)
        zT_hi, zT_lo = sb("zT_hi", [P, KB, CT], F32R), sb("zT_lo", [P, KB, CT], F32R)

        tp = pb("tp", [P, 512])
        rp = [pb(f"rp{i}", [P, CT]) for i in range(3)]
        fp = [pb(f"fp{i}", [P, CT]) for i in range(2)]
        yp = [pb(f"yp{i}", [P, 512]) for i in range(2)]

        sq_in, ch_in, b_in, w1_in, w2_in = sem("sq_in"), sem("ch_in"), sem("b_in"), sem("w1_in"), sem("w2_in")
        ident_done, zeroed, td_act, td_dve = sem("ident"), sem("zeroed"), sem("td_act"), sem("td_dve")
        bias_zero, ones_done, bias_done = sem("bias_zero"), sem("ones_done"), sem("bias_done")
        sq_hi_done, sq_lo_done = sem("sq_hi"), sem("sq_lo")
        w1_hi_done, w1_lo_done, w2_hi_done, w2_lo_done = sem("w1_hi"), sem("w1_lo"), sem("w2_hi"), sem("w2_lo")
        ln_step, xn_done = [sem("ln_step0"), sem("ln_step1")], [sem("xn_done0"), sem("xn_done1")]
        tp_ready, tp_read = [sem("tp_ready0"), sem("tp_ready1")], [sem("tp_read0"), sem("tp_read1")]
        zT_lo_done = sem("zT_lo_done")
        diff_done, mix_done, mix_hi, mix_lo = sem("diff_done"), sem("mix_done"), sem("mix_hi"), sem("mix_lo")
        r_ready, exps_done, wkv_step = sem("r_ready"), sem("exps_done"), sem("wkv_step")
        wkv_hi_done, wkv_lo_done = sem("wkv_hi_done"), sem("wkv_lo_done")
        g_ready, g_added = sem("g_ready"), sem("g_added")
        f_ready, hid_done, hid_lo_done = sem("f_ready"), sem("hid_done"), sem("hid_lo_done")
        y_ready, y_added, stored = sem("y_ready"), sem("y_added"), sem("stored")
        block = ctx.enter_context(nc.Block())

        LN = CTT + 7 + 1 + 5
        WS = 9

        def tile_of(c, t):
            return resid[:, bass.ds(c * CTT + t, 1), :].rearrange("p a d -> p (a d)")

        def fresh(c):
            return isinstance(c, int) and c == 0

        def passes(eng, run):
            run(-2, "A")
            run(-1, "AB")
            run(0, "ABC")
            with eng.Fori(1, NC - 2) as i:
                run(i, "ABC")
            run(NC - 2, "BC")
            run(NC - 1, "C")

        @block.sync
        def _(sp):
            sp.dma_start(channel[:, :, :], channels).then_inc(ch_in, 16)
            sp.dma_start(b1_col[:, :], b1_cols).then_inc(ch_in, 16)
            for m in range(4):
                sp.dma_start(square[:, m, :, :], squares[m, :, :].rearrange("(k p) n -> p k n", p=P)).then_inc(sq_in, 16)
            sp.dma_start(w1_raw, w1.rearrange("(k p) n -> p k n", p=P)).then_inc(w1_in, 16)
            sp.dma_start(w2_raw, w2.rearrange("(k p) n -> p k n", p=P)).then_inc(w2_in, 16)
            sp.wait_ge(bias_zero, 1)
            for n, v in enumerate((bo, b2)):
                for row in (0, BR - 1):
                    sp.dma_start(bias_raw[row:row + 1, n, :], v.rearrange("(a n) -> a n", a=1)).then_inc(b_in, 16)
            out_v = out.rearrange("(c u b) q d -> (b q) (c u) d", b=P // NQ, u=CTT)
            with sp.Fori(0, NC) as c:
                sp.wait_ge(y_added, (c + 1) * CTT)
                sp.dma_start(out_v[:, bass.ds(c * CTT, CTT), :], resid[:, bass.ds(c * CTT, CTT), :]).then_inc(stored, 16)
            sp.wait_ge(stored, NC * 16)

        @block.gpsimd
        def _(pool):
            identity(nc, pool, ident, ident_done)
            nc.gpsimd.memset(bias_raw[:, :, :], 0.0).then_inc(bias_zero, 1)
            nc.gpsimd.memset(xnT[:, :, :, 0:1], 0.0).then_inc(zeroed, 1)
            for o in range(KB):
                nc.gpsimd.memset(ek[o][:, :, 0:1], 0.0).then_inc(zeroed, 1)
                nc.gpsimd.memset(ekv[o][:, :, 0:1], 0.0).then_inc(zeroed, 1)
            nc.gpsimd.memset(tdm[:, :, :, :], 1.0).then_inc(zeroed, 1)
            pool.wait_ge(zeroed, 2 * KB + 2)
            nc.gpsimd.memset(tdm[:, :, :, 0:1], 0.0).then_inc(zeroed, 1)
            nc.gpsimd.memset(bits(ones[:, :]), 1.0).then_inc(ones_done, 1)
            pool.wait_ge(sq_hi_done, 1)
            nc.gpsimd.tensor_tensor(sqT_lo[:, :, :, :], square, bits(sqT_hi[:, :, :, :]), ALU.subtract).then_inc(sq_lo_done, 1)

            def mixed_sub(c):
                for n in range(NM):
                    k, m = n // 3, n % 3
                    pool.wait_ge(mix_hi, c * NM + (n + 1))
                    nc.gpsimd.tensor_tensor(mixed_lo[:, m, k, :], mixed[:, m, :, :].rearrange("p b q -> p (b q)"),
                                            bits(mixed_hi[:, m, k, :]), ALU.subtract).then_inc(mix_lo, 1)

            def wkv_sub(c):
                for o in range(KB):
                    pool.wait_ge(wkv_hi_done, c * KB + (o + 1))
                    nc.gpsimd.tensor_tensor(wkv_lo[:, o, :], wkv[o][:, :], bits(wkv_hi[:, o, :]), ALU.subtract).then_inc(wkv_lo_done, 1)

            def feed_sub(c):
                for k in range(KB):
                    pool.wait_ge(tp_read[1], c * KB + (k + 1))
                    nc.gpsimd.tensor_tensor(zT_lo[:, k, :], zT[:, k, :], bits(zT_hi[:, k, :]), ALU.subtract).then_inc(zT_lo_done, 1)

            def hidden_sub(c):
                for f in range(FB):
                    pool.wait_ge(hid_done, c * FB + (f + 1))
                    if not fresh(c) and f == 0:
                        pool.wait_ge(y_ready, c * CTT)
                    nc.gpsimd.tensor_tensor(hid_lo[:, f, :], hid[f % 2][:, :], bits(hid_hi[:, f, :]), ALU.subtract).then_inc(hid_lo_done, 1)

            def run(i, stages):
                if "C" in stages:
                    hidden_sub(i)
                if "B" in stages:
                    wkv_sub(i + 1)
                if "A" in stages:
                    mixed_sub(i + 2)
                if "B" in stages:
                    feed_sub(i + 1)
                if isinstance(i, int) and i == -2:
                    pool.wait_ge(w1_hi_done, 1)
                    nc.gpsimd.tensor_tensor(w1_lo[:, :, :], w1_raw, bits(w1_hi[:, :, :]), ALU.subtract).then_inc(w1_lo_done, 1)
                    pool.wait_ge(w2_hi_done, 1)
                    nc.gpsimd.tensor_tensor(w2_lo[:, :, :], w2_raw, bits(w2_hi[:, :, :]), ALU.subtract).then_inc(w2_lo_done, 1)

            passes(pool, run)

        @block.scalar
        def _(act):
            def first_weights():
                act.wait_ge(ch_in, 2 * 16)
                nc.scalar.activation(td[:, 0, :], channel[:, 0, :], ACT.Exp).then_inc(td_act, 1)
                act.wait_ge(td_act, 1)
                nc.scalar.activation(td[:, 1, :], td[:, 0, :], ACT.Exp, scale=-1.0).then_inc(td_act, 1)
                act.wait_ge(sq_in, 64)
                nc.scalar.activation(sqT_hi[:, :, :, :], square, ACT.Copy).then_inc(sq_hi_done, 1)

            def root(c, m):
                act.wait_ge(ln_step[m], c * LN + (CTT + 7))
                nc.scalar.activation(std[m][:, 1, :], std[m][:, 0, :], ACT.Sqrt).then_inc(ln_step[m], 1)

            def mix_in(c):
                for k in range(KB):
                    act.wait_ge(tp_ready[0], c * KB + (k + 1))
                    if k == 0 and fresh(c):
                        act.wait_ge(zeroed, 2 * KB + 3)
                    if k == 0 and not fresh(c):
                        act.wait_ge(mix_done, c * NM)
                    nc.scalar.activation(xnT[:, k, :, 1:NQ + 1], tp[:, :].rearrange("p (b q) -> p b q", q=NQ),
                                         ACT.Copy).then_inc(tp_read[0], 1)

            def feed_copy(c):
                for k in range(KB):
                    act.wait_ge(tp_ready[1], c * KB + (k + 1))
                    if not fresh(c) and k == 0:
                        act.wait_ge(f_ready, c * FB)
                    nc.scalar.activation(zT_hi[:, k, :], tp[:, :], ACT.Copy)
                    nc.scalar.activation(zT[:, k, :], tp[:, :], ACT.Copy).then_inc(tp_read[1], 1)

            def mix_round(c):
                for n in range(NM):
                    k, m = n // 3, n % 3
                    act.wait_ge(mix_done, c * NM + (n + 1))
                    if not fresh(c) and n == 0:
                        act.wait_ge(r_ready, c * NM)
                    nc.scalar.activation(mixed_hi[:, m, k, :], mixed[:, m, :, :].rearrange("p b q -> p (b q)"),
                                         ACT.Copy).then_inc(mix_hi, 1)

            def exps(c, o):
                act.wait_ge(r_ready, c * NM + 3 * (o + 1))
                if fresh(c) and o == 0:
                    act.wait_ge(w1_lo_done, 1)
                    act.wait_ge(w2_lo_done, 1)
                if not fresh(c):
                    act.wait_ge(wkv_step, c * (KB * WS) - (KB - 1 - o) * WS)
                kp = rp[0][:, :].rearrange("p (b q) -> p b q", q=NQ)
                nc.scalar.activation(ek[o][:, :, 1:NQ], kp[:, :, 0:NQ - 1], ACT.Exp)
                nc.scalar.activation(eb[o][:, :], rp[0][:, :], ACT.Exp, bias=channel[:, 1, o:o + 1])
                nc.scalar.activation(er[o][:, :], rp[2][:, :], ACT.Exp, scale=-1.0).then_inc(exps_done, 1)

            def wkv_round(c, o):
                act.wait_ge(wkv_step, c * (KB * WS) + (o + 1) * WS)
                if not fresh(c) and o == 0:
                    act.wait_ge(g_ready, c * CTT)
                nc.scalar.activation(wkv_hi[:, o, :], wkv[o][:, :], ACT.Copy).then_inc(wkv_hi_done, 1)

            def relus(c, blocks):
                for f in blocks:
                    act.wait_ge(f_ready, c * FB + (f + 1))
                    if not (fresh(c) and f < 2):
                        act.wait_ge(hid_lo_done, c * FB + (f - 1))
                    if not fresh(c) and f == 0:
                        act.wait_ge(y_ready, c * CTT)
                    for dst in (hid_hi[:, f, :], hid[f % 2][:, :]):
                        last = nc.scalar.activation(dst, fp[f % 2][:, :], ACT.Relu, bias=b1_col[:, f:f + 1])
                    last.then_inc(hid_done, 1)

            def run(i, stages):
                if "A" in stages:
                    root(i + 2, 0)
                if isinstance(i, int) and i == -2:
                    first_weights()
                if "B" in stages:
                    exps(i + 1, 0)
                if "C" in stages:
                    relus(i, range(0, 2))
                if "A" in stages:
                    mix_in(i + 2)
                if "B" in stages:
                    exps(i + 1, 1)
                if "C" in stages:
                    relus(i, range(2, FB))
                if "B" in stages:
                    for o in range(KB):
                        wkv_round(i + 1, o)
                if "A" in stages:
                    mix_round(i + 2)
                if "B" in stages:
                    root(i + 1, 1)
                    feed_copy(i + 1)
                if isinstance(i, int) and i == -2:
                    act.wait_ge(w1_in, 16)
                    nc.scalar.activation(w1_hi[:, :, :], w1_raw, ACT.Copy).then_inc(w1_hi_done, 1)
                    act.wait_ge(w2_in, 16)
                    nc.scalar.activation(w2_hi[:, :, :], w2_raw, ACT.Copy).then_inc(w2_hi_done, 1)

            passes(act, run)

        @block.vector
        def _(dve):
            def norm(c, m):
                step, std_m, parts_m = ln_step[m], std[m], parts[m]
                base = c * LN
                for t in range(CTT):
                    if m == 1:
                        dve.wait_ge(g_added, c * CTT + (t + 1))
                        dve.wait_ge(td_dve, KB)
                    nc.vector.bn_stats(stats[m][:, t, :], tile_of(c, t)).then_inc(step, 1)
                even_mean, even_sq, odd_mean, odd_sq = (stats[m][:, :, n] for n in (1, 2, 4, 5))
                dve.wait_ge(step, base + CTT)
                nc.vector.tensor_tensor(parts_m[:, 0, :], even_mean, odd_mean, ALU.add).then_inc(step, 1)
                nc.vector.tensor_tensor(parts_m[:, 1, :], even_mean, odd_mean, ALU.subtract).then_inc(step, 1)
                nc.vector.tensor_tensor(parts_m[:, 2, :], even_sq, odd_sq, ALU.add).then_inc(step, 1)
                dve.wait_ge(step, base + (CTT + 3))
                nc.vector.tensor_scalar(mean[m][:, :], parts_m[:, 0, :], 0.5, None, ALU.mult).then_inc(step, 1)
                nc.vector.scalar_tensor_tensor(parts_m[:, 1, :], parts_m[:, 1, :], 0.25, parts_m[:, 1, :], ALU.mult, ALU.mult).then_inc(step, 1)
                nc.vector.tensor_scalar(parts_m[:, 2, :], parts_m[:, 2, :], 1.0 / DM, EPS, ALU.mult, ALU.add).then_inc(step, 1)
                dve.wait_ge(step, base + (CTT + 6))
                nc.vector.tensor_tensor(std_m[:, 0, :], parts_m[:, 1, :], parts_m[:, 2, :], ALU.add).then_inc(step, 1)
                dve.wait_ge(step, base + (CTT + 8))
                nc.vector.reciprocal(std_m[:, 2, :], std_m[:, 1, :]).then_inc(step, 1)
                dve.wait_ge(step, base + (CTT + 9))
                nc.vector.tensor_tensor(std_m[:, 2, :], std_m[:, 2, :], std_m[:, 0, :], ALU.mult).then_inc(step, 1)
                dve.wait_ge(step, base + (CTT + 10))
                nc.vector.tensor_tensor(std_m[:, 1, :], std_m[:, 1, :], std_m[:, 2, :], ALU.add).then_inc(step, 1)
                dve.wait_ge(step, base + (CTT + 11))
                nc.vector.reciprocal(std_m[:, 2, :], std_m[:, 1, :]).then_inc(step, 1)
                dve.wait_ge(step, base + (CTT + 12))
                nc.vector.tensor_scalar(std_m[:, 3, :], std_m[:, 2, :], 2.0, None, ALU.mult).then_inc(step, 1)
                dve.wait_ge(step, base + LN)
                if not fresh(c):
                    dve.wait_ge(tp_ready[m], c * KB)
                for t in range(CTT):
                    nc.vector.tensor_scalar(xn[m][:, t, :], tile_of(c, t), mean[m][:, t:t + 1], std_m[:, 3, t:t + 1],
                                            ALU.subtract, ALU.mult).then_inc(xn_done[m], 1)

            def mix(c):
                for k in range(KB):
                    now, before = xnT[:, k, :, 1:NQ + 1], xnT[:, k, :, 0:NQ]
                    dve.wait_ge(tp_read[0], c * KB + (k + 1))
                    nc.vector.tensor_tensor(diff[:, k, :, :], now, before, ALU.subtract).then_inc(diff_done, 1)
                for k in range(KB):
                    before = xnT[:, k, :, 0:NQ]
                    for m in range(3):
                        if m == 0:
                            dve.wait_ge(diff_done, c * KB + (k + 1))
                        if not (fresh(c) and k == 0):
                            dve.wait_ge(mix_lo, c * NM + (3 * k + m - 2))
                        nc.vector.scalar_tensor_tensor(mixed[:, m, :, :], diff[:, k, :, :], channel[:, 2 + m, k:k + 1],
                                                       before, ALU.mult, ALU.add).then_inc(mix_done, 1)

            def recur(c, o):
                base = c * (KB * WS) + o * WS
                vp = rp[1][:, :].rearrange("p (b q) -> p b q", q=NQ)
                flat = lambda ap: ap.rearrange("p b q -> p (b q)")
                decays = flat(tdm[:, o, :, :])
                dve.wait_ge(exps_done, c * KB + (o + 1))
                if fresh(c) and o == 0:
                    dve.wait_ge(td_dve, KB)
                nc.vector.tensor_tensor(ekv[o][:, :, 1:NQ], vp[:, :, 0:NQ - 1], ek[o][:, :, 1:NQ], ALU.mult).then_inc(wkv_step, 1)
                nc.vector.tensor_tensor(prod[:, :], rp[1][:, :], eb[o][:, :], ALU.mult).then_inc(wkv_step, 1)
                nc.vector.tensor_tensor_scan(den[:, :], decays, flat(ek[o][:, :, :]), 0.0, ALU.mult, ALU.add).then_inc(wkv_step, 1)
                dve.wait_ge(wkv_step, base + 1)
                nc.vector.tensor_tensor_scan(num[:, :], decays, flat(ekv[o][:, :, :]), 0.0, ALU.mult, ALU.add).then_inc(wkv_step, 1)
                dve.wait_ge(wkv_step, base + 3)
                nc.vector.tensor_tensor(den[:, :], den[:, :], eb[o][:, :], ALU.add).then_inc(wkv_step, 1)
                dve.wait_ge(wkv_step, base + 4)
                nc.vector.tensor_tensor(num[:, :], num[:, :], prod[:, :], ALU.add).then_inc(wkv_step, 1)
                dve.wait_ge(wkv_step, base + 5)
                nc.vector.scalar_tensor_tensor(er[o][:, :], er[o][:, :], 1.0, den[:, :], ALU.add, ALU.mult).then_inc(wkv_step, 1)
                dve.wait_ge(wkv_step, base + 7)
                nc.vector.reciprocal(er[o][:, :], er[o][:, :]).then_inc(wkv_step, 1)
                dve.wait_ge(wkv_step, base + 8)
                if not fresh(c):
                    dve.wait_ge(wkv_lo_done, c * KB - (KB - 1 - o))
                nc.vector.tensor_tensor(wkv[o][:, :], num[:, :], er[o][:, :], ALU.mult).then_inc(wkv_step, 1)

            def decays_and_biases():
                dve.wait_ge(td_act, 2)
                dve.wait_ge(zeroed, 2 * KB + 3)
                for k in range(KB):
                    nc.vector.tensor_scalar(tdm[:, k, :, :], tdm[:, k, :, :], td[:, 1, k:k + 1], None, ALU.mult).then_inc(td_dve, 1)
                low = slice(BR - 1, BR)
                dve.wait_ge(b_in, 4 * 16)
                nc.vector.tensor_copy(bias[:, :, :], bias_raw[:, :, :]).then_inc(bias_done, 1)
                dve.wait_ge(bias_done, 1)
                nc.vector.tensor_tensor(bias[low], bias_raw[low], bits(bias[low]), ALU.subtract).then_inc(bias_done, 1)

            def add_out(c, ready, added, t):
                dve.wait_ge(ready, c * CTT + (t + 1))
                nc.vector.tensor_tensor(tile_of(c, t), yp[t % 2][:, 0:DM], tile_of(c, t), ALU.add).then_inc(added, 1)

            def run(i, stages):
                if "A" in stages:
                    norm(i + 2, 0)
                if isinstance(i, int) and i == -2:
                    decays_and_biases()
                if "B" in stages:
                    for o in range(KB):
                        recur(i + 1, o)
                if "A" in stages:
                    mix(i + 2)
                if "C" in stages:
                    for t in range(2):
                        add_out(i, y_ready, y_added, t)
                if "B" in stages:
                    for t in range(CTT):
                        add_out(i + 1, g_ready, g_added, t)
                    norm(i + 1, 1)
                if "C" in stages:
                    for t in range(2, CTT):
                        add_out(i, y_ready, y_added, t)

            passes(dve, run)

        @block.tensor
        def _(pe):
            pe.wait_ge(ident_done, 2)

            def transposes(c, m, before):
                pe.wait_ge(xn_done[m], (c + 1) * CTT)
                for k in range(KB):
                    if k > 0:
                        pe.wait_ge(tp_read[m], c * KB + k)
                    elif before is not None:
                        pe.wait_ge(*before)
                    for t in range(CTT):
                        last = nc.tensor.transpose(tp[:, t * P:(t + 1) * P], xn[m][:, t, k * P:(k + 1) * P], ident[:, :])
                    last.then_inc(tp_ready[m], 1)

            def split_terms(w_hi, w_lo, a_hi, a_lo):
                return ((w_hi, a_hi), (w_lo, a_hi), (w_hi, a_lo))

            def mixing(c, o):
                if o == 0:
                    pe.wait_ge(mix_lo, (c + 1) * NM)
                if fresh(c) and o == 0:
                    pe.wait_ge(sq_lo_done, 1)
                if not (fresh(c) and o == 0):
                    pe.wait_ge(exps_done, c * KB + o)
                    pe.wait_ge(wkv_step, c * (KB * WS) + (o * WS - WS + 2))
                cols = slice(o * P, (o + 1) * P)
                for m in range(3):
                    terms = [t for k in range(KB) for t in split_terms(sqT_hi[:, m, k, cols], sqT_lo[:, m, k, cols],
                                                                      mixed_hi[:, m, k, :], mixed_lo[:, m, k, :])]
                    for n, (w, a) in enumerate(terms):
                        last = nc.tensor.matmul(rp[m][:, :], w, a, start=n == 0, stop=n == len(terms) - 1)
                    last.then_inc(r_ready, 1)

            def out_tile(t, which, blocks, a_hi, a_lo, w_hi, w_lo, ready):
                tok = slice(t * P, (t + 1) * P)
                terms = [(ones[:, :], bias[:, which, :])]
                terms += [x for k in range(blocks) for x in ((a_hi[:, k, tok], w_hi[:, k, :]), (a_hi[:, k, tok], w_lo[:, k, :]),
                                                             (a_lo[:, k, tok], w_hi[:, k, :]))]
                for n, (a, w) in enumerate(terms):
                    last = nc.tensor.matmul(yp[t % 2][:, 0:DM], a, w, start=n == 0, stop=n == len(terms) - 1)
                last.then_inc(ready, 1)

            def mixed_out(c, with_c):
                pe.wait_ge(wkv_lo_done, (c + 1) * KB)
                if fresh(c):
                    pe.wait_ge(ones_done, 1)
                    pe.wait_ge(bias_done, 2)
                for t in range(CTT):
                    if t >= 2:
                        pe.wait_ge(g_added, c * CTT + (t - 1))
                    elif with_c:
                        pe.wait_ge(y_added, (c - 1) * CTT + (t + 1))
                    out_tile(t, 0, KB, wkv_hi, wkv_lo, sqT_hi[:, 3], sqT_lo[:, 3], g_ready)

            def feed_in(c, blocks):
                for f in blocks:
                    if f == 0:
                        pe.wait_ge(zT_lo_done, (c + 1) * KB)
                        if fresh(c):
                            pe.wait_ge(w1_lo_done, 1)
                    if not (fresh(c) and f < 2):
                        pe.wait_ge(hid_done, c * FB + (f - 1))
                    cols = slice(f * P, (f + 1) * P)
                    terms = [t for k in range(KB) for t in split_terms(w1_hi[:, k, cols], w1_lo[:, k, cols],
                                                                      zT_hi[:, k, :], zT_lo[:, k, :])]
                    for n, (w, a) in enumerate(terms):
                        last = nc.tensor.matmul(fp[f % 2][:, :], w, a, start=n == 0, stop=n == len(terms) - 1)
                    last.then_inc(f_ready, 1)

            def feed_out(c, tiles, with_b):
                for t in tiles:
                    if t == 0:
                        pe.wait_ge(hid_lo_done, (c + 1) * FB)
                        if fresh(c):
                            pe.wait_ge(w2_lo_done, 1)
                    if t < 2 and fresh(c):
                        pe.wait_ge(g_added, CTT - 1 + t)
                    elif t < 2:
                        pe.wait_ge(y_added, c * CTT + (t - 1))
                    elif with_b:
                        pe.wait_ge(g_added, (c + 1) * CTT + (t + 1))
                    else:
                        pe.wait_ge(y_added, c * CTT + (t - 1))
                    out_tile(t, 1, FB, hid_hi, hid_lo, w2_hi, w2_lo, y_ready)

            def run(i, stages):
                a, b, c = ("A" in stages), ("B" in stages), ("C" in stages)
                if b:
                    mixing(i + 1, 0)
                if c:
                    feed_in(i, range(0, 2))
                if a:
                    before = (tp_read[1], (i + 1) * KB) if c else (tp_read[0], (i + 2) * KB) if b else None
                    transposes(i + 2, 0, before)
                if b:
                    mixing(i + 1, 1)
                if c:
                    feed_in(i, range(2, FB))
                    feed_out(i, range(0, 2), b)
                if b:
                    mixed_out(i + 1, c)
                if c:
                    feed_out(i, range(2, CTT), b)
                if b:
                    transposes(i + 1, 1, (tp_read[0], (i + 3 if a else i + 2) * KB))

            passes(pe, run)


def kernel(x, ctx_768, L0_xattn_w_q, L0_xattn_w_kv, L0_xattn_w_out, L0_xattn_b_out, L0_attn_time_decay,
           L0_attn_time_first, L0_attn_time_mix_key, L0_attn_time_mix_value, L0_attn_time_mix_receptance,
           L0_attn_Wk, L0_attn_Wv, L0_attn_Wr, L0_attn_Wo, L0_attn_bo, L0_ffn_w1, L0_ffn_b1, L0_ffn_w2, L0_ffn_b2):
    import concourse.bacc as bacc
    from concourse.bass_utils import run_bass_kernel_spmd

    nc = bacc.Bacc("TRN2", target_bir_lowering=False, num_devices=1)
    columns = lambda vectors: np.stack([np.asarray(v).reshape(-1, P) for v in vectors]).transpose(2, 0, 1)
    data = {
        "x": x, "ctx": ctx_768, "ctxT": np.asarray(ctx_768).transpose(0, 2, 1), "w_q": L0_xattn_w_q, "w_kv": L0_xattn_w_kv, "w_out": L0_xattn_w_out, "b_out": L0_xattn_b_out,
        "channels": columns([L0_attn_time_decay, L0_attn_time_first, L0_attn_time_mix_key, L0_attn_time_mix_value,
                             L0_attn_time_mix_receptance]),
        "squares": np.stack([np.asarray(w).T for w in (L0_attn_Wk, L0_attn_Wv, L0_attn_Wr, L0_attn_Wo)]),
        "bo": L0_attn_bo, "w1": L0_ffn_w1, "b1": np.asarray(L0_ffn_b1).reshape(-1, P).T, "w2": L0_ffn_w2, "b2": L0_ffn_b2,
    }
    data = {name: np.ascontiguousarray(a) for name, a in data.items()}
    t = {name: nc.dram_tensor(f"in_{name}", a.shape, F32, kind="ExternalInput").ap() for name, a in data.items()}
    out = nc.dram_tensor("out_x", (NB, NQ, DM), F32, kind="ExternalOutput").ap()
    qk_dram = nc.dram_tensor("qk_scratch", (NB, DC, HQ), F32).ap()
    o_dram = nc.dram_tensor("o_scratch", (NB, DC, HQ), F32).ap()
    perceiver_layer(nc, t, qk_dram, o_dram, out)
    result = run_bass_kernel_spmd(nc, [{f"in_{name}": a for name, a in data.items()}], core_ids=[0])
    return result.results[0]["out_x"]


def perceiver_layer(nc, t, qk_dram, o_dram, out):
    project_queries(nc, t["x"], t["w_q"], t["w_kv"], qk_dram)
    attend(nc, t["ctx"], t["ctxT"], qk_dram, o_dram)
    with nc.sbuf_tensor("resid", [P, TT, DM], F32) as resid:
        attention_output(nc, t["w_kv"], t["w_out"], t["b_out"], t["x"], o_dram, resid)
        mix_and_feed(nc, t["channels"], t["squares"], t["bo"], t["w1"], t["b1"], t["w2"], t["b2"], resid, out)
```

```python
import numpy as np
import concourse.bass as bass
from concourse import mybir
from contextlib import ExitStack

F32 = mybir.dt.float32
F32R = mybir.dt.float32r
ALU = mybir.AluOpType
ACT = mybir.ActivationFunctionType
AX = mybir.AxisListType

P = 128
NB, NQ, DM = 32, 64, 256
NKV, DC = 1601, 192
NH, DH = 16, 64
INNER = NH * DH
HQ = NH * NQ
TOK = NB * NQ
TT = TOK // P
DCB = DC - P
SCALE = DH ** -0.5
EPS = 1e-5


def bits(ap):
    return ap.bitcast(F32)


def identity(nc, pool, ident, ident_done):
    nc.gpsimd.memset(ident[:, :], 0.0).then_inc(ident_done, 1)
    pool.wait_ge(ident_done, 1)
    nc.gpsimd.affine_select(out=ident[:, :], in_=ident[:, :], compare_op=ALU.not_equal, fill=1.0,
                            base=0, pattern=[[-1, P]], channel_multiplier=1).then_inc(ident_done, 1)


def project_queries(nc, x, w_q, wkT, qk_dram):
    KB = DM // P
    NC, CT = 4, TOK // 4
    CB = CT // NQ
    HP = NH // 2
    NSTG = 4
    PPB = HP // NSTG
    with ExitStack() as ctx:
        sb = lambda name, shape, dt=F32: ctx.enter_context(nc.sbuf_tensor("p1_" + name, shape, dt))
        pb = lambda name, shape: ctx.enter_context(nc.psum_tensor("p1_" + name, shape, F32))
        sem = lambda name: ctx.enter_context(nc.semaphore("p1_" + name))

        xt = sb("x", [P, TT, DM])
        stats = sb("stats", [P, TT, 6])
        mv = sb("mv", [P, TT, 2])
        std = sb("std", [P, 4, TT])
        wq = sb("wq", [P, KB, INNER])
        wq_hi, wq_lo = sb("wq_hi", [P, KB, INNER], F32R), sb("wq_lo", [P, KB, INNER], F32R)
        wks = sb("wks", [P, NH, DC])
        wks_hi, wks_lo = sb("wks_hi", [P, NH, DC], F32R), sb("wks_lo", [P, NH, DC], F32R)
        xT_hi, xT_lo = sb("xT_hi", [P, KB, TOK], F32R), sb("xT_lo", [P, KB, TOK], F32R)
        stack = sb("stack", [P, 2, 2, CT], F32R)
        staged = [(sb(f"out_a{i}", [P, CB, PPB * 2, NQ]), sb(f"out_b{i}", [DCB, CB, PPB * 2, NQ])) for i in range(NSTG)]
        ident = sb("ident", [P, P])

        tp = [pb(f"tp{i}", [P, 512]) for i in range(2)]
        qp = [pb(f"qp{i}", [P, 512]) for i in range(2)]
        ap = [pb(f"ap{i}", [P, 512]) for i in range(2)]
        bp = [pb(f"bp{i}", [DCB, 512]) for i in range(2)]

        x_in, wq_in, wk_in = sem("x_in"), sem("wq_in"), sem("wk_in")
        ident_done, wq_hi_done, wq_lo_done = sem("ident"), sem("wqh"), sem("wql")
        wk_hi_done, wk_lo_done = sem("wkh"), sem("wkl")
        stat_done, std_done, xn_done = sem("stat"), sem("std"), sem("xn")
        tp_ready, tp_hi, tp_lo = sem("tp_ready"), sem("tp_hi"), sem("tp_lo")
        q_ready, stack_hi, stack_lo = sem("q_ready"), sem("stack_hi"), sem("stack_lo")
        qk_ready, evac_act, evac_dve = sem("qk_ready"), sem("evac_act"), sem("evac_dve")
        stored = [sem(f"stored{i}") for i in range(NSTG)]
        block = ctx.enter_context(nc.Block())

        NT = NC * KB
        AHEAD = KB

        @block.sync
        def _(sp):
            sp.dma_start(xt[:, :, :], x.rearrange("(t b) q d -> (b q) t d", b=P // NQ)).then_inc(x_in, 16)
            sp.dma_start(wq[:, :, :], w_q.rearrange("(k p) n -> p k n", p=P)).then_inc(wq_in, 16)
            for r in range(2):
                sp.dma_start(wks[r * DH:(r + 1) * DH, :, :], wkT.rearrange("(h d) c -> d h c", d=DH)).then_inc(wk_in, 16)
            with sp.Fori(0, NC) as c:
                for i in range(NSTG):
                    sp.wait_ge(evac_act, c * (2 * HP) + (i + 1) * 2 * PPB)
                    sp.wait_ge(evac_dve, c * (2 * HP) + (i + 1) * 2 * PPB)
                    cols = slice(i * PPB * 2 * NQ, (i + 1) * PPB * 2 * NQ)
                    for buf, rows in zip(staged[i], (slice(0, P), slice(P, DC))):
                        dst = qk_dram[bass.ds(c * CB, CB), rows, cols].rearrange("b c n -> c b n")
                        sp.dma_start(dst, buf[:, :, :, :].rearrange("p b h q -> p b (h q)")).then_inc(stored[i], 16)
            for s in stored:
                sp.wait_ge(s, 32 * NC)

        @block.gpsimd
        def _(pool):
            identity(nc, pool, ident, ident_done)
            pool.wait_ge(wq_hi_done, 1)
            nc.gpsimd.tensor_tensor(wq_lo[:, :, :], wq[:, :, :], bits(wq_hi[:, :, :]), ALU.subtract).then_inc(wq_lo_done, 1)
            pool.wait_ge(wk_hi_done, 1)
            nc.gpsimd.tensor_tensor(wks_lo[:, :, :], wks[:, :, :], bits(wks_hi[:, :, :]), ALU.subtract).then_inc(wk_lo_done, 1)

        def evacuate(eng, scalar, c, j, first):
            i, jj = divmod(j, PPB)
            buf_a, buf_b = staged[i]
            for r in range(2):
                eng.wait_ge(qk_ready, c * NH + (2 * j + r + 1))
                if not first and jj == 0 and r == 0:
                    eng.wait_ge(stored[i], c * 32)
                block_a = (r == 0) == scalar
                dst = (buf_a if block_a else buf_b)[:, :, 2 * jj + r, :]
                src = (ap if block_a else bp)[r][:, :].rearrange("p (b q) -> p b q", q=NQ)
                if scalar:
                    nc.scalar.activation(dst, src, ACT.Copy).then_inc(evac_act, 1)
                else:
                    nc.vector.tensor_copy(dst, src).then_inc(evac_dve, 1)

        @block.scalar
        def _(act):
            act.wait_ge(wq_in, 16)
            nc.scalar.activation(wq_hi[:, :, :], wq[:, :, :], ACT.Copy).then_inc(wq_hi_done, 1)
            act.wait_ge(stat_done, TT + TT + 1)
            nc.scalar.activation(std[:, 1, :], std[:, 0, :], ACT.Sqrt).then_inc(std_done, 1)
            act.wait_ge(wk_in, 32)
            nc.scalar.activation(wks_hi[:, :, :], wks[:, :, :], ACT.Copy).then_inc(wk_hi_done, 1)

            def x_hi(n):
                c, k = divmod(n, KB)
                act.wait_ge(tp_ready, n + 1)
                nc.scalar.activation(xT_hi[:, k, c * CT:(c + 1) * CT], tp[n % 2][:, :], ACT.Copy).then_inc(tp_hi, 1)

            def chunk(c, first):
                for j in range(HP):
                    act.wait_ge(q_ready, c * HP + (j + 1))
                    if not first or j >= 2:
                        act.wait_ge(qk_ready, c * NH + 2 * (j - 1))
                    s = stack[:, j % 2]
                    nc.scalar.activation(s[0:DH, 0, :], qp[j % 2][0:DH, :], ACT.Copy, scale=SCALE)
                    nc.scalar.activation(s[DH:P, 1, :], qp[j % 2][DH:P, :], ACT.Copy, scale=SCALE).then_inc(stack_hi, 1)
                    if j >= 1:
                        evacuate(act, True, c, j - 1, first)
                    elif not first:
                        evacuate(act, True, c - 1, HP - 1, False)
                    if first and j + AHEAD < NT:
                        x_hi(j + AHEAD)

            for n in range(AHEAD):
                x_hi(n)
            chunk(0, True)
            with act.Fori(1, NC) as c:
                chunk(c, False)
            evacuate(act, True, NC - 1, HP - 1, False)

        @block.vector
        def _(dve):
            dve.wait_ge(x_in, 16)
            for t in range(TT):
                nc.vector.bn_stats(stats[:, t, :], xt[:, t, :]).then_inc(stat_done, 1)
            for t in range(TT):
                dve.wait_ge(stat_done, t + 1)
                nc.vector.bn_aggr(mv[:, t, :], stats[:, t, :]).then_inc(stat_done, 1)
            dve.wait_ge(stat_done, 2 * TT)
            nc.vector.tensor_scalar(std[:, 0, :], mv[:, :, 1], EPS, None, ALU.add).then_inc(stat_done, 1)
            dve.wait_ge(std_done, 1)
            newton_rstd(nc, dve, std, std_done)
            for t in range(TT):
                nc.vector.tensor_scalar(xt[:, t, :], xt[:, t, :], mv[:, t, 0:1], std[:, 3, t:t + 1],
                                        ALU.subtract, ALU.mult).then_inc(xn_done, 1)

            def x_lo(n):
                c, k = divmod(n, KB)
                cols = slice(c * CT, (c + 1) * CT)
                dve.wait_ge(tp_hi, n + 1)
                nc.vector.tensor_tensor(xT_lo[:, k, cols], tp[n % 2][:, :], bits(xT_hi[:, k, cols]), ALU.subtract).then_inc(tp_lo, 1)

            def chunk(c, first):
                for j in range(HP):
                    dve.wait_ge(stack_hi, c * HP + (j + 1))
                    s, q = stack[:, j % 2], qp[j % 2]
                    nc.vector.scalar_tensor_tensor(s[DH:P, 0, :], q[0:DH, :], SCALE, bits(s[0:DH, 0, :]), ALU.mult, ALU.subtract)
                    nc.vector.scalar_tensor_tensor(s[0:DH, 1, :], q[DH:P, :], SCALE, bits(s[DH:P, 1, :]), ALU.mult,
                                                   ALU.subtract).then_inc(stack_lo, 1)
                    if j >= 1:
                        evacuate(dve, False, c, j - 1, first)
                    elif not first:
                        evacuate(dve, False, c - 1, HP - 1, False)
                    if first and j + AHEAD < NT:
                        x_lo(j + AHEAD)

            for n in range(AHEAD):
                x_lo(n)
            chunk(0, True)
            with dve.Fori(1, NC) as c:
                chunk(c, False)
            evacuate(dve, False, NC - 1, HP - 1, False)

        @block.tensor
        def _(pe):
            pe.wait_ge(ident_done, 2)

            def transposes(n):
                c, k = divmod(n, KB)
                per = CT // P
                if n >= 2:
                    pe.wait_ge(tp_lo, n - 1)
                pe.wait_ge(xn_done, (c + 1) * per)
                for i in range(per):
                    last = nc.tensor.transpose(tp[n % 2][:, i * P:(i + 1) * P],
                                               xt[:, c * per + i, k * P:(k + 1) * P], ident[:, :])
                last.then_inc(tp_ready, 1)

            def q_pair(c, j, first):
                if first and j == 0:
                    pe.wait_ge(wq_lo_done, 1)
                    pe.wait_ge(tp_lo, AHEAD)
                if not first and isinstance(c, int) and c == 1 and j == 0:
                    pe.wait_ge(tp_lo, NT)
                if not first or j >= 2:
                    pe.wait_ge(stack_lo, c * HP + (j - 1))
                terms = [(wh, xh, k) for k in range(KB) for wh, xh in ((wq_hi, xT_hi), (wq_lo, xT_hi), (wq_hi, xT_lo))]
                for n, (w, xv, k) in enumerate(terms):
                    last = nc.tensor.matmul(qp[j % 2][:, :], w[:, k, j * P:(j + 1) * P], xv[:, k, bass.ds(c * CT, CT)],
                                            start=n == 0, stop=n == len(terms) - 1)
                last.then_inc(q_ready, 1)

            def qk_pair(c, j, first):
                pe.wait_ge(stack_lo, c * HP + (j + 1))
                if first and j == 0:
                    pe.wait_ge(wk_lo_done, 1)
                for r in range(2):
                    s = stack[:, j % 2, r, :]
                    if not first or j >= 1:
                        pe.wait_ge(evac_act, c * NH + (2 * (j - 1) + r + 1))
                        pe.wait_ge(evac_dve, c * NH + (2 * (j - 1) + r + 1))
                    h = 2 * j + r
                    for n, w in enumerate((wks_hi, wks_lo)):
                        nc.tensor.matmul(ap[r][:, :], w[:, h, 0:P], s, start=n == 0, stop=n == 1)
                    for n, w in enumerate((wks_hi, wks_lo)):
                        last = nc.tensor.matmul(bp[r][:, :], w[:, h, P:DC], s, start=n == 0, stop=n == 1)
                    last.then_inc(qk_ready, 1)

            def chunk(c, first, last):
                for j in range(HP):
                    if first and j + AHEAD < NT:
                        transposes(j + AHEAD)
                    if j + 1 < HP:
                        q_pair(c, j + 1, first)
                    elif not last:
                        q_pair(c + 1, 0, False)
                    qk_pair(c, j, first)

            for n in range(AHEAD):
                transposes(n)
            q_pair(0, 0, True)
            chunk(0, True, False)
            with pe.Fori(1, NC - 1) as c:
                chunk(c, False, False)
            chunk(NC - 1, False, True)


def newton_rstd(nc, dve, std, std_done):
    nc.vector.reciprocal(std[:, 2, :], std[:, 1, :]).then_inc(std_done, 1)
    dve.wait_ge(std_done, 2)
    nc.vector.tensor_tensor(std[:, 2, :], std[:, 2, :], std[:, 0, :], ALU.mult).then_inc(std_done, 1)
    dve.wait_ge(std_done, 3)
    nc.vector.tensor_tensor(std[:, 1, :], std[:, 1, :], std[:, 2, :], ALU.add).then_inc(std_done, 1)
    dve.wait_ge(std_done, 4)
    nc.vector.reciprocal(std[:, 2, :], std[:, 1, :]).then_inc(std_done, 1)
    dve.wait_ge(std_done, 5)
    nc.vector.tensor_scalar(std[:, 3, :], std[:, 2, :], 2.0, None, ALU.mult).then_inc(std_done, 1)
    dve.wait_ge(std_done, 6)


def attend(nc, ctx_in, ctxT_in, qk_dram, o_dram):
    KT = -(-NKV // P)
    FULL = KT - 1
    TAIL = NKV - FULL * P
    SB = HQ // P
    STEPS = SB * NB
    QC = 2 * P
    QB = SB // 2
    TG = [range(0, 4), range(4, 8), range(8, 12), range(12, KT)]
    NG = len(TG)
    CW = NKV + NKV % 2
    EDGE = (CW - 2 * 512) // 4 * 2
    CHUNKS = [(0, EDGE), (EDGE, EDGE + 512), (EDGE + 512, EDGE + 1024), (EDGE + 1024, CW)]
    S0 = 512 - EDGE
    FIRST_PART = 7
    SPB = 2
    with ExitStack() as ctx:
        sb = lambda name, shape, dt=F32: ctx.enter_context(nc.sbuf_tensor("p2_" + name, shape, dt))
        pb = lambda name, shape: ctx.enter_context(nc.psum_tensor("p2_" + name, shape, F32))
        sem = lambda name: ctx.enter_context(nc.semaphore("p2_" + name))

        raw = sb("raw", [P, KT, DC])
        nat = [sb(f"nat{i}", [P, KT, 2 * DC], F32R) for i in range(2)]
        ct_raw = sb("ct_raw", [P, CW])
        ct_hi = [sb(f"ct_hi{i}", [P, 2, CW], F32R) for i in range(2)]
        ct_lo = [sb(f"ct_lo{i}", [P, CW], F32R) for i in range(2)]
        qraw = sb("qraw", [P, 2, HQ])
        q_hi = [sb(f"q_hi{i}", [P, 2, HQ], F32R) for i in range(2)]
        q_lo = [sb(f"q_lo{i}", [P, 2, HQ], F32R) for i in range(2)]
        prob = [sb(f"prob{i}", [P, CW]) for i in range(2)]
        pt_hi = [sb(f"pt_hi{i}", [P, KT, QC], F32R) for i in range(2)]
        pt_lo = [sb(f"pt_lo{i}", [P, KT, QC], F32R) for i in range(2)]
        o_a = [sb(f"o_a{i}", [P, QC]) for i in range(2)]
        o_b = [sb(f"o_b{i}", [P, QC]) for i in range(2)]
        first_b = prob[1]
        negmax, rowsum, rinv = sb("negmax", [P, 2]), sb("rowsum", [P, 2]), sb("rinv", [P, 2])
        ident, zero = sb("ident", [P, P]), sb("zero", [P, 1])

        scores = pb("scores", [P, 2048])
        work = [pb(f"work{i}", [P, 512]) for i in range(3)]
        acc = pb("acc", [P, 2, QC])
        WORK_OF = (0, 1, 2, 0)

        raw_in, qk_in = sem("raw_in"), sem("qk_in")
        ct_a_in, ct_b_in = sem("ct_a_in"), sem("ct_b_in")
        zero_done = sem("zero_done")
        ident_done, raw_pad, prob_pad = sem("ident"), sem("raw_pad"), sem("prob_pad")
        nat_hi_done, nat_done = sem("nat_hi_done"), sem("nat_done")
        q_hi_done, q_done = sem("q_hi_done"), sem("q_done")
        ct_a_hi_done, ct_a_done = sem("ct_a_hi_done"), sem("ct_a_done")
        ct_b_hi_done, ct_b_done = sem("ct_b_hi_done"), sem("ct_b_done")
        scores_ready, max_done, exp_done = sem("scores_ready"), sem("max_done"), sem("exp_done")
        rinv_done, prob_done = sem("rinv_done"), sem("prob_done")
        pt_ready, pt_hi_done, pt_lo_done = sem("pt_ready"), sem("pt_hi_done"), sem("pt_lo_done")
        acc_ready, acc_act, acc_dve = sem("acc_ready"), sem("acc_act"), sem("acc_dve")
        stored = [sem("stored0"), sem("stored1")]
        block = ctx.enter_context(nc.Block())

        SPP, QPP = SPB * SB, SPB * QB

        def passes(eng, body):
            body(0, True, False)
            with eng.Fori(1, NB // SPB - 1) as r:
                body(r, False, False)
            body(NB // SPB - 1, False, True)

        @block.sync
        def _(sp):
            def load_raw(n):
                src = ctx_in[bass.ds(n, 1), :, :].rearrange("a k c -> (a k) c")
                sp.dma_start(raw[:, 0:FULL, :], src[0:FULL * P, :].rearrange("(t p) c -> p t c", p=P)).then_inc(raw_in, 16)
                sp.dma_start(raw[0:TAIL, FULL, :], src[FULL * P:NKV, :]).then_inc(raw_in, 16)

            def load_ct_a(n):
                src = ctxT_in[bass.ds(n, 1), :, :].rearrange("a c k -> (a c) k")
                sp.dma_start(ct_raw[:, 0:NKV], src[0:P, :]).then_inc(ct_a_in, 16)

            def load_ct_b(n, dst=ct_raw):
                src = ctxT_in[bass.ds(n, 1), :, :].rearrange("a c k -> (a c) k")
                sp.dma_start(dst[0:DCB, 0:NKV], src[P:DC, :]).then_inc(ct_b_in, 16)
                sp.dma_start(dst[DCB:P, 0:NKV], src[P:DC, :]).then_inc(ct_b_in, 16)

            def load_qk(n):
                src = qk_dram[bass.ds(n, 1), :, :].rearrange("a c n -> (a c) n")
                sp.dma_start(qraw[:, 0, :], src[0:P, :]).then_inc(qk_in, 16)
                sp.dma_start(qraw[0:DCB, 1, :], src[P:DC, :]).then_inc(qk_in, 16)
                sp.dma_start(qraw[DCB:P, 1, :], src[P:DC, :]).then_inc(qk_in, 16)

            def store(i, b, quarter, parity):
                sp.wait_ge(acc_act, i + 1)
                sp.wait_ge(acc_dve, i + 1)
                dst = o_dram[bass.ds(b, 1), :, quarter * QC:(quarter + 1) * QC].rearrange("a c n -> (a c) n")
                sp.dma_start(dst[0:P, :], o_a[parity][:, :]).then_inc(stored[parity], 16)
                sp.dma_start(dst[P:DC, :], o_b[parity][0:DCB, :]).then_inc(stored[parity], 16)

            def body(r, first, last):
                for u in range(SPB):
                    b = r * SPB + u
                    i = r * QPP + u * QB
                    final = last and u == SPB - 1
                    if not (first and u == 0):
                        store(i - 2, b - 1, QB - 2, 0)
                    if not final:
                        sp.wait_ge(ct_a_done, b + 2)
                        load_ct_b(b + 1)
                    if not last:
                        sp.wait_ge(q_done, b + 2)
                        load_qk(b + 2)
                    if not (first and u == 0):
                        store(i - 1, b - 1, QB - 1, 1)
                    if not last:
                        sp.wait_ge(ct_b_done, b + 2)
                        load_ct_a(b + 2)
                    store(i, b, 0, 0)
                    if not last:
                        sp.wait_ge(nat_done, b + 2)
                        load_raw(b + 2)
                    store(i + 1, b, 1, 1)

            sp.wait_ge(raw_pad, 3)
            load_ct_a(0)
            load_qk(0)
            load_ct_b(0, first_b)
            load_raw(0)
            sp.wait_ge(ct_a_done, 1)
            load_ct_a(1)
            sp.wait_ge(q_done, 1)
            load_qk(1)
            sp.wait_ge(nat_done, 1)
            load_raw(1)
            passes(sp, body)
            store(NB * QB - 2, NB - 1, QB - 2, 0)
            store(NB * QB - 1, NB - 1, QB - 1, 1)
            for s in stored:
                sp.wait_ge(s, 32 * NB * QB // 2)

        @block.gpsimd
        def _(pool):
            nc.gpsimd.memset(raw[:, FULL, :], 0.0).then_inc(raw_pad, 1)
            nc.gpsimd.memset(ct_raw[:, NKV:CW], 0.0).then_inc(raw_pad, 1)
            nc.gpsimd.memset(first_b[:, NKV:CW], 0.0).then_inc(raw_pad, 1)
            for i in range(2):
                nc.gpsimd.memset(bits(pt_hi[i][:, FULL, :]), 0.0).then_inc(prob_pad, 1)
                nc.gpsimd.memset(bits(pt_lo[i][:, FULL, :]), 0.0).then_inc(prob_pad, 1)
            nc.gpsimd.memset(zero[:, :], 0.0).then_inc(zero_done, 1)
            pool.wait_ge(zero_done, 1)
            identity(nc, pool, ident, ident_done)

            def round_to(dst, src):
                flat = (zero[:, :] if len(src.shape) == 2 else zero[:, :].unsqueeze(1)).broadcast_to(src.shape)
                return nc.gpsimd.tensor_tensor(dst, src, flat, ALU.add)

            def prepare(n, par, fresh):
                pool.wait_ge(ct_a_in, (n + 1) * 16)
                if not fresh:
                    pool.wait_ge(scores_ready, (n - 1) * SB)
                round_to(ct_hi[par][:, 0, :], ct_raw[:, :]).then_inc(ct_a_hi_done, 1)
                pool.wait_ge(ct_a_hi_done, n + 1)
                nc.gpsimd.tensor_tensor(ct_lo[par][:, :], ct_raw[:, :], bits(ct_hi[par][:, 0, :]),
                                        ALU.subtract).then_inc(ct_a_done, 1)
                pool.wait_ge(qk_in, (n + 1) * 48)
                round_to(q_hi[par][:, :, :], qraw[:, :, :]).then_inc(q_hi_done, 1)
                pool.wait_ge(q_hi_done, n + 1)
                nc.gpsimd.tensor_tensor(q_lo[par][:, :, :], qraw[:, :, :], bits(q_hi[par][:, :, :]),
                                        ALU.subtract).then_inc(q_done, 1)
                lower = slice(DCB, P)
                pool.wait_ge(ct_b_in, (n + 1) * 32)
                round_to(ct_hi[par][:, 1, :], ct_raw[:, :]).then_inc(ct_b_hi_done, 1)
                pool.wait_ge(ct_b_hi_done, n + 1)
                nc.gpsimd.tensor_tensor(ct_hi[par][lower, 1, :], ct_raw[lower, :], bits(ct_hi[par][lower, 1, :]),
                                        ALU.subtract).then_inc(ct_b_done, 1)
                x = nat[par]
                pool.wait_ge(ct_b_done, n + 1)
                pool.wait_ge(raw_in, (n + 1) * 32)
                if not fresh:
                    pool.wait_ge(acc_ready, (n - 1) * QB)
                round_to(x[:, :, 0:DC], raw[:, :, :]).then_inc(nat_hi_done, 1)
                pool.wait_ge(nat_hi_done, n + 1)
                nc.gpsimd.tensor_tensor(x[:, :, DC:DC + DCB], raw[:, :, P:DC], bits(x[:, :, P:DC]), ALU.subtract)
                nc.gpsimd.tensor_tensor(x[:, :, DC + DCB:2 * DC], raw[:, :, 0:P], bits(x[:, :, 0:P]),
                                        ALU.subtract).then_inc(nat_done, 1)

            def body(r, first, last):
                for u in range(SPB):
                    if not (last and u == SPB - 1):
                        prepare(r * SPB + (u + 1), (u + 1) % 2, first and u == 0)

            passes(pool, body)

        def transposed(buf, slot, g, half):
            tiles, rows = TG[g], slice(0, TAIL if g == NG - 1 else P)
            src = work[WORK_OF[g]][rows, 0:len(tiles) * P].rearrange("p (t n) -> p t n", n=P)
            return src, buf[slot][rows, tiles[0]:tiles[-1] + 1, half * P:(half + 1) * P]

        @block.scalar
        def _(act):
            def pt_copy(s, g, slot, half):
                act.wait_ge(pt_ready, s * NG + (g + 1))
                src, dst = transposed(pt_hi, slot, g, half)
                nc.scalar.activation(dst, src, ACT.Copy).then_inc(pt_hi_done, 1)

            def acc_copy(i, parity, fresh):
                if not fresh:
                    act.wait_ge(stored[parity], (i - parity) * 16)
                act.wait_ge(acc_ready, i + 1)
                nc.scalar.activation(o_a[parity][:, :], acc[:, 0, :], ACT.Copy)
                nc.scalar.activation(o_b[parity][DCB:P, :], acc[DCB:P, 1, :], ACT.Copy).then_inc(acc_act, 1)

            def step(r, j, first):
                s = r * SPP + j
                prev = not (first and j == 0)
                if prev:
                    slot, half = ((j - 1) // 2) % 2, (j - 1) % 2
                    if first and j == 1:
                        act.wait_ge(prob_pad, 4)
                    if not (first and j < 5):
                        act.wait_ge(acc_ready, r * QPP + ((j - 1) // 2 - 1))
                    pt_copy(s - 1, 0, slot, half)
                    pt_copy(s - 1, 1, slot, half)
                act.wait_ge(max_done, s + 1)
                nc.scalar.activation(prob[j % 2][:, 0:NKV], scores[:, S0:S0 + NKV], ACT.Exp, bias=negmax[:, j % 2:j % 2 + 1],
                                     accum_out=rowsum[:, j % 2:j % 2 + 1]).then_inc(exp_done, 1)
                if prev:
                    pt_copy(s - 1, 2, slot, half)
                act.wait_ge(rinv_done, s + 1)
                nc.scalar.activation(prob[j % 2][:, 0:NKV], prob[j % 2][:, 0:NKV], ACT.Copy,
                                     scale=rinv[:, j % 2:j % 2 + 1]).then_inc(prob_done, 1)
                if prev:
                    pt_copy(s - 1, 3, slot, half)
                if j % 2 == 0 and not (first and j < 4):
                    acc_copy(r * QPP + (j // 2 - 2), (j // 2) % 2, first and j < 8)

            def body(r, first, last):
                for j in range(SPP):
                    step(r, j, first)

            act.wait_ge(ct_a_in, 16)
            nc.scalar.activation(ct_hi[0][:, 0, :], ct_raw[:, :], ACT.Copy).then_inc(ct_a_hi_done, 1)
            act.wait_ge(qk_in, 48)
            nc.scalar.activation(q_hi[0][:, :, :], qraw[:, :, :], ACT.Copy).then_inc(q_hi_done, 1)
            act.wait_ge(ct_b_in, 32)
            nc.scalar.activation(ct_hi[0][:, 1, :], first_b[:, :], ACT.Copy).then_inc(ct_b_hi_done, 1)
            act.wait_ge(raw_in, 32)
            nc.scalar.activation(nat[0][:, :, 0:DC], raw[:, :, :], ACT.Copy).then_inc(nat_hi_done, 1)
            passes(act, body)
            act.wait_ge(acc_ready, STEPS // 2 - 2)
            for g in range(NG):
                pt_copy(STEPS - 1, g, 1, 1)
            acc_copy(NB * QB - 2, 0, False)
            acc_copy(NB * QB - 1, 1, False)

        @block.vector
        def _(dve):
            def pt_sub(s, g, slot, half):
                dve.wait_ge(pt_hi_done, s * NG + (g + 1))
                src, lo = transposed(pt_lo, slot, g, half)
                _, hi = transposed(pt_hi, slot, g, half)
                nc.vector.tensor_tensor(lo, src, bits(hi), ALU.subtract).then_inc(pt_lo_done, 1)

            def acc_add(i, parity):
                dve.wait_ge(acc_act, i + 1)
                nc.vector.tensor_tensor(o_b[parity][0:DCB, :], acc[0:DCB, 1, :], o_b[parity][DCB:P, :],
                                        ALU.add).then_inc(acc_dve, 1)

            def step(r, j, first):
                s = r * SPP + j
                prev = not (first and j == 0)
                slot, half = ((j - 1) // 2) % 2, (j - 1) % 2
                dve.wait_ge(scores_ready, s + 1)
                nc.vector.tensor_reduce(negmax[:, j % 2:j % 2 + 1], scores[:, S0:S0 + NKV], AX.X, ALU.max,
                                        negate=True).then_inc(max_done, 1)
                if prev:
                    pt_sub(s - 1, 0, slot, half)
                    pt_sub(s - 1, 1, slot, half)
                dve.wait_ge(exp_done, s + 1)
                nc.vector.reciprocal(rinv[:, j % 2:j % 2 + 1], rowsum[:, j % 2:j % 2 + 1]).then_inc(rinv_done, 1)
                if prev:
                    pt_sub(s - 1, 2, slot, half)
                    pt_sub(s - 1, 3, slot, half)
                if j % 2 == 0 and not (first and j < 4):
                    acc_add(r * QPP + (j // 2 - 2), (j // 2) % 2)

            def body(r, first, last):
                for j in range(SPP):
                    step(r, j, first)

            lower = slice(DCB, P)
            dve.wait_ge(ct_a_hi_done, 1)
            nc.vector.tensor_tensor(ct_lo[0][:, :], ct_raw[:, :], bits(ct_hi[0][:, 0, :]), ALU.subtract).then_inc(ct_a_done, 1)
            dve.wait_ge(q_hi_done, 1)
            nc.vector.tensor_tensor(q_lo[0][:, :, :], qraw[:, :, :], bits(q_hi[0][:, :, :]), ALU.subtract).then_inc(q_done, 1)
            dve.wait_ge(ct_b_hi_done, 1)
            nc.vector.tensor_tensor(ct_hi[0][lower, 1, :], first_b[lower, :], bits(ct_hi[0][lower, 1, :]),
                                    ALU.subtract).then_inc(ct_b_done, 1)
            dve.wait_ge(nat_hi_done, 1)
            nc.vector.tensor_tensor(nat[0][:, :, DC:DC + DCB], raw[:, :, P:DC], bits(nat[0][:, :, P:DC]), ALU.subtract)
            nc.vector.tensor_tensor(nat[0][:, :, DC + DCB:2 * DC], raw[:, :, 0:P], bits(nat[0][:, :, 0:P]),
                                    ALU.subtract).then_inc(nat_done, 1)
            passes(dve, body)
            for g in range(NG):
                pt_sub(STEPS - 1, g, 1, 1)
            acc_add(NB * QB - 2, 0)
            acc_add(NB * QB - 1, 1)

        @block.tensor
        def _(pe):
            def step_scores(r, j, par, first):
                s, b = r * SPP + j, r * SPB + j // SB
                if j % SB == 0:
                    pe.wait_ge(ct_b_done, b + 1)
                    pe.wait_ge(q_done, b + 1)
                if not (first and j == 0):
                    pe.wait_ge(exp_done, s)
                rows = slice((j % SB) * P, (j % SB + 1) * P)
                q_a, q_b = (slice(None), 0, rows), (slice(None), 1, rows)
                for lo, hi in CHUNKS:
                    ct_a, ct_b, ct_al = (t[:, lo:hi] for t in (ct_hi[par][:, 0, :], ct_hi[par][:, 1, :], ct_lo[par]))
                    terms = ((q_hi[par][q_a], ct_a), (q_lo[par][q_a], ct_a), (q_hi[par][q_a], ct_al),
                             (q_hi[par][q_b], ct_b), (q_lo[par][q_b], ct_b))
                    for m, (w, c) in enumerate(terms):
                        last = nc.tensor.matmul(scores[:, S0 + lo:S0 + hi], w, c, start=m == 0, stop=m == len(terms) - 1)
                last.then_inc(scores_ready, 1)

            def pt_transpose(g, j):
                for k, t in enumerate(TG[g]):
                    width = min(P, NKV - t * P)
                    last = nc.tensor.transpose(work[WORK_OF[g]][0:width, k * P:(k + 1) * P],
                                               prob[(j - 1) % 2][:, t * P:t * P + width], ident[:, :])
                last.then_inc(pt_ready, 1)

            def product(slot, par, tiles):
                x = nat[par]
                for k in tiles:
                    a_hi, b_both, a_lo = x[:, k, 0:P], x[:, k, P:P + 2 * DCB], x[:, k, DC + DCB:2 * DC]
                    terms = ((0, a_hi, pt_hi), (0, a_hi, pt_lo), (0, a_lo, pt_hi), (1, b_both, pt_hi), (1, b_both, pt_lo))
                    for m, (blk, w, pt) in enumerate(terms):
                        last = nc.tensor.matmul(acc[:, blk, :], w, pt[slot][:, k, :], start=k == 0 and m == 0,
                                                stop=k == KT - 1 and m in (2, 4), skip_group_check=True)
                if tiles[-1] == KT - 1:
                    last.then_inc(acc_ready, 1)

            def step(r, j, first):
                s = r * SPP + j
                prev = not (first and j == 0)
                step_scores(r, j, (j // SB) % 2, first)
                work_left, q_at = [], None
                if j % 2 == 1 and not (first and j < 3):
                    q_at, work_left = (j - 3) // 2, list(range(0, FIRST_PART))
                elif j % 2 == 0 and not (first and j < 4):
                    q_at, work_left = (j - 4) // 2, list(range(FIRST_PART, KT))
                slot, par = (q_at % 2, (q_at // QB) % 2) if q_at is not None else (0, 0)
                if work_left and j % 2 == 1:
                    i = r * QPP + (j - 3) // 2
                    if (j - 3) // 2 % QB == 0:
                        pe.wait_ge(nat_done, r * SPB + (j - 3) // SB + 1)
                    pe.wait_ge(pt_lo_done, (i + 1) * 2 * NG)
                    if not (first and j == 3):
                        pe.wait_ge(acc_dve, i)
                if prev:
                    pe.wait_ge(prob_done, s)
                    if not (first and j == 1):
                        pe.wait_ge(pt_lo_done, (s - 1) * NG)
                    pt_transpose(0, j)
                    pt_transpose(1, j)
                if work_left:
                    product(slot, par, work_left[0:4])
                if prev:
                    pt_transpose(2, j)
                if work_left:
                    product(slot, par, work_left[4:6])
                if prev:
                    pe.wait_ge(pt_lo_done, (s - 1) * NG + 1)
                    pt_transpose(3, j)
                if work_left[6:]:
                    product(slot, par, work_left[6:])

            def body(r, first, last):
                for j in range(SPP):
                    step(r, j, first)

            pe.wait_ge(ident_done, 2)
            passes(pe, body)
            pe.wait_ge(prob_done, STEPS)
            pe.wait_ge(pt_lo_done, (STEPS - 1) * NG)
            for g in range(3):
                pt_transpose(g, 2)
            pe.wait_ge(pt_lo_done, (STEPS - 1) * NG + 1)
            pt_transpose(3, 2)
            product(0, 1, list(range(FIRST_PART, KT)))
            pe.wait_ge(pt_lo_done, STEPS * NG)
            pe.wait_ge(acc_dve, NB * QB - 1)
            product(1, 1, list(range(KT)))


def attention_output(nc, w_kv, w_out, b_out, x, o_dram, resid):
    NC, CT = 4, TOK // 4
    CB, CTT = CT // NQ, CT // P
    HP = NH // 2
    DEEP = 4
    W = 2 * NQ
    with ExitStack() as ctx:
        sb = lambda name, shape, dt=F32: ctx.enter_context(nc.sbuf_tensor("p3_" + name, shape, dt))
        pb = lambda name, shape: ctx.enter_context(nc.psum_tensor("p3_" + name, shape, F32))
        sem = lambda name: ctx.enter_context(nc.semaphore("p3_" + name))

        wv = sb("wv", [P, 2, INNER])
        wo = sb("wo", [P, HP, DM])
        wv_hi, wv_lo = sb("wv_hi", [P, 2, HP, 2, P], F32R), sb("wv_lo", [P, 2, HP, 2, P], F32R)
        wo_hi, wo_lo = sb("wo_hi", [P, HP, DM], F32R), sb("wo_lo", [P, HP, DM], F32R)
        bias = sb("bias", [P, DM])
        oa = [sb(f"oa{i}", [P, CB, W]) for i in range(DEEP)]
        ob = [sb(f"ob{i}", [DCB, CB, W]) for i in range(DEEP)]
        oa_hi = [sb(f"oa_hi{i}", [P, CB, W], F32R) for i in range(DEEP)]
        oa_lo = [sb(f"oa_lo{i}", [P, CB, W], F32R) for i in range(DEEP)]
        ob_both = [sb(f"ob_both{i}", [P, CB, W], F32R) for i in range(DEEP)]
        at_hi, at_lo = sb("at_hi", [P, HP, CT], F32R), sb("at_lo", [P, HP, CT], F32R)
        vp = [pb(f"vp{i}", [P, CT]) for i in range(2)]
        yp = [pb(f"yp{i}", [P, 512]) for i in range(2)]

        w_in, wo_in, x_in, b_in = sem("w_in"), sem("wo_in"), sem("x_in"), sem("b_in")
        o_in = [sem(f"o_in{i}") for i in range(DEEP)]
        zeroed, lo_zeroed, w_hi_done, w_lo_done, biased = sem("zeroed"), sem("lo_zeroed"), sem("w_hi"), sem("w_lo"), sem("biased")
        oa_hi_done, ob_hi_done, oa_lo_done, ob_lo_done = sem("oa_hi"), sem("ob_hi"), sem("oa_lo"), sem("ob_lo")
        v_ready, at_hi_done, at_lo_done = sem("v_ready"), sem("at_hi"), sem("at_lo")
        y_ready, y_added = sem("y_ready"), sem("y_added")
        block = ctx.enter_context(nc.Block())

        def over_chunks(eng, chunk):
            chunk(0, True, False)
            with eng.Fori(1, NC - 1) as c:
                chunk(c, False, False)
            chunk(NC - 1, False, True)

        def split_next(c, j, last, split):
            if j + DEEP < HP:
                split(c, j + DEEP)
            elif not last:
                split(c + 1, j + DEEP - HP)

        @block.sync
        def _(sp):
            sp.dma_start(wv[:, 0, :], w_kv[0:P, INNER:2 * INNER]).then_inc(w_in, 16)
            for half in (slice(0, DCB), slice(DCB, P)):
                sp.dma_start(wv[half, 1, :], w_kv[P:DC, INNER:2 * INNER]).then_inc(w_in, 16)

            def load(c, j, fresh):
                if not fresh:
                    sp.wait_ge(oa_lo_done, c * HP + (j - DEEP + 1))
                    sp.wait_ge(ob_lo_done, c * HP + (j - DEEP + 1))
                src = o_dram[bass.ds(c * CB, CB), :, j * W:(j + 1) * W]
                for dst, rows in ((oa[j % DEEP], slice(0, P)), (ob[j % DEEP], slice(P, DC))):
                    sp.dma_start(dst[:, :, :], src[:, rows, :].rearrange("b c n -> c b n")).then_inc(o_in[j % DEEP], 16)

            for j in range(DEEP):
                load(0, j, True)
            sp.dma_start(wo[:, :, :], w_out.rearrange("(j p) n -> p j n", p=P)).then_inc(wo_in, 16)
            sp.dma_start(resid[:, :, :], x.rearrange("(t b) q d -> (b q) t d", b=P // NQ)).then_inc(x_in, 16)
            sp.dma_start(bias[:, :], b_out.rearrange("(a n) -> a n", a=1).partition_broadcast(P)).then_inc(b_in, 16)
            for j in range(DEEP, HP):
                load(0, j, False)
            with sp.Fori(1, NC) as c:
                for j in range(HP):
                    load(c, j, False)

        @block.gpsimd
        def _(pool):
            nc.gpsimd.memset(bits(wv_hi[:, :, :, :, :]), 0.0).then_inc(zeroed, 1)

            def split(c, j):
                i = j % DEEP
                pool.wait_ge(oa_hi_done, c * HP + (j + 1))
                nc.gpsimd.tensor_tensor(oa_lo[i][:, :, :], oa[i][:, :, :], bits(oa_hi[i][:, :, :]),
                                        ALU.subtract).then_inc(oa_lo_done, 1)

            def chunk(c, first, last):
                for j in range(HP):
                    split_next(c, j, last, split)
                    if first:
                        if j == 0:
                            pool.wait_ge(x_in, 16)
                            pool.wait_ge(b_in, 16)
                        for t in range(j * TT // HP, (j + 1) * TT // HP):
                            nc.gpsimd.tensor_tensor(resid[:, t, :], resid[:, t, :], bias[:, :], ALU.add).then_inc(biased, 1)

            for j in range(DEEP):
                split(0, j)
            over_chunks(pool, chunk)

        def wv_place(dst, blk, r):
            half = slice(r * DH, (r + 1) * DH)
            return dst[:, blk, :, r, half], wv[:, blk, :].rearrange("p (j r d) -> p j r d", r=2, d=DH)[:, :, r, :]

        @block.scalar
        def _(act):
            act.wait_ge(w_in, 48)
            act.wait_ge(zeroed, 1)
            for blk in range(2):
                for r in range(2):
                    dst, src = wv_place(wv_hi, blk, r)
                    nc.scalar.activation(dst, src, ACT.Copy).then_inc(w_hi_done, 1)

            def split(c, j, fresh=False):
                i = j % DEEP
                act.wait_ge(o_in[i], c * (HP // DEEP * 32) + (j // DEEP + 1) * 32)
                if not fresh:
                    act.wait_ge(v_ready, c * HP + (j - DEEP + 1))
                nc.scalar.activation(oa_hi[i][:, :, :], oa[i][:, :, :], ACT.Copy).then_inc(oa_hi_done, 1)
                nc.scalar.activation(ob_both[i][0:DCB], ob[i][:, :, :], ACT.Copy).then_inc(ob_hi_done, 1)

            def chunk(c, first, last):
                for j in range(HP):
                    act.wait_ge(v_ready, c * HP + (j + 1))
                    if j == 0 and not first:
                        act.wait_ge(y_ready, c * CTT)
                    nc.scalar.activation(at_hi[:, j, :], vp[j % 2][:, :], ACT.Copy).then_inc(at_hi_done, 1)
                    split_next(c, j, last, split)

            for j in range(DEEP):
                split(0, j, True)
            act.wait_ge(wo_in, 16)
            nc.scalar.activation(wo_hi[:, :, :], wo[:, :, :], ACT.Copy).then_inc(w_hi_done, 1)
            over_chunks(act, chunk)

        @block.vector
        def _(dve):
            nc.vector.memset(bits(wv_lo[:, :, :, :, :]), 0.0).then_inc(lo_zeroed, 1)
            dve.wait_ge(lo_zeroed, 1)
            for blk in range(2):
                for r in range(2):
                    dst, src = wv_place(wv_lo, blk, r)
                    hi, _ = wv_place(wv_hi, blk, r)
                    dve.wait_ge(w_hi_done, blk * 2 + r + 1)
                    nc.vector.tensor_tensor(dst, src, bits(hi), ALU.subtract).then_inc(w_lo_done, 1)

            def split(c, j):
                i = j % DEEP
                dve.wait_ge(ob_hi_done, c * HP + (j + 1))
                nc.vector.tensor_tensor(ob_both[i][DCB:P], ob[i][:, :, :], bits(ob_both[i][0:DCB]),
                                        ALU.subtract).then_inc(ob_lo_done, 1)

            def chunk(c, first, last):
                for j in range(HP):
                    dve.wait_ge(at_hi_done, c * HP + (j + 1))
                    nc.vector.tensor_tensor(at_lo[:, j, :], vp[j % 2][:, :], bits(at_hi[:, j, :]),
                                            ALU.subtract).then_inc(at_lo_done, 1)
                    split_next(c, j, last, split)
                for t in range(CTT):
                    if t == 0:
                        dve.wait_ge(biased, CTT if first else TT)
                    dve.wait_ge(y_ready, c * CTT + (t + 1))
                    tile = resid[:, bass.ds(c * CTT + t, 1), :].rearrange("p a d -> p (a d)")
                    nc.vector.tensor_tensor(tile, yp[t % 2][:, 0:DM], tile, ALU.add).then_inc(y_added, 1)

            for j in range(DEEP):
                split(0, j)
            dve.wait_ge(w_hi_done, 5)
            nc.vector.tensor_tensor(wo_lo[:, :, :], wo[:, :, :], bits(wo_hi[:, :, :]), ALU.subtract).then_inc(w_lo_done, 1)
            over_chunks(dve, chunk)

        @block.tensor
        def _(pe):
            def values(c, j, first):
                i = j % DEEP
                pe.wait_ge(oa_lo_done, c * HP + (j + 1))
                pe.wait_ge(ob_lo_done, c * HP + (j + 1))
                if not (first and j < 2):
                    pe.wait_ge(at_lo_done, c * HP + (j - 1))
                terms = []
                for r in range(2):
                    h = slice(r * NQ, (r + 1) * NQ)
                    a_hi, a_lo, b_both = oa_hi[i][:, :, h], oa_lo[i][:, :, h], ob_both[i][:, :, h]
                    terms += [(wv_hi[:, 0, j, r, :], a_hi), (wv_lo[:, 0, j, r, :], a_hi), (wv_hi[:, 0, j, r, :], a_lo),
                              (wv_hi[:, 1, j, r, :], b_both), (wv_lo[:, 1, j, r, :], b_both)]
                for m, (w, o) in enumerate(terms):
                    last = nc.tensor.matmul(vp[j % 2][:, :].rearrange("p (b q) -> p b q", q=NQ), w, o,
                                            start=m == 0, stop=m == len(terms) - 1)
                last.then_inc(v_ready, 1)

            def output(c, t, first):
                if t == 0:
                    pe.wait_ge(at_lo_done, c * HP + (HP - 1))
                if not (first and t < 2):
                    pe.wait_ge(y_added, c * CTT + (t - 1))
                tok = slice(t * P, (t + 1) * P)
                for j in range(HP):
                    if t == 0 and j == HP - 1:
                        pe.wait_ge(at_lo_done, (c + 1) * HP)
                    for m, (a, w) in enumerate(((at_hi, wo_hi), (at_hi, wo_lo), (at_lo, wo_hi))):
                        last = nc.tensor.matmul(yp[t % 2][:, 0:DM], a[:, j, tok], w[:, j, :], start=j == 0 and m == 0,
                                                stop=j == HP - 1 and m == 2)
                last.then_inc(y_ready, 1)

            def chunk(c, first, last):
                for j in range(HP):
                    values(c, j, first)
                if first:
                    pe.wait_ge(w_lo_done, 5)
                for t in range(CTT):
                    output(c, t, first)

            pe.wait_ge(w_lo_done, 4)
            over_chunks(pe, chunk)


def mix_and_feed(nc, channels, squares, bo, w1, b1_cols, w2, b2, resid, out):
    NC, CT = 4, TOK // 4
    CB, CTT = CT // NQ, CT // P
    KB = DM // P
    WIDTH = w1.shape[1]
    FB = WIDTH // P
    NM = 3 * KB
    BR = 33
    with ExitStack() as ctx:
        sb = lambda name, shape, dt=F32: ctx.enter_context(nc.sbuf_tensor("p4_" + name, shape, dt))
        pb = lambda name, shape: ctx.enter_context(nc.psum_tensor("p4_" + name, shape, F32))
        sem = lambda name: ctx.enter_context(nc.semaphore("p4_" + name))

        sqT_hi, sqT_lo = sb("sqT_hi", [P, 4, KB, DM], F32R), sb("sqT_lo", [P, 4, KB, DM], F32R)
        w1_hi, w1_lo = sb("w1_hi", [P, KB, WIDTH], F32R), sb("w1_lo", [P, KB, WIDTH], F32R)
        w2_hi, w2_lo = sb("w2_hi", [P, FB, DM], F32R), sb("w2_lo", [P, FB, DM], F32R)
        hid_hi, hid_lo = sb("hid_hi", [P, FB, CT], F32R), sb("hid_lo", [P, FB, CT], F32R)
        area = sb("area", [P, 13, CT])
        slot = lambda n: area[:, n, :]
        eb, er, wkv = [slot(0), slot(1)], [slot(2), slot(3)], [slot(4), slot(5)]
        num, den, prod = slot(6), slot(7), slot(8)
        hid = [slot(9), slot(10)]
        zT = area[:, 11:13, :]
        weights = lambda n, inner: area[:, n:n + 4, :].rearrange("p f n -> p (f n)").rearrange("p (k n) -> p k n", n=inner)
        w1_raw, w2_raw = weights(0, WIDTH), weights(8, DM)
        square = area[:, 4:8, :].rearrange("p m (k n) -> p m k n", n=DM)
        bias_raw, bias = sb("bias_raw", [BR, 2, DM]), sb("bias", [BR, 2, DM], F32R)
        ones = sb("ones", [BR, P], F32R)
        channel = sb("channel", [P, 5, KB])
        td = sb("td", [P, 2, KB])
        tdm = sb("tdm", [P, KB, CB, NQ])
        b1_col = sb("b1_col", [P, FB])
        ident = sb("ident", [P, P])
        stats = [sb(f"stats{m}", [P, CTT, 6]) for m in range(2)]
        parts = [sb(f"parts{m}", [P, 3, CTT]) for m in range(2)]
        mean = [sb(f"mean{m}", [P, CTT]) for m in range(2)]
        std = [sb(f"std{m}", [P, 4, CTT]) for m in range(2)]
        xn = [sb(f"xn{m}", [P, CTT, DM]) for m in range(2)]
        xnT = sb("xnT", [P, KB, CB, NQ + 1])
        diff = sb("diff", [P, KB, CB, NQ])
        mixed = sb("mixed", [P, 3, CB, NQ])
        mixed_hi, mixed_lo = sb("mixed_hi", [P, 3, KB, CT], F32R), sb("mixed_lo", [P, 3, KB, CT], F32R)
        ek, ekv = ([sb(f"{n}{o}", [P, CB, NQ]) for o in range(KB)] for n in ("ek", "ekv"))
        wkv_hi, wkv_lo = sb("wkv_hi", [P, KB, CT], F32R), sb("wkv_lo", [P, KB, CT], F32R)
        zT_hi, zT_lo = sb("zT_hi", [P, KB, CT], F32R), sb("zT_lo", [P, KB, CT], F32R)

        tp = pb("tp", [P, 512])
        rp = [pb(f"rp{i}", [P, CT]) for i in range(3)]
        fp = [pb(f"fp{i}", [P, CT]) for i in range(2)]
        yp = [pb(f"yp{i}", [P, 512]) for i in range(2)]

        sq_in, ch_in, b_in, w1_in, w2_in = sem("sq_in"), sem("ch_in"), sem("b_in"), sem("w1_in"), sem("w2_in")
        ident_done, zeroed, td_act, td_dve = sem("ident"), sem("zeroed"), sem("td_act"), sem("td_dve")
        bias_zero, ones_done, bias_done = sem("bias_zero"), sem("ones_done"), sem("bias_done")
        sq_hi_done, sq_lo_done = sem("sq_hi"), sem("sq_lo")
        w1_hi_done, w1_lo_done, w2_hi_done, w2_lo_done = sem("w1_hi"), sem("w1_lo"), sem("w2_hi"), sem("w2_lo")
        ln_step, xn_done = [sem("ln_step0"), sem("ln_step1")], [sem("xn_done0"), sem("xn_done1")]
        tp_ready, tp_read = [sem("tp_ready0"), sem("tp_ready1")], [sem("tp_read0"), sem("tp_read1")]
        zT_lo_done = sem("zT_lo_done")
        diff_done, mix_done, mix_hi, mix_lo = sem("diff_done"), sem("mix_done"), sem("mix_hi"), sem("mix_lo")
        r_ready, exps_done, wkv_step = sem("r_ready"), sem("exps_done"), sem("wkv_step")
        wkv_hi_done, wkv_lo_done = sem("wkv_hi_done"), sem("wkv_lo_done")
        g_ready, g_added = sem("g_ready"), sem("g_added")
        f_ready, hid_done, hid_lo_done = sem("f_ready"), sem("hid_done"), sem("hid_lo_done")
        y_ready, y_added, stored = sem("y_ready"), sem("y_added"), sem("stored")
        block = ctx.enter_context(nc.Block())

        LN = CTT + 7 + 1 + 5
        WS = 9

        def tile_of(c, t):
            return resid[:, bass.ds(c * CTT + t, 1), :].rearrange("p a d -> p (a d)")

        def fresh(c):
            return isinstance(c, int) and c == 0

        def passes(eng, run):
            run(-2, "A")
            run(-1, "AB")
            run(0, "ABC")
            with eng.Fori(1, NC - 2) as i:
                run(i, "ABC")
            run(NC - 2, "BC")
            run(NC - 1, "C")

        @block.sync
        def _(sp):
            sp.dma_start(channel[:, :, :], channels).then_inc(ch_in, 16)
            sp.dma_start(b1_col[:, :], b1_cols).then_inc(ch_in, 16)
            for m in range(4):
                sp.dma_start(square[:, m, :, :], squares[m, :, :].rearrange("(k p) n -> p k n", p=P)).then_inc(sq_in, 16)
            sp.dma_start(w1_raw, w1.rearrange("(k p) n -> p k n", p=P)).then_inc(w1_in, 16)
            sp.dma_start(w2_raw, w2.rearrange("(k p) n -> p k n", p=P)).then_inc(w2_in, 16)
            sp.wait_ge(bias_zero, 1)
            for n, v in enumerate((bo, b2)):
                for row in (0, BR - 1):
                    sp.dma_start(bias_raw[row:row + 1, n, :], v.rearrange("(a n) -> a n", a=1)).then_inc(b_in, 16)
            out_v = out.rearrange("(c u b) q d -> (b q) (c u) d", b=P // NQ, u=CTT)
            with sp.Fori(0, NC) as c:
                sp.wait_ge(y_added, (c + 1) * CTT)
                sp.dma_start(out_v[:, bass.ds(c * CTT, CTT), :], resid[:, bass.ds(c * CTT, CTT), :]).then_inc(stored, 16)
            sp.wait_ge(stored, NC * 16)

        @block.gpsimd
        def _(pool):
            identity(nc, pool, ident, ident_done)
            nc.gpsimd.memset(bias_raw[:, :, :], 0.0).then_inc(bias_zero, 1)
            nc.gpsimd.memset(xnT[:, :, :, 0:1], 0.0).then_inc(zeroed, 1)
            for o in range(KB):
                nc.gpsimd.memset(ek[o][:, :, 0:1], 0.0).then_inc(zeroed, 1)
                nc.gpsimd.memset(ekv[o][:, :, 0:1], 0.0).then_inc(zeroed, 1)
            nc.gpsimd.memset(tdm[:, :, :, :], 1.0).then_inc(zeroed, 1)
            pool.wait_ge(zeroed, 2 * KB + 2)
            nc.gpsimd.memset(tdm[:, :, :, 0:1], 0.0).then_inc(zeroed, 1)
            nc.gpsimd.memset(bits(ones[:, :]), 1.0).then_inc(ones_done, 1)
            def mixed_sub(c):
                for n in range(NM):
                    k, m = n // 3, n % 3
                    pool.wait_ge(mix_hi, c * NM + (n + 1))
                    nc.gpsimd.tensor_tensor(mixed_lo[:, m, k, :], mixed[:, m, :, :].rearrange("p b q -> p (b q)"),
                                            bits(mixed_hi[:, m, k, :]), ALU.subtract).then_inc(mix_lo, 1)

            def wkv_sub(c):
                for o in range(KB):
                    pool.wait_ge(wkv_hi_done, c * KB + (o + 1))
                    nc.gpsimd.tensor_tensor(wkv_lo[:, o, :], wkv[o][:, :], bits(wkv_hi[:, o, :]), ALU.subtract).then_inc(wkv_lo_done, 1)

            def feed_sub(c):
                for k in range(KB):
                    pool.wait_ge(tp_read[1], c * KB + (k + 1))
                    nc.gpsimd.tensor_tensor(zT_lo[:, k, :], zT[:, k, :], bits(zT_hi[:, k, :]), ALU.subtract).then_inc(zT_lo_done, 1)

            def hidden_sub(c):
                for f in range(FB):
                    pool.wait_ge(hid_done, c * FB + (f + 1))
                    if not fresh(c) and f == 0:
                        pool.wait_ge(y_ready, c * CTT)
                    nc.gpsimd.tensor_tensor(hid_lo[:, f, :], hid[f % 2][:, :], bits(hid_hi[:, f, :]), ALU.subtract).then_inc(hid_lo_done, 1)

            def run(i, stages):
                if "C" in stages:
                    hidden_sub(i)
                if "B" in stages:
                    wkv_sub(i + 1)
                if "A" in stages:
                    mixed_sub(i + 2)
                if "B" in stages:
                    feed_sub(i + 1)
                if isinstance(i, int) and i == -2:
                    pool.wait_ge(w2_hi_done, 1)
                    nc.gpsimd.tensor_tensor(w2_lo[:, :, :], w2_raw, bits(w2_hi[:, :, :]), ALU.subtract).then_inc(w2_lo_done, 1)

            passes(pool, run)

        @block.scalar
        def _(act):
            def first_weights():
                act.wait_ge(ch_in, 2 * 16)
                nc.scalar.activation(td[:, 0, :], channel[:, 0, :], ACT.Exp).then_inc(td_act, 1)
                act.wait_ge(td_act, 1)
                nc.scalar.activation(td[:, 1, :], td[:, 0, :], ACT.Exp, scale=-1.0).then_inc(td_act, 1)
                act.wait_ge(sq_in, 64)
                nc.scalar.activation(sqT_hi[:, :, :, :], square, ACT.Copy).then_inc(sq_hi_done, 1)

            def root(c, m):
                act.wait_ge(ln_step[m], c * LN + (CTT + 7))
                nc.scalar.activation(std[m][:, 1, :], std[m][:, 0, :], ACT.Sqrt).then_inc(ln_step[m], 1)

            def mix_in(c):
                for k in range(KB):
                    act.wait_ge(tp_ready[0], c * KB + (k + 1))
                    if k == 0 and fresh(c):
                        act.wait_ge(zeroed, 2 * KB + 3)
                    if k == 0 and not fresh(c):
                        act.wait_ge(mix_done, c * NM)
                    nc.scalar.activation(xnT[:, k, :, 1:NQ + 1], tp[:, :].rearrange("p (b q) -> p b q", q=NQ),
                                         ACT.Copy).then_inc(tp_read[0], 1)

            def feed_copy(c):
                for k in range(KB):
                    act.wait_ge(tp_ready[1], c * KB + (k + 1))
                    if not fresh(c) and k == 0:
                        act.wait_ge(f_ready, c * FB)
                    nc.scalar.activation(zT_hi[:, k, :], tp[:, :], ACT.Copy)
                    nc.scalar.activation(zT[:, k, :], tp[:, :], ACT.Copy).then_inc(tp_read[1], 1)

            def mix_round(c):
                for n in range(NM):
                    k, m = n // 3, n % 3
                    act.wait_ge(mix_done, c * NM + (n + 1))
                    if not fresh(c) and n == 0:
                        act.wait_ge(r_ready, c * NM)
                    nc.scalar.activation(mixed_hi[:, m, k, :], mixed[:, m, :, :].rearrange("p b q -> p (b q)"),
                                         ACT.Copy).then_inc(mix_hi, 1)

            def exps(c, o):
                act.wait_ge(r_ready, c * NM + 3 * (o + 1))
                if fresh(c) and o == 0:
                    act.wait_ge(w1_lo_done, 1)
                    act.wait_ge(w2_lo_done, 1)
                if not fresh(c):
                    act.wait_ge(wkv_step, c * (KB * WS) - (KB - 1 - o) * WS)
                kp = rp[0][:, :].rearrange("p (b q) -> p b q", q=NQ)
                nc.scalar.activation(ek[o][:, :, 1:NQ], kp[:, :, 0:NQ - 1], ACT.Exp)
                nc.scalar.activation(eb[o][:, :], rp[0][:, :], ACT.Exp, bias=channel[:, 1, o:o + 1])
                nc.scalar.activation(er[o][:, :], rp[2][:, :], ACT.Exp, scale=-1.0).then_inc(exps_done, 1)

            def wkv_round(c, o):
                act.wait_ge(wkv_step, c * (KB * WS) + (o + 1) * WS)
                if not fresh(c) and o == 0:
                    act.wait_ge(g_ready, c * CTT)
                nc.scalar.activation(wkv_hi[:, o, :], wkv[o][:, :], ACT.Copy).then_inc(wkv_hi_done, 1)

            def relus(c, blocks):
                for f in blocks:
                    act.wait_ge(f_ready, c * FB + (f + 1))
                    if not (fresh(c) and f < 2):
                        act.wait_ge(hid_lo_done, c * FB + (f - 1))
                    if not fresh(c) and f == 0:
                        act.wait_ge(y_ready, c * CTT)
                    for dst in (hid_hi[:, f, :], hid[f % 2][:, :]):
                        last = nc.scalar.activation(dst, fp[f % 2][:, :], ACT.Relu, bias=b1_col[:, f:f + 1])
                    last.then_inc(hid_done, 1)

            def run(i, stages):
                if "A" in stages:
                    root(i + 2, 0)
                if isinstance(i, int) and i == -2:
                    first_weights()
                if "B" in stages:
                    exps(i + 1, 0)
                if "C" in stages:
                    relus(i, range(0, 2))
                if "A" in stages:
                    mix_in(i + 2)
                if "B" in stages:
                    exps(i + 1, 1)
                if "C" in stages:
                    relus(i, range(2, FB))
                if "B" in stages:
                    for o in range(KB):
                        wkv_round(i + 1, o)
                if "A" in stages:
                    mix_round(i + 2)
                if "B" in stages:
                    root(i + 1, 1)
                    feed_copy(i + 1)
                if isinstance(i, int) and i == -2:
                    act.wait_ge(w1_in, 16)
                    nc.scalar.activation(w1_hi[:, :, :], w1_raw, ACT.Copy).then_inc(w1_hi_done, 1)
                    act.wait_ge(w2_in, 16)
                    nc.scalar.activation(w2_hi[:, :, :], w2_raw, ACT.Copy).then_inc(w2_hi_done, 1)

            passes(act, run)

        @block.vector
        def _(dve):
            def norm(c, m):
                step, std_m, parts_m = ln_step[m], std[m], parts[m]
                base = c * LN
                for t in range(CTT):
                    if m == 1:
                        dve.wait_ge(g_added, c * CTT + (t + 1))
                        dve.wait_ge(td_dve, KB)
                    nc.vector.bn_stats(stats[m][:, t, :], tile_of(c, t)).then_inc(step, 1)
                even_mean, even_sq, odd_mean, odd_sq = (stats[m][:, :, n] for n in (1, 2, 4, 5))
                dve.wait_ge(step, base + CTT)
                nc.vector.tensor_tensor(parts_m[:, 0, :], even_mean, odd_mean, ALU.add).then_inc(step, 1)
                nc.vector.tensor_tensor(parts_m[:, 1, :], even_mean, odd_mean, ALU.subtract).then_inc(step, 1)
                nc.vector.tensor_tensor(parts_m[:, 2, :], even_sq, odd_sq, ALU.add).then_inc(step, 1)
                dve.wait_ge(step, base + (CTT + 3))
                nc.vector.tensor_scalar(mean[m][:, :], parts_m[:, 0, :], 0.5, None, ALU.mult).then_inc(step, 1)
                nc.vector.scalar_tensor_tensor(parts_m[:, 1, :], parts_m[:, 1, :], 0.25, parts_m[:, 1, :], ALU.mult, ALU.mult).then_inc(step, 1)
                nc.vector.tensor_scalar(parts_m[:, 2, :], parts_m[:, 2, :], 1.0 / DM, EPS, ALU.mult, ALU.add).then_inc(step, 1)
                dve.wait_ge(step, base + (CTT + 6))
                nc.vector.tensor_tensor(std_m[:, 0, :], parts_m[:, 1, :], parts_m[:, 2, :], ALU.add).then_inc(step, 1)
                dve.wait_ge(step, base + (CTT + 8))
                nc.vector.reciprocal(std_m[:, 2, :], std_m[:, 1, :]).then_inc(step, 1)
                dve.wait_ge(step, base + (CTT + 9))
                nc.vector.tensor_tensor(std_m[:, 2, :], std_m[:, 2, :], std_m[:, 0, :], ALU.mult).then_inc(step, 1)
                dve.wait_ge(step, base + (CTT + 10))
                nc.vector.tensor_tensor(std_m[:, 1, :], std_m[:, 1, :], std_m[:, 2, :], ALU.add).then_inc(step, 1)
                dve.wait_ge(step, base + (CTT + 11))
                nc.vector.reciprocal(std_m[:, 2, :], std_m[:, 1, :]).then_inc(step, 1)
                dve.wait_ge(step, base + (CTT + 12))
                nc.vector.tensor_scalar(std_m[:, 3, :], std_m[:, 2, :], 2.0, None, ALU.mult).then_inc(step, 1)
                dve.wait_ge(step, base + LN)
                if not fresh(c):
                    dve.wait_ge(tp_ready[m], c * KB)
                for t in range(CTT):
                    nc.vector.tensor_scalar(xn[m][:, t, :], tile_of(c, t), mean[m][:, t:t + 1], std_m[:, 3, t:t + 1],
                                            ALU.subtract, ALU.mult).then_inc(xn_done[m], 1)

            def mix(c):
                for k in range(KB):
                    now, before = xnT[:, k, :, 1:NQ + 1], xnT[:, k, :, 0:NQ]
                    dve.wait_ge(tp_read[0], c * KB + (k + 1))
                    nc.vector.tensor_tensor(diff[:, k, :, :], now, before, ALU.subtract).then_inc(diff_done, 1)
                for k in range(KB):
                    before = xnT[:, k, :, 0:NQ]
                    for m in range(3):
                        if m == 0:
                            dve.wait_ge(diff_done, c * KB + (k + 1))
                        if not (fresh(c) and k == 0):
                            dve.wait_ge(mix_lo, c * NM + (3 * k + m - 2))
                        nc.vector.scalar_tensor_tensor(mixed[:, m, :, :], diff[:, k, :, :], channel[:, 2 + m, k:k + 1],
                                                       before, ALU.mult, ALU.add).then_inc(mix_done, 1)

            def recur(c, o):
                base = c * (KB * WS) + o * WS
                vp = rp[1][:, :].rearrange("p (b q) -> p b q", q=NQ)
                flat = lambda ap: ap.rearrange("p b q -> p (b q)")
                decays = flat(tdm[:, o, :, :])
                dve.wait_ge(exps_done, c * KB + (o + 1))
                if fresh(c) and o == 0:
                    dve.wait_ge(td_dve, KB)
                nc.vector.tensor_tensor(ekv[o][:, :, 1:NQ], vp[:, :, 0:NQ - 1], ek[o][:, :, 1:NQ], ALU.mult).then_inc(wkv_step, 1)
                nc.vector.tensor_tensor(prod[:, :], rp[1][:, :], eb[o][:, :], ALU.mult).then_inc(wkv_step, 1)
                nc.vector.tensor_tensor_scan(den[:, :], decays, flat(ek[o][:, :, :]), 0.0, ALU.mult, ALU.add).then_inc(wkv_step, 1)
                dve.wait_ge(wkv_step, base + 1)
                nc.vector.tensor_tensor_scan(num[:, :], decays, flat(ekv[o][:, :, :]), 0.0, ALU.mult, ALU.add).then_inc(wkv_step, 1)
                dve.wait_ge(wkv_step, base + 3)
                nc.vector.tensor_tensor(den[:, :], den[:, :], eb[o][:, :], ALU.add).then_inc(wkv_step, 1)
                dve.wait_ge(wkv_step, base + 4)
                nc.vector.tensor_tensor(num[:, :], num[:, :], prod[:, :], ALU.add).then_inc(wkv_step, 1)
                dve.wait_ge(wkv_step, base + 5)
                nc.vector.scalar_tensor_tensor(er[o][:, :], er[o][:, :], 1.0, den[:, :], ALU.add, ALU.mult).then_inc(wkv_step, 1)
                dve.wait_ge(wkv_step, base + 7)
                nc.vector.reciprocal(er[o][:, :], er[o][:, :]).then_inc(wkv_step, 1)
                dve.wait_ge(wkv_step, base + 8)
                if not fresh(c):
                    dve.wait_ge(wkv_lo_done, c * KB - (KB - 1 - o))
                nc.vector.tensor_tensor(wkv[o][:, :], num[:, :], er[o][:, :], ALU.mult).then_inc(wkv_step, 1)

            def decays_and_biases():
                dve.wait_ge(td_act, 2)
                dve.wait_ge(zeroed, 2 * KB + 3)
                for k in range(KB):
                    nc.vector.tensor_scalar(tdm[:, k, :, :], tdm[:, k, :, :], td[:, 1, k:k + 1], None, ALU.mult).then_inc(td_dve, 1)
                low = slice(BR - 1, BR)
                dve.wait_ge(b_in, 4 * 16)
                nc.vector.tensor_copy(bias[:, :, :], bias_raw[:, :, :]).then_inc(bias_done, 1)
                dve.wait_ge(bias_done, 1)
                nc.vector.tensor_tensor(bias[low], bias_raw[low], bits(bias[low]), ALU.subtract).then_inc(bias_done, 1)

            def add_out(c, ready, added, t):
                dve.wait_ge(ready, c * CTT + (t + 1))
                nc.vector.tensor_tensor(tile_of(c, t), yp[t % 2][:, 0:DM], tile_of(c, t), ALU.add).then_inc(added, 1)

            def run(i, stages):
                if "A" in stages:
                    norm(i + 2, 0)
                if isinstance(i, int) and i == -2:
                    dve.wait_ge(sq_hi_done, 1)
                    nc.vector.tensor_tensor(sqT_lo[:, :, :, :], square, bits(sqT_hi[:, :, :, :]), ALU.subtract).then_inc(sq_lo_done, 1)
                if "B" in stages:
                    for o in range(KB):
                        recur(i + 1, o)
                if "A" in stages:
                    mix(i + 2)
                if isinstance(i, int) and i == -2:
                    decays_and_biases()
                    dve.wait_ge(w1_hi_done, 1)
                    nc.vector.tensor_tensor(w1_lo[:, :, :], w1_raw, bits(w1_hi[:, :, :]), ALU.subtract).then_inc(w1_lo_done, 1)
                if "C" in stages:
                    for t in range(2):
                        add_out(i, y_ready, y_added, t)
                if "B" in stages:
                    for t in range(CTT):
                        add_out(i + 1, g_ready, g_added, t)
                    norm(i + 1, 1)
                if "C" in stages:
                    for t in range(2, CTT):
                        add_out(i, y_ready, y_added, t)

            passes(dve, run)

        @block.tensor
        def _(pe):
            pe.wait_ge(ident_done, 2)

            def transposes(c, m, before):
                pe.wait_ge(xn_done[m], (c + 1) * CTT)
                for k in range(KB):
                    if k > 0:
                        pe.wait_ge(tp_read[m], c * KB + k)
                    elif before is not None:
                        pe.wait_ge(*before)
                    for t in range(CTT):
                        last = nc.tensor.transpose(tp[:, t * P:(t + 1) * P], xn[m][:, t, k * P:(k + 1) * P], ident[:, :])
                    last.then_inc(tp_ready[m], 1)

            def split_terms(w_hi, w_lo, a_hi, a_lo):
                return ((w_hi, a_hi), (w_lo, a_hi), (w_hi, a_lo))

            def mixing(c, o):
                if o == 0:
                    pe.wait_ge(mix_lo, (c + 1) * NM)
                if fresh(c) and o == 0:
                    pe.wait_ge(sq_lo_done, 1)
                if not (fresh(c) and o == 0):
                    pe.wait_ge(exps_done, c * KB + o)
                    pe.wait_ge(wkv_step, c * (KB * WS) + (o * WS - WS + 2))
                cols = slice(o * P, (o + 1) * P)
                for m in range(3):
                    terms = [t for k in range(KB) for t in split_terms(sqT_hi[:, m, k, cols], sqT_lo[:, m, k, cols],
                                                                      mixed_hi[:, m, k, :], mixed_lo[:, m, k, :])]
                    for n, (w, a) in enumerate(terms):
                        last = nc.tensor.matmul(rp[m][:, :], w, a, start=n == 0, stop=n == len(terms) - 1)
                    last.then_inc(r_ready, 1)

            def out_tile(t, which, blocks, a_hi, a_lo, w_hi, w_lo, ready):
                tok = slice(t * P, (t + 1) * P)
                terms = [(ones[:, :], bias[:, which, :])]
                terms += [x for k in range(blocks) for x in ((a_hi[:, k, tok], w_hi[:, k, :]), (a_hi[:, k, tok], w_lo[:, k, :]),
                                                             (a_lo[:, k, tok], w_hi[:, k, :]))]
                for n, (a, w) in enumerate(terms):
                    last = nc.tensor.matmul(yp[t % 2][:, 0:DM], a, w, start=n == 0, stop=n == len(terms) - 1)
                last.then_inc(ready, 1)

            def mixed_out(c, with_c):
                pe.wait_ge(wkv_lo_done, (c + 1) * KB)
                if fresh(c):
                    pe.wait_ge(ones_done, 1)
                    pe.wait_ge(bias_done, 2)
                for t in range(CTT):
                    if t >= 2:
                        pe.wait_ge(g_added, c * CTT + (t - 1))
                    elif with_c:
                        pe.wait_ge(y_added, (c - 1) * CTT + (t + 1))
                    out_tile(t, 0, KB, wkv_hi, wkv_lo, sqT_hi[:, 3], sqT_lo[:, 3], g_ready)

            def feed_in(c, blocks):
                for f in blocks:
                    if f == 0:
                        pe.wait_ge(zT_lo_done, (c + 1) * KB)
                        if fresh(c):
                            pe.wait_ge(w1_lo_done, 1)
                    if not (fresh(c) and f < 2):
                        pe.wait_ge(hid_done, c * FB + (f - 1))
                    cols = slice(f * P, (f + 1) * P)
                    terms = [t for k in range(KB) for t in split_terms(w1_hi[:, k, cols], w1_lo[:, k, cols],
                                                                      zT_hi[:, k, :], zT_lo[:, k, :])]
                    for n, (w, a) in enumerate(terms):
                        last = nc.tensor.matmul(fp[f % 2][:, :], w, a, start=n == 0, stop=n == len(terms) - 1)
                    last.then_inc(f_ready, 1)

            def feed_out(c, tiles, with_b):
                for t in tiles:
                    if t == 0:
                        pe.wait_ge(hid_lo_done, (c + 1) * FB)
                        if fresh(c):
                            pe.wait_ge(w2_lo_done, 1)
                    if t < 2 and fresh(c):
                        pe.wait_ge(g_added, CTT - 1 + t)
                    elif t < 2:
                        pe.wait_ge(y_added, c * CTT + (t - 1))
                    elif with_b:
                        pe.wait_ge(g_added, (c + 1) * CTT + (t + 1))
                    else:
                        pe.wait_ge(y_added, c * CTT + (t - 1))
                    out_tile(t, 1, FB, hid_hi, hid_lo, w2_hi, w2_lo, y_ready)

            def run(i, stages):
                a, b, c = ("A" in stages), ("B" in stages), ("C" in stages)
                if b:
                    mixing(i + 1, 0)
                if c:
                    feed_in(i, range(0, 2))
                if a:
                    before = (tp_read[1], (i + 1) * KB) if c else (tp_read[0], (i + 2) * KB) if b else None
                    transposes(i + 2, 0, before)
                if b:
                    mixing(i + 1, 1)
                if c:
                    feed_in(i, range(2, FB))
                    feed_out(i, range(0, 2), b)
                if b:
                    mixed_out(i + 1, c)
                if c:
                    feed_out(i, range(2, CTT), b)
                if b:
                    transposes(i + 1, 1, (tp_read[0], (i + 3 if a else i + 2) * KB))

            passes(pe, run)


def kernel(x, ctx_768, L0_xattn_w_q, L0_xattn_w_kv, L0_xattn_w_out, L0_xattn_b_out, L0_attn_time_decay,
           L0_attn_time_first, L0_attn_time_mix_key, L0_attn_time_mix_value, L0_attn_time_mix_receptance,
           L0_attn_Wk, L0_attn_Wv, L0_attn_Wr, L0_attn_Wo, L0_attn_bo, L0_ffn_w1, L0_ffn_b1, L0_ffn_w2, L0_ffn_b2):
    import concourse.bacc as bacc
    from concourse.bass_utils import run_bass_kernel_spmd

    nc = bacc.Bacc("TRN2", target_bir_lowering=False, num_devices=1)
    columns = lambda vectors: np.stack([np.asarray(v).reshape(-1, P) for v in vectors]).transpose(2, 0, 1)
    data = {
        "x": x, "ctx": ctx_768, "ctxT": np.asarray(ctx_768).transpose(0, 2, 1), "w_q": L0_xattn_w_q, "w_kv": L0_xattn_w_kv,
        "wkT": np.asarray(L0_xattn_w_kv)[:, 0:INNER].T, "w_out": L0_xattn_w_out, "b_out": L0_xattn_b_out,
        "channels": columns([L0_attn_time_decay, L0_attn_time_first, L0_attn_time_mix_key, L0_attn_time_mix_value,
                             L0_attn_time_mix_receptance]),
        "squares": np.stack([np.asarray(w).T for w in (L0_attn_Wk, L0_attn_Wv, L0_attn_Wr, L0_attn_Wo)]),
        "bo": L0_attn_bo, "w1": L0_ffn_w1, "b1": np.asarray(L0_ffn_b1).reshape(-1, P).T, "w2": L0_ffn_w2, "b2": L0_ffn_b2,
    }
    data = {name: np.ascontiguousarray(a) for name, a in data.items()}
    t = {name: nc.dram_tensor(f"in_{name}", a.shape, F32, kind="ExternalInput").ap() for name, a in data.items()}
    out = nc.dram_tensor("out_x", (NB, NQ, DM), F32, kind="ExternalOutput").ap()
    qk_dram = nc.dram_tensor("qk_scratch", (NB, DC, HQ), F32).ap()
    o_dram = nc.dram_tensor("o_scratch", (NB, DC, HQ), F32).ap()
    perceiver_layer(nc, t, qk_dram, o_dram, out)
    result = run_bass_kernel_spmd(nc, [{f"in_{name}": a for name, a in data.items()}], core_ids=[0])
    return result.results[0]["out_x"]


def perceiver_layer(nc, t, qk_dram, o_dram, out):
    project_queries(nc, t["x"], t["w_q"], t["wkT"], qk_dram)
    attend(nc, t["ctx"], t["ctxT"], qk_dram, o_dram)
    with nc.sbuf_tensor("resid", [P, TT, DM], F32) as resid:
        attention_output(nc, t["w_kv"], t["w_out"], t["b_out"], t["x"], o_dram, resid)
        mix_and_feed(nc, t["channels"], t["squares"], t["bo"], t["w1"], t["b1"], t["w2"], t["b2"], resid, out)
```
